# Optimizing a Trainium2 kernel written in Bass

```python
import numpy as np
import jax
import jax.numpy as jnp

def _softmax(x, axis=-1):
    return jax.nn.softmax(x, axis=axis)

def _gelu(x):
    return jax.nn.gelu(x, approximate=True)

def _silu(x):
    return jax.nn.silu(x)

def _sigmoid(x):
    return jax.nn.sigmoid(x)

def _layernorm(x, axis=-1, eps=1e-05):
    m = jnp.mean(x, axis=axis, keepdims=True)
    v = jnp.var(x, axis=axis, keepdims=True)
    return (x - m) / jnp.sqrt(v + eps)

def _scatter_add(tgt, idx, src, axis=0):
    return tgt.at[idx].add(src)

def _segment_sum(src, seg, n):
    return jax.ops.segment_sum(src, seg, n)
kernel_name = 'mk_flamingo_gated_d1_seqx_r8_82ab09'

def setup_inputs(seed: int=0):
    np.random.seed(seed)
    _w = jnp.asarray

    def _rec_inputs():
        import jax
        import jax.numpy as jnp
        _rk = jax.random.key(seed)
        x = 7.22e-05 + 1 * jax.random.normal(jax.random.fold_in(_rk, 1), (8, 128, 256), jnp.float32)
        _lenS = 128 - jax.random.randint(jax.random.fold_in(_rk, 7), (8,), 0, max(1, 128 // 4) + 1, jnp.int32)
        _lenS2 = 128 - jax.random.randint(jax.random.fold_in(_rk, 8), (8,), 0, max(1, 128 // 4) + 1, jnp.int32)
        _ctx_2048P = jax.random.normal(jax.random.fold_in(_rk, 11), (8, 16, 256), jnp.float32)
        _ctx_2048c = jax.random.dirichlet(jax.random.fold_in(_rk, 511), 0.3 * jnp.ones((16,), jnp.float32), (8, 128))
        _ctx_2048t = jnp.einsum('bsk,bkd->bsd', _ctx_2048c, _ctx_2048P)
        _ctx_2048t = _ctx_2048t * jax.lax.rsqrt(jnp.mean(jnp.square(_ctx_2048t)) + 1e-12) * 0.953939
        ctx_2048 = 4.13588e-05 + 0.999923 * (_ctx_2048t + 0.3 * jax.random.normal(jax.random.fold_in(_rk, 611), (8, 128, 256), jnp.float32))
        _g = jax.random.normal(jax.random.fold_in(_rk, 9001), (2, 1), jnp.float32)
        _g = jnp.sign(_g) * jnp.maximum(jnp.abs(_g), 1.0) + (_g == 0) * 1.0
        g_xattn = _g[0]
        g_ffn = _g[1]
        return (x, ctx_2048, g_xattn, g_ffn)
    x, ctx_2048, g_xattn, g_ffn = _rec_inputs()

    def _L0_xattn_setup():
        import jax, jax.numpy as jnp
        import numpy as np
        N_HEADS = 16
        K_CH = 128 // N_HEADS
        SCALE = 1.0 / np.sqrt(K_CH)
        key = jax.random.key(seed)
        ks = jax.random.split(key, 10)
        B, C, T = (4, 128, 256)
        Cout = 128
        xavier = lambda k, o, i: jax.random.uniform(k, (o, i), jnp.float32, -1.0, 1.0) * np.sqrt(6.0 / (o + i))
        return {'x': jax.random.normal(ks[0], (B, C, T), jnp.float32), 'c': jax.random.normal(ks[1], (B, C, T), jnp.float32), 'Wq': xavier(ks[2], C, C), 'bq': jnp.zeros((C,), jnp.float32), 'Wk': xavier(ks[3], C, C), 'bk': jnp.zeros((C,), jnp.float32), 'Wv': xavier(ks[4], C, C), 'bv': jnp.zeros((C,), jnp.float32), 'Wo': xavier(ks[5], Cout, C), 'bo': jnp.zeros((Cout,), jnp.float32)}
    _L0_xattn_all = _L0_xattn_setup()
    _L0_xattn_in = {k: v for k, v in _L0_xattn_all.items() if k in ('Wq', 'bq', 'Wk', 'bk', 'Wv', 'bv', 'Wo', 'bo')}
    del _L0_xattn_all

    def _L0_ffn_setup():
        import jax, jax.numpy as jnp
        import numpy as np
        H = 256
        M = 176
        E = 32
        TOPK = 6
        G = 8
        TOPK_G = 4
        SH = 2
        B, S = (1, 128)
        key = jax.random.key(seed)
        ks = jax.random.split(key, 9)
        sc = 0.02
        return {'x': jax.random.normal(ks[0], (B, S, H), dtype=jnp.float32), 'w_router': jax.random.normal(ks[1], (H, E), dtype=jnp.float32) * sc, 'corr_bias': jax.random.normal(ks[2], (E,), dtype=jnp.float32) * 0.1, 'gate_w': jax.random.normal(ks[3], (E, H, M), dtype=jnp.float32) * sc, 'up_w': jax.random.normal(ks[4], (E, H, M), dtype=jnp.float32) * sc, 'down_w': jax.random.normal(ks[5], (E, M, H), dtype=jnp.float32) * sc, 'sh_gate_w': jax.random.normal(ks[6], (H, M * SH), dtype=jnp.float32) * sc, 'sh_up_w': jax.random.normal(ks[7], (H, M * SH), dtype=jnp.float32) * sc, 'sh_down_w': jax.random.normal(ks[8], (M * SH, H), dtype=jnp.float32) * sc}
    _L0_ffn_all = _L0_ffn_setup()
    _L0_ffn_in = {k: v for k, v in _L0_ffn_all.items() if k in ('w_router', 'corr_bias', 'gate_w', 'up_w', 'down_w', 'sh_gate_w', 'sh_up_w', 'sh_down_w')}
    del _L0_ffn_all
    return {'x': x, 'ctx_2048': ctx_2048, 'g_xattn': g_xattn, 'g_ffn': g_ffn, 'L0_xattn_Wq': _L0_xattn_in['Wq'], 'L0_xattn_bq': _L0_xattn_in['bq'], 'L0_xattn_Wk': _L0_xattn_in['Wk'], 'L0_xattn_bk': _L0_xattn_in['bk'], 'L0_xattn_Wv': _L0_xattn_in['Wv'], 'L0_xattn_bv': _L0_xattn_in['bv'], 'L0_xattn_Wo': _L0_xattn_in['Wo'], 'L0_xattn_bo': _L0_xattn_in['bo'], 'L0_ffn_w_router': _L0_ffn_in['w_router'], 'L0_ffn_corr_bias': _L0_ffn_in['corr_bias'], 'L0_ffn_gate_w': _L0_ffn_in['gate_w'], 'L0_ffn_up_w': _L0_ffn_in['up_w'], 'L0_ffn_down_w': _L0_ffn_in['down_w'], 'L0_ffn_sh_gate_w': _L0_ffn_in['sh_gate_w'], 'L0_ffn_sh_up_w': _L0_ffn_in['sh_up_w'], 'L0_ffn_sh_down_w': _L0_ffn_in['sh_down_w']}

def reference(x, ctx_2048, g_xattn, g_ffn, L0_xattn_Wq, L0_xattn_bq, L0_xattn_Wk, L0_xattn_bk, L0_xattn_Wv, L0_xattn_bv, L0_xattn_Wo, L0_xattn_bo, L0_ffn_w_router, L0_ffn_corr_bias, L0_ffn_gate_w, L0_ffn_up_w, L0_ffn_down_w, L0_ffn_sh_gate_w, L0_ffn_sh_up_w, L0_ffn_sh_down_w):
    import jax
    import jax.numpy as jnp

    def _L0_xattn_ref(x, c, Wq, bq, Wk, bk, Wv, bv, Wo, bo):
        import jax, jax.numpy as jnp
        import numpy as np
        N_HEADS = 16
        K_CH = 128 // N_HEADS
        SCALE = 1.0 / np.sqrt(K_CH)
        B, C, T = x.shape
        H, K = (N_HEADS, K_CH)
        q = jnp.einsum('oc,bct->bot', Wq, x) + bq[None, :, None]
        k = jnp.einsum('oc,bct->bot', Wk, c) + bk[None, :, None]
        v = jnp.einsum('oc,bct->bot', Wv, c) + bv[None, :, None]
        q = q.reshape(B, H, K, T)
        k = k.reshape(B, H, K, -1)
        v = v.reshape(B, H, K, -1)
        scores = jnp.einsum('bhkt,bhks->bhts', q, k) * SCALE
        p = jax.nn.softmax(scores, axis=-1)
        out = jnp.einsum('bhts,bhks->bhkt', p, v)
        out = out.reshape(B, H * K, T)
        return jnp.einsum('oc,bct->bot', Wo, out) + bo[None, :, None]

    def _L0_ffn_ref(x, w_router, corr_bias, gate_w, up_w, down_w, sh_gate_w, sh_up_w, sh_down_w):
        import jax, jax.numpy as jnp
        import numpy as np
        H = 256
        M = 176
        E = 32
        TOPK = 6
        G = 8
        TOPK_G = 4
        SH = 2
        B, S = (1, 128)
        b, s, h = x.shape
        xf = x.reshape(-1, h)
        T = xf.shape[0]
        logits = xf @ w_router
        scores = jax.nn.sigmoid(logits)
        sfc = scores + corr_bias
        grp = sfc.reshape(T, G, E // G)
        top2, _ = jax.lax.top_k(grp, 2)
        group_scores = top2.sum(-1)
        _, gidx = jax.lax.top_k(group_scores, TOPK_G)
        group_mask = jax.nn.one_hot(gidx, G, dtype=jnp.float32).sum(axis=1) > 0
        score_mask = jnp.repeat(group_mask, E // G, axis=1)
        masked = jnp.where(score_mask, sfc, -jnp.inf)
        _, topk_idx = jax.lax.top_k(masked, TOPK)
        topk_w = jnp.take_along_axis(scores, topk_idx, axis=1)
        combine = jnp.zeros((T, E), dtype=x.dtype).at[jnp.arange(T)[:, None], topk_idx].add(topk_w)
        g = jnp.einsum('th,ehm->etm', xf, gate_w)
        u = jnp.einsum('th,ehm->etm', xf, up_w)
        eo = jnp.einsum('etm,emh->eth', jax.nn.silu(g) * u, down_w)
        routed = jnp.einsum('te,eth->th', combine, eo)
        shared = jax.nn.silu(xf @ sh_gate_w) * (xf @ sh_up_w) @ sh_down_w
        return (routed + shared).reshape(b, s, h)
    x = x + jnp.tanh(g_xattn[0]) * _L0_xattn_ref(_layernorm(x, axis=-1), ctx_2048, L0_xattn_Wq, L0_xattn_bq, L0_xattn_Wk, L0_xattn_bk, L0_xattn_Wv, L0_xattn_bv, L0_xattn_Wo, L0_xattn_bo)
    x = x + jnp.tanh(g_ffn[0]) * _L0_ffn_ref(_layernorm(x, axis=-1), L0_ffn_w_router, L0_ffn_corr_bias, L0_ffn_gate_w, L0_ffn_up_w, L0_ffn_down_w, L0_ffn_sh_gate_w, L0_ffn_sh_up_w, L0_ffn_sh_down_w)
    return x

_drawn_inputs = setup_inputs


def setup_inputs(seed=0):
    import zlib

    import numpy as np

    out = dict(_drawn_inputs(seed))
    spreads = {'L0_xattn_bq': (0.0, 0.378),
     'L0_xattn_bk': (0.0, 0.8),
     'L0_xattn_bv': (0.0, 0.1),
     'L0_xattn_bo': (0.0, 0.1)}
    factors = {'L0_ffn_w_router': 4.539,
     'L0_ffn_corr_bias': 3.857,
     'L0_ffn_gate_w': 3.242,
     'L0_ffn_up_w': 3.207,
     'L0_ffn_down_w': 3.216,
     'L0_ffn_sh_gate_w': 3.19,
     'L0_ffn_sh_up_w': 3.124,
     'L0_ffn_sh_down_w': 3.137}
    for name, (base, spread) in spreads.items():
        noise = np.random.default_rng([zlib.crc32(name.encode()), seed]).standard_normal(out[name].shape)
        drawn = base * np.exp(spread * noise) if base else spread * noise
        out[name] = jnp.asarray(drawn.astype(out[name].dtype))
    for name, factor in factors.items():
        out[name] = (out[name] * factor).astype(out[name].dtype)
    return out
```

```python
from contextlib import ExitStack

import concourse.bass as bass
from concourse import mybir

F32 = mybir.dt.float32
F16 = mybir.dt.float16
I32 = mybir.dt.int32
U32 = mybir.dt.uint32
ALU = mybir.AluOpType
ACT = mybir.ActivationFunctionType
AXX = mybir.AxisListType.X

B, C, T = 8, 128, 256
NH, KC = 16, 8
NG, NJ = 4, 4
NE, M = 32, 176
MH = M // 2
KT = T // 128
GROUPS, TOPG, TOPK = 8, 4, 6
SCALE = float(KC) ** -0.5
EPS = 1e-5
WS = 64.0
ROW = 3 * KC
ROUTE_STEPS = 29
DISPATCH_STEPS = 4
N = B * C
CAP = N + 128
SPARE = NE * CAP
NB = (N * TOPK + NE * 127) // 128
PAY = T + 1 + NE
WB = 4
TABLE_STEPS = 11
RANK_AT, COUNT_AT, TABLE_AT = 0, 2, 5
RING = 3
NP = 4

TURNS = ["A0", "A1", "B0", "WO", "A2", "RK", "B1", "PROJ", "A3", "B2", "A4", "B3", "XT", "A5", "B4",
         "QS", "KS", "A6", "A7", "B5", "LG", "NMT", "B6", "B7"]
USES = [len(TURNS[s::RING]) for s in range(RING)]


def slot(job):
    return TURNS.index(job) % RING


def use(job, n):
    return USES[slot(job)] * n + TURNS.index(job) // RING


def build(nc, x, ctx_in, g_xattn, g_ffn, Wq, bq, Wk, bk, Wv, bv, Wo, bo, w_router, corr_bias,
          gate_w, up_w, down_w, sh_gate_w, sh_up_w, sh_down_w, out):
    with ExitStack() as stack:
        def sb(name, shape, dt=F32):
            return stack.enter_context(nc.sbuf_tensor(name, shape, dt))

        def sem(name):
            return stack.enter_context(nc.semaphore(name))

        ident = sb("ident", [128, 128])
        zeros = sb("zeros", [128, 128])
        ones = sb("ones", [128, NE])
        pick = sb("pick", [128, 4, NJ, NG, 4, KC], F16)
        onesrow = sb("onesrow", [128, 1])
        onesM = sb("onesM", [128, NJ, 128])
        wnat = sb("wnat", [128, 4, 128])
        wT = sb("wT", [128, 4, 128])
        bias = sb("bias", [128, 4])
        gates = sb("gates", [128, 2])
        tg = sb("tg", [128, 2])
        wr = sb("wr", [128, KT, NE])
        corr = sb("corr", [128, NE])
        xs = sb("xs", [128, B, T])
        st = sb("st", [128, B, 6])
        mv = sb("mv", [128, B, 2])
        ve = sb("ve", [128, B])
        lnv = sb("lnv", [128, B])
        r0 = sb("r0", [128, B])
        r1 = sb("r1", [128, B])
        r2 = sb("r2", [128, B])
        r3 = sb("r3", [128, B])
        rstd = sb("rstd", [128, B, 1])
        xnb = sb("xnb", [128, 2, T])
        ctxb = sb("ctxb", [128, 2, T])
        qk32 = sb("qk32", [128, 2, T])
        v32 = sb("v32", [128, KT, 128])
        qkh = sb("qkh", [128, 2, T], F16)
        qkl = sb("qkl", [128, 2, T], F16)
        qS = sb("qS", [128, 2, NJ, T], F16)
        kS = sb("kS", [128, 2, NJ, T], F16)
        kB = sb("kB", [128, NJ, T], F16)
        kM = sb("kM", [128, 2, NJ, NG, T], F16)
        q2S = sb("q2S", [128, NJ, T], F16)
        q2M = sb("q2M", [128, 2, NJ, NG, T], F16)
        vM = sb("vM", [128, 2, KT, NJ, 128])
        nmx = sb("nmx", [128, KT, NJ, NG, 32])
        Pb = sb("Pb", [128, NP, NG, T])
        rD = sb("rD", [128, T])
        on = sb("on", [128, T])
        ob = sb("ob", [128, T])
        wo_t = sb("wo_t", [128, T])
        st2 = sb("st2", [128, 6])
        mv2 = sb("mv2", [128, 2])
        ve2 = sb("ve2", [128, 1])
        ln2 = sb("ln2", [128, 1])
        s0 = sb("s0", [128, 1])
        s1 = sb("s1", [128, 1])
        s2 = sb("s2", [128, 1])
        s3 = sb("s3", [128, 1])
        rstd2 = sb("rstd2", [128, 1])
        xc = sb("xc", [128, T])
        pay = sb("pay", [128, 2, PAY])
        xT32 = sb("xT32", [128, KT, 128])
        xT = sb("xT", [128, B, KT, 2, 128], F16)
        el = sb("el", [128, NE])
        rt = sb("rt", [128, 24, NE])
        tri = sb("tri", [128, 128])
        tri16 = sb("tri16", [128, 128], F16)
        ones16 = sb("ones16", [128, 128], F16)
        em16 = sb("em16", [128, NE], F16)
        emsum = sb("emsum", [128, NE], F16)
        counting = sb("counting", [128, 2 * (NE + 1) + (B + 1) + 8 * NE], I32)
        counts = sb("counts", [128, 2 * (NE + 1) + (B + 1) + 8 * NE])
        first_row = counts[:, 0:NE]
        pad_row = counts[:, NE + 1:2 * NE + 2]
        number = counts[:, 2 * NE + 2:2 * NE + 3 + B]
        full = counts[:, 2 * NE + 3 + B:].rearrange("p (e k) -> p e k", k=8)
        dp = sb("dp", [128, 3, NE])
        place = sb("place", [128, 2, TOPK], U32)
        pad_place = sb("pad_place", [128, NE], U32)
        filling = sb("filling", [128, PAY])
        tb = sb("tb", [128, 4, NE])
        over = sb("over", [128, NE, 8])
        cols = sb("cols", [128, 8])
        table = sb("table", [1, 2 * 128], I32)
        wraw = sb("wraw", [128, 2, KT, 2, M])
        draw = sb("draw", [MH, 2, 2, T])
        W = sb("W", [128, 2, KT, 2, 2 * M], F16)
        D = sb("D", [MH, 2, 2, 2, T], F16)
        sg = sb("sg", [128, 2, M])
        h = sb("h", [128, 2, M])
        hT = sb("hT", [MH, 2, 2, 2, 128], F16)
        acc = sb("acc", [128, B, T])
        acc1 = sb("acc1", [128, B, T])
        bx = sb("bx", [128, WB, PAY])
        bid = sb("bid", [128, WB], U32)
        bw = sb("bw", [128, WB, KT, 2, M])
        bd = sb("bd", [MH, WB, 2, T])
        bxT = sb("bxT", [128, 2, KT, 128])
        bsg = sb("bsg", [128, 2, M])
        bh = sb("bh", [128, 2, M])
        bhT = sb("bhT", [MH, 2, 2, 128])
        by = sb("by", [128, WB, T])
        tick = sb("tick", [128, 2])

        XS = nc.dram_tensor("rows_by_expert", (SPARE + 128, PAY), F32).ap()
        SUM = [nc.dram_tensor(f"routed_sum{i}", (N + 128, T), F32).ap() for i in range(2)]

        ps = stack.enter_context(nc.psum_tensor("ps", [128, 8, 512], F32))

        def ring(job):
            s = slot(job)
            return ps[:, 2 * s:2 * s + 2, :].rearrange("p a b -> p (a b)")

        def od(par):
            return ps[:, 6 + par, :]

        filled = [sem(f"ring_filled{s}") for s in range(RING)]
        emptied = [sem(f"ring_emptied{s}") for s in range(RING)]
        consts_in = sem("consts_in")
        x_in = sem("x_in")
        ctx_in_s = [sem("ctx_in0"), sem("ctx_in1")]
        memsets = sem("memsets")
        pool_setup = sem("pool_setup")
        setup_done = sem("setup_done")
        wt_filled = sem("wt_filled")
        wt_ready = sem("wt_ready")
        proj0_filled = sem("proj0_filled")
        qkv0_ready = sem("qkv0_ready")
        qs0_filled = sem("qs0_filled")
        ks0_filled = sem("ks0_filled")
        stacks0_ready = sem("stacks0_ready")
        keys_kept = sem("keys_kept")
        tanh_done = sem("tanh_done")
        ln1 = sem("ln1")
        ln1_act = sem("ln1_act")
        xn_ready = sem("xn_ready")
        split_hi = sem("split_hi")
        split_lo = sem("split_lo")
        v_masked = sem("v_masked")
        k_masked = sem("k_masked")
        q2_masked = sem("q2_masked")
        p_used = sem("p_used")
        o_step = sem("o_step")
        x1_step = sem("x1_step")
        rs_act = sem("rs_act")
        rs_step = sem("rs_step")
        xT_ready = sem("xT_ready")
        xT_lo = sem("xT_lo")
        sig_exp = sem("sig_exp")
        rt_step = sem("rt_step")
        w_in = [sem("w_in0"), sem("w_in1")]
        w_hi = sem("w_hi")
        w_lo = sem("w_lo")
        gu_done = sem("gu_done")
        silu_done = sem("silu_done")
        h_done = sem("h_done")
        hT_filled = sem("hT_filled")
        hT_hi = sem("hT_hi")
        hT_lo = sem("hT_lo")
        y_done = sem("y_done")
        acc_done = sem("acc_done")
        fin_done = sem("fin_done")
        dp_step = sem("dp_step")
        sent = [sem("sent0"), sem("sent1")]
        pads_sent = sem("pads_sent")
        zeroed = sem("zeroed")
        rank7_filled = sem("rank7_filled")
        counts_filled = sem("counts_filled")
        tb_step = sem("tb_step")
        table_filled = sem("table_filled")
        table_ready = sem("table_ready")
        bx_in = [sem(f"bx_in{j}") for j in range(WB)]
        bw_in = [sem(f"bw_in{j}") for j in range(WB)]
        bid_done = sem("bid_done")
        bxT_filled = sem("bxT_filled")
        bxT_done = sem("bxT_done")
        bgu_done = sem("bgu_done")
        bsilu_done = sem("bsilu_done")
        bh_done = sem("bh_done")
        bhT_filled = sem("bhT_filled")
        bhT_done = sem("bhT_done")
        by_filled = sem("by_filled")
        by_done = sem("by_done")
        added = [sem("added0"), sem("added1")]
        sums_in = sem("sums_in")
        tail_sum = sem("tail_sum")
        send_tick = sem("send_tick")
        add_tick = sem("add_tick")
        rank7_read = sem("rank7_read")
        out_ready = sem("out_ready")
        out_done = sem("out_done")

        block = stack.enter_context(nc.Block())

        def wait_filled(eng, job, n):
            eng.wait_ge(filled[slot(job)], use(job, n) + 1)

        def wait_emptied(eng, job, n):
            eng.wait_ge(emptied[slot(job)], use(job, n) + 1)

        def link(eng, semaphore, base, count):
            done = [0]

            def step(instruction):
                done[0] += 1
                assert done[0] <= count
                instruction.then_inc(semaphore, 1)
                eng.wait_ge(semaphore, base + done[0])
            return step

        def periods(eng, period):
            period(0, 0)
            period(1, 1)
            period(2, 2)
            with eng.Fori(0, 2) as t:
                period(3, t * 2 + 3)
                period(4, t * 2 + 4)
            period(7, 7)
            period(8, 8)
            period(9, 9)

        def blocks(eng, step):
            first = 2 * WB - 1
            rounds = (NB - (WB - 1) - first) // WB
            for b in range(first):
                step(b, b % WB)
            with eng.Fori(0, rounds) as t:
                for u in range(WB):
                    step(t * WB + (first + u), (first + u) % WB)
            for b in range(first + WB * rounds, NB + 2):
                step(b, b % WB)

        def since(b, k):
            return not isinstance(b, int) or b >= k

        def until(b):
            return not isinstance(b, int) or b < NB

        def has(kind, job):
            if job[0] == "A" or job == "NMT":
                return kind < B
            if job[0] == "B":
                return 1 <= kind <= B
            if job in ("PROJ", "QS", "KS"):
                return kind < B - 1
            return kind >= (3 if job == "RK" else 2)

        @block.sync
        def _(sp):
            for i, w in enumerate((Wq, Wk, Wv, Wo)):
                sp.dma_start(wnat[:, i, :], w).then_inc(consts_in, 16)
            for i, v in enumerate((bq, bk, bv, bo)):
                sp.dma_start(bias[:, i:i + 1], v.rearrange("(p a) -> p a", a=1)).then_inc(consts_in, 16)
            sp.dma_start(ctxb[:, 0, :], ctx_in[0]).then_inc(ctx_in_s[0], 16)
            for i, v in enumerate((g_xattn, g_ffn)):
                sp.dma_start(gates[:, i:i + 1], v.partition_broadcast(128)).then_inc(consts_in, 16)
            sp.dma_start(wr[:, :, :], w_router.rearrange("(k p) e -> p k e", p=128)).then_inc(consts_in, 16)
            sp.dma_start(corr[:, :], corr_bias.partition_broadcast(128)).then_inc(consts_in, 16)

            def load_ctx(b, par, first):
                if not first:
                    wait_filled(sp, "PROJ", b - 3)
                sp.dma_start(ctxb[:, par, :], ctx_in[b]).then_inc(ctx_in_s[par], 16)

            load_ctx(1, 1, True)
            sp.wait_ge(proj0_filled, 1)
            sp.dma_start(ctxb[:, 0, :], ctx_in[2]).then_inc(ctx_in_s[0], 16)
            for b in range(3, B):
                load_ctx(b, b % 2, False)

            def load_expert(par, gate, up, down):
                sp.dma_start(wraw[:, par, :, 0, :], gate.rearrange("(k p) m -> p k m", p=128)).then_inc(w_in[par], 16)
                sp.dma_start(wraw[:, par, :, 1, :], up.rearrange("(k p) m -> p k m", p=128)).then_inc(w_in[par], 16)
                sp.dma_start(draw[:, par, :, :], down.rearrange("(c p) n -> p c n", p=MH)).then_inc(w_in[par], 16)

            for par in range(2):
                half = slice(par * M, par * M + M)
                load_expert(par, sh_gate_w[:, half], sh_up_w[:, half], sh_down_w[half, :])
            sp.wait_ge(acc_done, B)
            for total in SUM:
                sp.dma_start(total[0:N].rearrange("(b p) t -> p b t", p=128), acc[:, :, :]).then_inc(zeroed, 16)
            sp.dma_start(SUM[1][N:N + 128], acc[:, 0, :]).then_inc(zeroed, 16)

            sp.wait_ge(table_ready, 1)

            def load_block(b, j):
                if not until(b):
                    return
                e = sp.value_load(table[0:1, bass.ds(b + 128, 1)], min_val=0, max_val=NE - 1)
                if since(b, WB):
                    sp.wait_ge(by_filled, b - WB + 1)
                for side, w in enumerate((gate_w, up_w)):
                    sp.dma_start(bw[:, j, :, side, :], w[bass.ds(e, 1)].rearrange("e (k p) m -> p (e k) m", p=128))\
                      .then_inc(bw_in[j], 16)
                sp.dma_start(bd[:, j, :, :], down_w[bass.ds(e, 1)].rearrange("e (c p) n -> p (e c) n", p=MH))\
                  .then_inc(bw_in[j], 16)

            blocks(sp, load_block)
            for i in range(2):
                sp.wait_ge(added[i], 16 * ((NB + 1 - i) // 2))
                sp.dma_start((acc, acc1)[i][:, :, :], SUM[i][0:N].rearrange("(b p) t -> p b t", p=128)).then_inc(sums_in, 16)
            for b in range(B):
                sp.wait_ge(out_ready, b + 1)
                sp.dma_start(out[b], xs[:, b, :]).then_inc(out_done, 16)
            sp.wait_ge(out_done, 16 * B)

        @block.gpsimd
        def _(pool):
            pool.sem_inc(send_tick, 1)
            pool.wait_ge(memsets, 1)
            nc.gpsimd.affine_select(out=ident[:, :], in_=zeros[:, :], compare_op=ALU.not_equal, fill=1.0, base=0,
                                    pattern=[[-1, 128]], channel_multiplier=1).then_inc(pool_setup, 1)
            nc.gpsimd.affine_select(out=ob[:, 0:NG], in_=zeros[:, 0:NG], compare_op=ALU.not_equal, fill=1.0,
                                    base=-ROW, pattern=[[-32, NG]], channel_multiplier=1).then_inc(pool_setup, 1)
            nc.gpsimd.affine_select(out=tri[:, :], in_=zeros[:, :], compare_op=ALU.is_ge, fill=1.0, base=0,
                                    pattern=[[-1, 128]], channel_multiplier=1).then_inc(pool_setup, 1)
            nc.gpsimd.iota(counting[:, 0:NE + 1], pattern=[[CAP, NE + 1]], base=1, channel_multiplier=0)\
                .then_inc(pool_setup, 1)
            nc.gpsimd.iota(counting[:, NE + 1:2 * NE + 2], pattern=[[CAP, NE + 1]], base=0, channel_multiplier=1)\
                .then_inc(pool_setup, 1)
            nc.gpsimd.iota(counting[:, 2 * NE + 2:2 * NE + 3 + B], pattern=[[128, B + 1]], base=0, channel_multiplier=1)\
                .then_inc(pool_setup, 1)
            nc.gpsimd.iota(counting[:, 2 * NE + 3 + B:], pattern=[[0, NE], [128, 8]], base=0, channel_multiplier=0)\
                .then_inc(pool_setup, 1)

            def split_low(p):
                pool.wait_ge(split_hi, p + 1)
                nc.gpsimd.tensor_tensor(qkl[:, :, :], qk32[:, :, :], qkh[:, :, :], ALU.subtract).then_inc(split_lo, 1)

            def mask_v(par):
                for s in range(KT):
                    for J in range(NJ):
                        cols = slice(KC * J, KC * J + KC)
                        nc.gpsimd.tensor_tensor(
                            vM[:, par, s, J, :].rearrange("p (g c) -> p g c", c=32)[:, :, cols],
                            v32[:, s, :].rearrange("p (g c) -> p g c", c=32)[:, :, cols],
                            zeros[:, :].rearrange("p (g c) -> p g c", c=32)[:, :, cols], ALU.add).then_inc(v_masked, 1)

            pool.wait_ge(setup_done, 2)
            nc.gpsimd.dma_start(XS[SPARE:SPARE + 128], filling[:, :]).then_inc(sent[0], 16)
            nc.gpsimd.dma_start(SUM[0][N:N + 128, 0:T], filling[:, 0:T]).then_inc(sent[1], 16)
            pool.wait_ge(qkv0_ready, 3)
            split_low(0)
            mask_v(0)

            def period(kind, n):
                par = kind % 2
                if has(kind, "PROJ"):
                    split_low(n + 1)
                if has(kind, "XT"):
                    c = n - 2
                    wait_emptied(pool, "XT", n)
                    nc.gpsimd.tensor_tensor(xT[:, c, :, 1, :], xT32[:, :, :], xT[:, c, :, 0, :], ALU.subtract)\
                        .then_inc(xT_lo, 1)
                if has(kind, "PROJ"):
                    wait_emptied(pool, "PROJ", n)
                    pool.wait_ge(p_used, 8 * n)
                    mask_v(1 - par)
                if has(kind, "RK"):
                    send(n - 3, 1 - par)

            def send(c, par):
                pool.wait_ge(dp_step, DISPATCH_STEPS * (c + 1) + 1)
                pool.wait_ge(send_tick, c + 1)
                nc.gpsimd.tensor_tensor(tick[:, 0:1], zeros[:, 0:1], zeros[:, 0:1], ALU.add).then_inc(send_tick, 1)
                for k in range(TOPK):
                    nc.gpsimd.indirect_dma_start(XS, bass.IndirectOffsetOnAxis(ap=place[:, par, k:k + 1], axis=0),
                                                 pay[:, par, :], None).then_inc(sent[par], 16)

            periods(pool, period)
            send(B - 1, (B - 1) % 2)
            pool.wait_ge(tb_step, 1)
            for e in range(NE):
                nc.gpsimd.indirect_dma_start(XS, bass.IndirectOffsetOnAxis(ap=pad_place[:, e:e + 1], axis=0),
                                             filling[:, :], None).then_inc(pads_sent, 16)

            def add_block(b, j):
                if not until(b):
                    return
                buf = j % 2
                pool.wait_ge(by_done, b + 1)
                pool.wait_ge(bid_done, b + 1)
                if since(b, 2):
                    pool.wait_ge(added[buf], (b - buf) * 8)
                pool.wait_ge(add_tick, b)
                nc.gpsimd.tensor_tensor(tick[:, 1:2], zeros[:, 0:1], zeros[:, 0:1], ALU.add).then_inc(add_tick, 1)
                nc.gpsimd.indirect_dma_start(SUM[buf], bass.IndirectOffsetOnAxis(ap=bid[:, j:j + 1], axis=0),
                                             by[:, j, :], None, compute_op=ALU.add).then_inc(added[buf], 16)

            pool.wait_ge(zeroed, 16 * 3)
            pool.wait_ge(sent[1], 16)
            blocks(pool, add_block)

        @block.scalar
        def _(act):
            act.dma_start(xs[:, :, :], x.rearrange("b p t -> p b t")).then_inc(x_in, 16)
            act.wait_ge(consts_in, 16 * 12)
            act.activation(tg[:, :], gates[:, :], ACT.Tanh).then_inc(tanh_done, 1)
            act.wait_ge(wt_filled, 1)
            act.activation(wT[:, :, :], ring("A0")[:, 0:512].rearrange("p (a b) -> p a b", a=4), ACT.Copy)\
               .then_inc(wt_ready, 1)
            act.wait_ge(ln1, 17)
            act.activation(lnv[:, :], ve[:, :], ACT.Ln).then_inc(ln1_act, 1)
            act.wait_ge(ln1_act, 1)
            act.activation(r0[:, :], lnv[:, :], ACT.Exp, scale=-0.5).then_inc(ln1_act, 1)

            def evacuate_qkv(src, semaphore, each):
                for i in range(2):
                    ins = act.activation(qk32[:, i, :], src[:, i * T:(i + 1) * T], ACT.Identity, bias=bias[:, i:i + 1])
                    if each:
                        ins.then_inc(semaphore, 1)
                act.activation(v32[:, :, :], src[:, 512:768].rearrange("p (a b) -> p a b", a=KT), ACT.Copy)\
                   .then_inc(semaphore, 1)

            def stack_q(src, par, semaphore):
                act.activation(qS[:, par, :, :], src.rearrange("p (j t) -> p j t", j=NJ), ACT.Copy).then_inc(semaphore, 1)

            def stack_k(src, par, semaphore):
                act.activation(kS[:, par, :, :], src.rearrange("p (j t) -> p j t", j=NJ), ACT.Identity,
                               bias=onesrow[:, 0:1]).then_inc(semaphore, 1)

            def mask_k(par):
                for g in range(NG):
                    rows = slice(32 * g, 32 * g + 32)
                    act.activation(kM[rows, par, :, g, :], kS[rows, par, :, :], ACT.Copy).then_inc(k_masked, 1)

            def exps(u, b, n, kind):
                wait_filled(act, f"B{u}", n)
                if not (kind == 1 and u < NP):
                    act.wait_ge(p_used, 8 * b + u - NP + 1)
                act.activation(Pb[:, u % NP, :, :], ring(f"B{u}").rearrange("p (g t) -> p g t", g=NG), ACT.Exp,
                               scale=SCALE).then_inc(emptied[slot(f"B{u}")], 1)

            act.wait_ge(proj0_filled, 1)
            evacuate_qkv(ring("A1"), qkv0_ready, True)
            act.wait_ge(qs0_filled, 1)
            act.wait_ge(setup_done, 2)
            stack_q(ring("B0"), 0, stacks0_ready)
            act.wait_ge(ks0_filled, 1)
            stack_k(ring("A0"), 0, stacks0_ready)
            act.wait_ge(stacks0_ready, 2)
            mask_k(0)

            def period(kind, n):
                par = kind % 2
                c = n - 2
                for job in TURNS:
                    if not has(kind, job):
                        continue
                    if job[0] == "B":
                        exps(int(job[1]), n - 1, n, kind)
                    elif job == "WO":
                        act.wait_ge(x1_step, 5 * c + 5)
                        act.activation(ln2[:, :], ve2[:, :], ACT.Ln).then_inc(rs_act, 1)
                        act.wait_ge(rs_act, 2 * c + 1)
                        act.activation(s0[:, :], ln2[:, :], ACT.Exp, scale=-0.5).then_inc(rs_act, 1)
                    elif job == "PROJ":
                        wait_filled(act, job, n)
                        act.wait_ge(v_masked, 8 * (n + 1))
                        act.wait_ge(split_lo, n + 1)
                        evacuate_qkv(ring(job), emptied[slot(job)], False)
                    elif job == "XT":
                        wait_filled(act, job, n)
                        if kind > 2:
                            act.wait_ge(xT_lo, c)
                            wait_filled(act, "LG", n - 1)
                        act.activation(xT32[:, :, :], ring(job)[:, 0:256].rearrange("p (k t) -> p k t", k=KT), ACT.Copy)\
                           .then_inc(xT_ready, 1)
                        act.activation(xT[:, c, :, 0, :], ring(job)[:, 0:256].rearrange("p (k t) -> p k t", k=KT),
                                       ACT.Copy).then_inc(emptied[slot(job)], 1)
                    elif job == "QS":
                        wait_filled(act, job, n)
                        if kind >= 1:
                            wait_emptied(act, "NMT", n - 1)
                        stack_q(ring(job), 1 - par, emptied[slot(job)])
                    elif job == "KS":
                        wait_filled(act, job, n)
                        if kind >= 1:
                            act.wait_ge(keys_kept, n)
                        stack_k(ring(job), 1 - par, emptied[slot(job)])
                        wait_emptied(act, job, n)
                        if kind >= 1:
                            wait_filled(act, "A7", n - 1)
                        mask_k(1 - par)
                    elif job == "LG":
                        wait_filled(act, job, n)
                        act.wait_ge(rt_step, ROUTE_STEPS * c)
                        act.activation(el[:, :], ring(job)[:, 0:NE], ACT.Exp, scale=-1.0).then_inc(emptied[slot(job)], 1)

            periods(act, period)

            def high_weights(par):
                act.wait_ge(w_in[par], 48)
                act.activation(W[:, par, :, 0, :], wraw[:, par, :, :, :].rearrange("p k a m -> p k (a m)"), ACT.Copy,
                               scale=WS).then_inc(w_hi, 1)
                act.activation(D[:, par, :, 0, :], draw[:, par, :, :], ACT.Copy, scale=WS).then_inc(w_hi, 1)

            def high(i, buf, fresh=False):
                act.wait_ge(hT_filled, i + 1)
                if not fresh:
                    act.wait_ge(y_done, i - 1)
                act.activation(hT[:, buf, 0, :, :], ps[0:MH, 2 + buf, 0:256].rearrange("p (c t) -> p c t", c=2),
                               ACT.Copy).then_inc(hT_hi, 1)

            for par in range(2):
                high_weights(par)
            for i in range(2 * B):
                buf = i % 2
                act.wait_ge(gu_done, i + 1)
                if i >= 2:
                    act.wait_ge(h_done, i - 1)
                act.activation(sg[:, buf, :], ps[:, buf, 0:M], ACT.Silu, scale=1.0 / WS).then_inc(silu_done, 1)
                if i >= 1:
                    high(i - 1, 1 - buf, i < 3)
            high(2 * B - 1, 1)

            def fetch(b, j):
                if not until(b):
                    return
                r = act.value_load(table[0:1, bass.ds(b, 1)], min_val=0, max_val=SPARE)
                if since(b, WB):
                    act.wait_ge(bh_done, b - WB + 1)
                act.dma_start(bx[:, j, :], XS[bass.ds(r, 128)]).then_inc(bx_in[j], 16)

            def keep_xT(b, buf):
                if not until(b):
                    return
                act.wait_ge(bxT_filled, b + 1)
                if since(b, 2):
                    act.wait_ge(bgu_done, b - 1)
                act.activation(bxT[:, buf, :, :], ps[:, 6 + buf, 0:256].rearrange("p (k t) -> p k t", k=KT),
                               ACT.Copy).then_inc(bxT_done, 1)

            def step(b, j):
                buf = j % 2
                fetch(b + WB - 1, (j + WB - 1) % WB)
                keep_xT(b + 1, 1 - buf)
                if until(b):
                    act.wait_ge(bgu_done, b + 1)
                    if since(b, 2):
                        act.wait_ge(bh_done, b - 1)
                    act.activation(bsg[:, buf, :], ps[:, buf, 0:M], ACT.Silu).then_inc(bsilu_done, 1)

            for par in range(2):
                act.wait_ge(sent[par], 16 * TOPK * B // 2 + 16)
            act.wait_ge(pads_sent, 16 * NE)
            act.wait_ge(table_ready, 1)
            for b in range(WB - 1):
                fetch(b, b)
            keep_xT(0, 0)
            blocks(act, step)

        @block.tensor
        def _(pe):
            def take(job, n, first=False):
                before = use(job, n)
                if not (isinstance(before, int) and before == 0):
                    pe.wait_ge(emptied[slot(job)], before)

            pe.wait_ge(consts_in, 16 * 12)
            pe.wait_ge(pool_setup, 1)
            for i in range(4):
                last = pe.transpose(ring("A0")[:, 128 * i:128 * i + 128], wnat[:, i, :], ident[:, :])
            last.then_inc(wt_filled, 1)

            def project(dst, par, semaphore):
                pe.matmul(dst[:, 0:T], wT[:, 0, :], xnb[:, par, :], start=True, stop=True)
                pe.matmul(dst[:, T:2 * T], wT[:, 1, :], ctxb[:, par, :], start=True, stop=True)
                for s in range(KT):
                    last = pe.matmul(dst[:, 512 + 128 * s:640 + 128 * s], ctxb[:, par, 128 * s:128 * s + 128], wT[:, 2, :],
                                     start=True, stop=True)
                last.then_inc(semaphore, 1)

            def stack_rows(dst, side, semaphore):
                for J in range(NJ):
                    cols = slice(T * J, T * J + T)
                    pe.matmul(dst[:, cols], pick[:, 2 * side, J, :, :, :].rearrange("p g r c -> p (g r c)"),
                              qkh[:, side, :], start=True, stop=False)
                    last = pe.matmul(dst[:, cols], pick[:, 2 * side + 1, J, :, :, :].rearrange("p g r c -> p (g r c)"),
                                     qkl[:, side, :], start=False, stop=True)
                last.then_inc(semaphore, 1)

            pe.wait_ge(wt_ready, 1)
            pe.wait_ge(xn_ready, 1)
            pe.wait_ge(ctx_in_s[0], 16)
            project(ring("A1"), 0, proj0_filled)
            pe.wait_ge(split_lo, 1)
            pe.wait_ge(setup_done, 2)
            stack_rows(ring("B0"), 0, qs0_filled)
            stack_rows(ring("A0"), 1, ks0_filled)
            pe.wait_ge(stacks0_ready, 2)

            def scores_max(u, n, par):
                tc, J = divmod(u, NJ)
                if u == 0:
                    pe.wait_ge(k_masked, 4 * (n + 1))
                for half in range(2):
                    last = pe.matmul(ring(f"A{u}")[:, 512 * half:512 * half + 512],
                                     qS[:, par, J, 128 * tc:128 * tc + 128],
                                     kM[:, par, J, 2 * half:2 * half + 2, :].rearrange("p g s -> p (g s)"),
                                     start=True, stop=True)
                last.then_inc(filled[slot(f"A{u}")], 1)

            def scores_exp(u, n, par):
                sc, J = divmod(u, NJ)
                if u == 0:
                    pe.wait_ge(q2_masked, 4 * n)
                    pe.wait_ge(keys_kept, n)
                for half in range(2):
                    last = pe.matmul(ring(f"B{u}")[:, 512 * half:512 * half + 512],
                                     kB[:, J, 128 * sc:128 * sc + 128],
                                     q2M[:, par, J, 2 * half:2 * half + 2, :].rearrange("p g t -> p (g t)"),
                                     start=True, stop=True)
                last.then_inc(filled[slot(f"B{u}")], 1)

            def weigh(u, n, kind, par):
                b = n - 1
                sc, J = divmod(u, NJ)
                wait_emptied(pe, f"B{u}", n)
                if u == 0:
                    pe.wait_ge(v_masked, 8 * n)
                    if kind > 2:
                        pe.wait_ge(o_step, 3 * (b - 1))
                for g in range(NG):
                    rows = slice(32 * g, 32 * g + 32)
                    pe.matmul(od(par)[rows, 0:T], vM[:, par, sc, J, rows], Pb[:, u % NP, g, :],
                              start=(u == 0), stop=(u == 7), skip_group_check=True, tile_position=(0, 32 * g))
                    last = pe.matmul(od(par)[rows, T:2 * T], onesM[:, J, rows], Pb[:, u % NP, g, :],
                                     start=False, stop=(u == 7), skip_group_check=True, tile_position=(0, 32 * g))
                last.then_inc(p_used, 1)

            def rank(c, dst, semaphore):
                pe.wait_ge(rt_step, ROUTE_STEPS * (c + 1))
                pe.matmul(dst[:, 0:NE], tri16[:, :], em16[:, :], start=True, stop=False)
                pe.wait_ge(dp_step, DISPATCH_STEPS * c + 1)
                pe.matmul(dst[:, 0:NE], ones16[:, :], emsum[:, :], start=False, stop=True).then_inc(semaphore, 1)

            def period(kind, n):
                par = kind % 2
                for job in TURNS:
                    take(job, n)
                    s = slot(job)
                    if not has(kind, job):
                        pe.sem_inc(filled[s], 1)
                        pe.sem_inc(emptied[s], 1)
                        continue
                    if job[0] == "A":
                        scores_max(int(job[1]), n, par)
                    elif job[0] == "B":
                        u = int(job[1])
                        scores_exp(u, n, 1 - par)
                        if u > 0:
                            weigh(u - 1, n, kind, 1 - par)
                    elif job == "WO":
                        pe.wait_ge(o_step, 3 * (n - 1))
                        pe.matmul(ring(job)[:, 0:T], wT[:, 3, :], ob[:, :], start=True, stop=True).then_inc(filled[s], 1)
                    elif job == "PROJ":
                        pe.wait_ge(xn_ready, n + 2)
                        pe.wait_ge(ctx_in_s[1 - par], 8 * (n + 1 - (1 - par)) + 16)
                        project(ring(job), 1 - par, filled[s])
                    elif job == "XT":
                        pe.wait_ge(rs_step, 6 * (n - 1))
                        for k in range(KT):
                            last = pe.transpose(ring(job)[:, 128 * k:128 * k + 128],
                                                pay[:, par, 128 * k:128 * k + 128], ident[:, :])
                        last.then_inc(filled[s], 1)
                    elif job in ("QS", "KS"):
                        pe.wait_ge(split_lo, n + 2)
                        stack_rows(ring(job), int(job == "KS"), filled[s])
                    elif job == "RK":
                        rank(n - 3, ring(job), filled[s])
                    elif job == "LG":
                        pe.wait_ge(xT_ready, n - 1)
                        for k in range(KT):
                            last = pe.matmul(ring(job)[:, 0:NE], xT32[:, k, :], wr[:, k, :], start=(k == 0),
                                             stop=(k == KT - 1))
                        last.then_inc(filled[s], 1)
                    elif job == "NMT":
                        wait_emptied(pe, "A7", n)
                        for tc in range(KT):
                            for J in range(NJ):
                                last = pe.transpose(ring(job)[:, T * J + 128 * tc:T * J + 128 * tc + 128],
                                                    nmx[:, tc, J, :, :].rearrange("p g c -> p (g c)"), ident[:, :])
                        last.then_inc(filled[s], 1)
                if has(kind, "B7"):
                    weigh(7, n, kind, 1 - par)

            periods(pe, period)

            def gate_up(i, k, par, fresh):
                buf = k % 2
                if not fresh:
                    pe.wait_ge(h_done, i - 1)
                n = 0
                for kt in range(KT):
                    for a, w in ((0, 0), (0, 1), (1, 0)):
                        last = pe.matmul(ps[:, buf, 0:2 * M], xT[:, k, kt, a, :], W[:, par, kt, w, :],
                                         start=(n == 0), stop=(n == 5))
                        n += 1
                last.then_inc(gu_done, 1)

            def turn(i, buf, fresh):
                pe.wait_ge(h_done, i + 1)
                if not fresh:
                    pe.wait_ge(hT_lo, i - 1)
                for c in range(2):
                    last = pe.transpose(ps[0:MH, 2 + buf, 128 * c:128 * c + 128], h[:, buf, MH * c:MH * c + MH],
                                        ident[:, :])
                last.then_inc(hT_filled, 1)

            def down(i, buf, par, fresh):
                pe.wait_ge(hT_lo, i + 1)
                if not fresh:
                    pe.wait_ge(acc_done, i - 1 + B)
                n = 0
                for c in range(2):
                    for a, w in ((0, 0), (0, 1), (1, 0)):
                        last = pe.matmul(ps[:, 4 + buf, 0:T], hT[:, buf, a, c, :], D[:, par, c, w, :],
                                         start=(n == 0), stop=(n == 5))
                        n += 1
                last.then_inc(y_done, 1)

            pe.wait_ge(xT_lo, B)
            for job in ("WO", "XT", "LG"):
                wait_emptied(pe, job, B + 1)
            for i in range(2 * B + 2):
                if i < 2 * B:
                    pe.wait_ge(w_lo, 2 * (i // B + 1))
                    gate_up(i, i % B, i // B, i < 2)
                if 1 <= i <= 2 * B:
                    turn(i - 1, (i - 1) % 2, i < 3)
                if i >= 2:
                    down(i - 2, i % 2, (i - 2) // B, i < 4)
                if i == RANK_AT:
                    pe.wait_ge(o_step, 3 * B)
                    rank(B - 1, od(0), rank7_filled)
                if i == COUNT_AT:
                    pe.wait_ge(dp_step, DISPATCH_STEPS * B + 1)
                    pe.matmul(od(1)[:, 0:NE], ones16[:, :], emsum[:, :], start=True, stop=True)\
                      .then_inc(counts_filled, 1)
                if i == TABLE_AT:
                    pe.wait_ge(tb_step, TABLE_STEPS)
                    for k in range(2):
                        last = pe.matmul(od(0)[0:1, 128 * k:128 * k + 128], cols[:, 6 + k:7 + k], ident[:, :],
                                         start=True, stop=True)
                    last.then_inc(table_filled, 1)

            def turn_x(b, j):
                if not until(b):
                    return
                buf = j % 2
                pe.wait_ge(bx_in[j], (b - j) * 4 + 16)
                if since(b, 2):
                    pe.wait_ge(bxT_done, b - 1)
                for k in range(KT):
                    last = pe.transpose(ps[:, 6 + buf, 128 * k:128 * k + 128], bx[:, j, 128 * k:128 * k + 128],
                                        ident[:, :])
                last.then_inc(bxT_filled, 1)

            def step(b, j):
                buf = j % 2
                turn_x(b + 1, (j + 1) % WB)
                if until(b):
                    pe.wait_ge(bxT_done, b + 1)
                    pe.wait_ge(bw_in[j], (b - j) * 12 + 48)
                    if since(b, 2):
                        pe.wait_ge(bh_done, b - 1)
                    for k in range(KT):
                        last = pe.matmul(ps[:, buf, 0:2 * M], bxT[:, buf, k, :],
                                         bw[:, j, k, :, :].rearrange("p a m -> p (a m)"), start=(k == 0),
                                         stop=(k == KT - 1))
                    last.then_inc(bgu_done, 1)
                if since(b, 1) and until(b - 1):
                    pe.wait_ge(bh_done, b)
                    if since(b, 3):
                        pe.wait_ge(bhT_done, b - 2)
                    for c in range(2):
                        last = pe.transpose(ps[0:MH, 3 - buf, 128 * c:128 * c + 128],
                                            bh[:, 1 - buf, MH * c:MH * c + MH], ident[:, :])
                    last.then_inc(bhT_filled, 1)
                if since(b, 2) and until(b - 2):
                    pe.wait_ge(bhT_done, b - 1)
                    if since(b, 4):
                        pe.wait_ge(by_done, b - 3)
                    for c in range(2):
                        last = pe.matmul(ps[:, 4 + buf, 0:T], bhT[:, buf, c, :], bd[:, (j - 2) % WB, c, :],
                                         start=(c == 0), stop=(c == 1))
                    last.then_inc(by_filled, 1)

            pe.wait_ge(acc_done, 3 * B)
            pe.wait_ge(table_ready, 1)
            turn_x(0, 0)
            blocks(pe, step)

        @block.vector
        def _(dve):
            dve.memset(zeros[:, :], 0.0).then_inc(memsets, 1)
            for tile in (nmx[:, :, :, :, :], pick[:, :, :, :, :, :], onesM[:, :, :], kM[:, :, :, :, :],
                         q2M[:, :, :, :, :], vM[:, :, :, :, :]):
                dve.memset(tile, 0.0).then_inc(memsets, 1)
            dve.memset(filling[:, :], 0.0).then_inc(memsets, 1)
            dve.memset(ones[:, :], 1.0).then_inc(memsets, 1)
            dve.memset(ones16[:, :], 1.0).then_inc(memsets, 1)
            dve.memset(emsum[:, :], 0.0).then_inc(dp_step, 1)
            for k in range(B):
                dve.memset(acc[:, k, :], 0.0).then_inc(acc_done, 1)
            dve.wait_ge(memsets, 10)
            for J in range(NJ):
                dve.memset(onesM[:, J, :].rearrange("p (g c) -> p g c", c=32)[:, :, KC * J:KC * J + KC], 1.0)
            dve.wait_ge(pool_setup, 7)
            dve.tensor_copy(tri16[:, :], tri[:, :])
            dve.tensor_copy(counts[:, :], counting[:, :]).then_inc(setup_done, 1)
            dve.wait_ge(setup_done, 1)
            dve.tensor_copy(filling[:, T:T + 1], number[:, B:B + 1])
            by_group = ident[:, :].rearrange("p (g j c) -> p j g c", g=NG, j=NJ)
            for which, rows in enumerate(((0, 1), (2,), (0, 2), (1,))):
                for r in rows:
                    for J in range(NJ):
                        dve.tensor_copy(pick[:, which, J, :, r, :], by_group[:, J, :, :])
            dve.tensor_reduce(onesrow[:, :], ob[:, 0:NG], AXX, ALU.max).then_inc(setup_done, 1)
            dve.wait_ge(x_in, 16)
            for b in range(B):
                dve.bn_stats(st[:, b, :], xs[:, b, :]).then_inc(ln1, 1)
            dve.wait_ge(ln1, B)
            for b in range(B):
                dve.bn_aggr(mv[:, b, :], st[:, b, :]).then_inc(ln1, 1)
            dve.wait_ge(ln1, 2 * B)
            dve.tensor_scalar(ve[:, :], mv[:, :, 1], EPS, None, ALU.add).then_inc(ln1, 1)
            dve.wait_ge(ln1_act, 2)
            step = link(dve, ln1, 2 * B + 1, 4)
            step(dve.tensor_tensor(r1[:, :], r0[:, :], r0[:, :], ALU.mult))
            step(dve.tensor_tensor(r2[:, :], r1[:, :], ve[:, :], ALU.mult))
            step(dve.tensor_scalar(r3[:, :], r2[:, :], -0.5, 1.5, ALU.mult, ALU.add))
            step(dve.tensor_tensor(rstd[:, :, 0], r3[:, :], r0[:, :], ALU.mult))

            def norm_x(b, par):
                dve.tensor_scalar(xnb[:, par, :], xs[:, b, :], mv[:, b, 0:1], rstd[:, b, 0:1], ALU.subtract, ALU.mult)\
                   .then_inc(xn_ready, 1)

            def split(p):
                dve.tensor_copy(qkh[:, :, :], qk32[:, :, :]).then_inc(split_hi, 1)

            norm_x(0, 0)
            dve.wait_ge(qkv0_ready, 2)
            split(0)

            def maxima(u, n, kind):
                tc, J = divmod(u, NJ)
                wait_filled(dve, f"A{u}", n)
                if u == 0 and kind > 0:
                    wait_filled(dve, "NMT", n - 1)
                dve.tensor_reduce(nmx[:, tc, J, :, ROW], ring(f"A{u}").rearrange("p (g s) -> p g s", g=NG), AXX,
                                  ALU.max, negate=True).then_inc(emptied[slot(f"A{u}")], 1)

            def stack_maxima(n, par, kind):
                wait_filled(dve, "NMT", n)
                if kind > 0:
                    dve.wait_ge(q2_masked, 4 * n)
                dve.tensor_tensor(q2S[:, :, :], ring("NMT").rearrange("p (j t) -> p j t", j=NJ), qS[:, par, :, :],
                                  ALU.add).then_inc(emptied[slot("NMT")], 1)
                wait_emptied(dve, "NMT", n)
                for g in range(NG):
                    rows = slice(32 * g, 32 * g + 32)
                    dve.tensor_copy(q2M[rows, par, :, g, :], q2S[rows, :, :]).then_inc(q2_masked, 1)

            def keep_keys(n, par, kind):
                if kind > 0:
                    wait_filled(dve, "B7", n)
                dve.tensor_copy(kB[:, :, :], kS[:, par, :, :]).then_inc(keys_kept, 1)

            def norm_o(n, par):
                dve.wait_ge(p_used, 8 * n)
                step = link(dve, o_step, 3 * (n - 1), 3)
                step(dve.reciprocal(rD[:, :], od(par)[:, T:2 * T]))
                step(dve.tensor_tensor(on[:, :], od(par)[:, 0:T], rD[:, :], ALU.mult))
                step(dve.tensor_scalar(ob[:, :], on[:, :], bias[:, 2:3], None, ALU.add))

            def residual(n):
                c = n - 2
                wait_filled(dve, "WO", n)
                step = link(dve, x1_step, 5 * c, 5)
                dve.tensor_scalar(wo_t[:, :], ring("WO")[:, 0:T], bias[:, 3:4], tg[:, 0:1], ALU.add, ALU.mult)\
                   .then_inc(emptied[slot("WO")], 1)
                wait_emptied(dve, "WO", n)
                step(dve.scalar_tensor_tensor(out=xs[:, c, :], in0=wo_t[:, :], scalar=1.0, in1=xs[:, c, :],
                                              op0=ALU.mult, op1=ALU.add, accum_out=st2[:, 0:1]))
                step(dve.tensor_scalar(mv2[:, 0:1], st2[:, 0:1], 1.0 / T, None, ALU.mult))
                step(dve.tensor_scalar(xc[:, :], xs[:, c, :], mv2[:, 0:1], None, ALU.subtract))
                step(dve.scalar_tensor_tensor(out=wo_t[:, :], in0=xc[:, :], scalar=1.0, in1=xc[:, :], op0=ALU.mult,
                                              op1=ALU.mult, accum_out=st2[:, 1:2]))
                step(dve.tensor_scalar(ve2[:, :], st2[:, 1:2], 1.0 / T, EPS, ALU.mult, ALU.add))

            def norm_x1(n, kind):
                c = n - 2
                dve.wait_ge(rs_act, 2 * c + 2)
                if kind > 2:
                    wait_filled(dve, "XT", n - 1)
                if kind > 2:
                    dve.wait_ge(sent[kind % 2], (c - kind % 2) * (8 * TOPK) + 16)
                step = link(dve, rs_step, 6 * c, 6)
                step(dve.tensor_tensor(s1[:, :], s0[:, :], s0[:, :], ALU.mult))
                step(dve.tensor_tensor(s2[:, :], s1[:, :], ve2[:, :], ALU.mult))
                step(dve.tensor_scalar(s3[:, :], s2[:, :], -0.5, 1.5, ALU.mult, ALU.add))
                step(dve.tensor_tensor(rstd2[:, :], s3[:, :], s0[:, :], ALU.mult))
                step(dve.tensor_copy(pay[:, kind % 2, T:T + 1], number[:, bass.ds(c, 1)]))
                step(dve.tensor_scalar(pay[:, kind % 2, 0:T], xc[:, :], rstd2[:, 0:1], None, ALU.mult))

            def route(n, par):
                c = n - 2
                wait_emptied(dve, "LG", n)
                step = link(dve, rt_step, ROUTE_STEPS * c, ROUTE_STEPS)
                NQ = NE // GROUPS

                def row(i, w=NE):
                    return rt[:, i, 0:w]
                step(dve.tensor_scalar(row(0), el[:, :], 1.0, None, ALU.add))
                step(dve.reciprocal(row(1), row(0)))
                step(dve.tensor_tensor(row(2), row(1), corr[:, :], ALU.add))
                q = row(2).rearrange("p (g q) -> p g q", q=NQ)
                pair = q.rearrange("p g (a b) -> p g a b", b=2)
                hi, lo = row(3, 16), row(4, 16)
                step(dve.tensor_tensor(hi.rearrange("p (g a) -> p g a", a=2), pair[:, :, :, 0], pair[:, :, :, 1], ALU.max))
                step(dve.tensor_tensor(lo.rearrange("p (g a) -> p g a", a=2), pair[:, :, :, 0], pair[:, :, :, 1], ALU.min))
                hv, lv = hi.rearrange("p (g a) -> p g a", a=2), lo.rearrange("p (g a) -> p g a", a=2)
                step(dve.tensor_tensor(row(5, 8), hv[:, :, 0], hv[:, :, 1], ALU.max))
                step(dve.tensor_tensor(row(6, 8), hv[:, :, 0], hv[:, :, 1], ALU.min))
                step(dve.tensor_tensor(row(7, 8), lv[:, :, 0], lv[:, :, 1], ALU.max))
                step(dve.tensor_tensor(row(8, 8), row(6, 8), row(7, 8), ALU.max))
                step(dve.tensor_tensor(row(9, 8), row(5, 8), row(8, 8), ALU.add))

                def best(values, width, count, r):
                    dve.tensor_copy(row(r + 1, 8), values[:, 0:8])
                    step(dve.max(row(r, 8), values))
                    kth = row(r, 8)[:, count - 1:count]
                    step(dve.tensor_scalar(row(r + 1, width), values, kth, None, ALU.is_gt))
                    step(dve.tensor_reduce(row(r + 2, 1), row(r + 1, width), AXX, ALU.add))
                    step(dve.tensor_scalar(row(r + 3, width), values, kth, None, ALU.is_equal))
                    step(dve.tensor_tensor_scan(row(r + 4, width), ones[:, 0:width], row(r + 3, width), row(r + 2, 1),
                                                ALU.mult, ALU.add))
                    step(dve.scalar_tensor_tensor(out=row(r + 5, width), in0=row(r + 4, width), scalar=float(count),
                                                  in1=row(r + 3, width), op0=ALU.is_le, op1=ALU.mult))
                    step(dve.tensor_tensor(row(r, width), row(r + 5, width), row(r + 1, width), ALU.add))
                    return row(r, width)

                gm = best(row(9, 8), 8, TOPG, 10)
                gmb = gm.unsqueeze(2).to_broadcast([128, GROUPS, NQ])
                step(dve.tensor_tensor(row(16).rearrange("p (g q) -> p g q", q=NQ), q, gmb, ALU.mult))
                step(dve.tensor_scalar(row(9, 8), gm, -1.0, 3.0e38, ALU.add, ALU.mult))
                step(dve.tensor_tensor(row(17).rearrange("p (g q) -> p g q", q=NQ),
                                       row(16).rearrange("p (g q) -> p g q", q=NQ),
                                       row(9, 8).unsqueeze(2).to_broadcast([128, GROUPS, NQ]), ALU.add))
                em = best(row(17), NE, TOPK, 18)
                step(dve.tensor_tensor(pay[:, par, T + 1:PAY], em, row(1), ALU.mult))
                step(dve.tensor_copy(em16[:, :], em))

            def dispatch(c, par):
                step = link(dve, dp_step, DISPATCH_STEPS * c + 1, DISPATCH_STEPS)
                step(dve.tensor_tensor(dp[:, 1, :], dp[:, 0, :], em16[:, :], ALU.mult))
                dve.tensor_copy(dp[:, 2, 8:16], dp[:, 1, 0:8])
                step(dve.max(dp[:, 2, 0:8], dp[:, 1, :]))
                step(dve.tensor_scalar(place[:, par, :], dp[:, 2, 0:TOPK], -1.0, None, ALU.add))
                step(dve.tensor_tensor(emsum[:, :], emsum[:, :], em16[:, :], ALU.add))

            def period(kind, n):
                par = kind % 2
                if has(kind, "PROJ"):
                    if kind > 0:
                        wait_filled(dve, "PROJ", n - 1)
                    norm_x(n + 1, 1 - par)
                for u in range(8):
                    if has(kind, f"A{u}"):
                        maxima(u, n, kind)
                    if u == 1 and has(kind, "WO"):
                        residual(n)
                    if u == 2 and has(kind, "RK"):
                        wait_filled(dve, "RK", n)
                        dve.tensor_tensor(dp[:, 0, :], ring("RK")[:, 0:NE], first_row, ALU.add)\
                           .then_inc(emptied[slot("RK")], 1)
                        wait_emptied(dve, "RK", n)
                        dispatch(n - 3, 1 - par)
                    if u == 3 and has(kind, "WO"):
                        norm_x1(n, kind)
                    if u == 4 and has(kind, "PROJ"):
                        wait_emptied(dve, "PROJ", n)
                        dve.wait_ge(k_masked, 4 * (n + 1))
                        split(n + 1)
                if has(kind, "NMT"):
                    stack_maxima(n, par, kind)
                    keep_keys(n, par, kind)
                if has(kind, "LG"):
                    route(n, par)
                if has(kind, "B7"):
                    if kind > 1:
                        wait_filled(dve, "WO", n)
                    norm_o(n, 1 - par)

            periods(dve, period)

            for par in range(2):
                dve.wait_ge(w_hi, 2 * par + 2)
                dve.scalar_tensor_tensor(out=W[:, par, :, 1, :], in0=wraw[:, par, :, :, :].rearrange("p k a m -> p k (a m)"),
                                         scalar=WS, in1=W[:, par, :, 0, :], op0=ALU.mult, op1=ALU.subtract)\
                   .then_inc(w_lo, 1)
                dve.scalar_tensor_tensor(out=D[:, par, :, 1, :], in0=draw[:, par, :, :], scalar=WS, in1=D[:, par, :, 0, :],
                                         op0=ALU.mult, op1=ALU.subtract).then_inc(w_lo, 1)

            def low(i, buf):
                dve.wait_ge(hT_hi, i + 1)
                dve.tensor_tensor(hT[:, buf, 1, :, :], ps[0:MH, 2 + buf, 0:256].rearrange("p (c t) -> p c t", c=2),
                                  hT[:, buf, 0, :, :], ALU.subtract).then_inc(hT_lo, 1)

            def add(i):
                k = i % B
                dve.wait_ge(y_done, i + 1)
                dve.wait_ge(acc_done, i + 1)
                dve.scalar_tensor_tensor(out=acc[:, k, :], in0=ps[:, 4 + i % 2, 0:T], scalar=1.0 / WS, in1=acc[:, k, :],
                                         op0=ALU.mult, op1=ALU.add).then_inc(acc_done, 1)

            def make_table():
                dve.wait_ge(counts_filled, 1)
                n_e = od(1)[:, 0:NE]
                step = link(dve, tb_step, 0, TABLE_STEPS)
                step(dve.tensor_tensor(pad_place[:, 0:NE], n_e, pad_row[:, 0:NE], ALU.add))
                step(dve.tensor_tensor(over[:, :, :], n_e.unsqueeze(2).to_broadcast([128, NE, 8]), full, ALU.is_gt))
                step(dve.tensor_reduce(tb[:, 0, :], over[:, :, :], AXX, ALU.add))
                step(dve.tensor_tensor_scan(tb[:, 1, :], ones[:, 0:NE], tb[:, 0, :], zeros[:, 0:1], ALU.mult, ALU.add))
                b = number[:, 0:1]
                step(dve.scalar_tensor_tensor(out=tb[:, 2, :], in0=tb[:, 1, :], scalar=b, in1=ones[:, 0:NE],
                                              op0=ALU.is_le, op1=ALU.mult, accum_out=cols[:, 0:1]))
                step(dve.scalar_tensor_tensor(out=tb[:, 3, :], in0=tb[:, 1, :], scalar=b, in1=tb[:, 0, :],
                                              op0=ALU.is_le, op1=ALU.mult, accum_out=cols[:, 1:2]))
                step(dve.tensor_tensor(cols[:, 2:3], b, cols[:, 1:2], ALU.subtract))
                step(dve.tensor_scalar(cols[:, 3:4], cols[:, 2:3], 128.0, None, ALU.mult))
                step(dve.scalar_tensor_tensor(out=cols[:, 4:5], in0=cols[:, 0:1], scalar=float(CAP), in1=cols[:, 3:4],
                                              op0=ALU.mult, op1=ALU.add))
                step(dve.tensor_scalar(cols[:, 6:7], cols[:, 4:5], float(SPARE), None, ALU.min))
                step(dve.tensor_scalar(cols[:, 7:8], cols[:, 0:1], float(NE - 1), None, ALU.min))

            dve.wait_ge(zeroed, 16 * 3)
            for i in range(2 * B + 3):
                if i < 2 * B:
                    dve.wait_ge(silu_done, i + 1)
                    if i >= 2:
                        dve.wait_ge(hT_filled, i - 1)
                    dve.scalar_tensor_tensor(out=h[:, i % 2, :], in0=ps[:, i % 2, M:2 * M], scalar=1.0 / WS,
                                             in1=sg[:, i % 2, :], op0=ALU.mult, op1=ALU.mult).then_inc(h_done, 1)
                if 1 <= i <= 2 * B:
                    low(i - 1, (i - 1) % 2)
                if i >= 3:
                    add(i - 3)
                if i == RANK_AT:
                    dve.wait_ge(rank7_filled, 1)
                    dve.tensor_tensor(dp[:, 0, :], od(0)[:, 0:NE], first_row, ALU.add).then_inc(rank7_read, 1)
                    dve.wait_ge(rank7_read, 1)
                    dispatch(B - 1, (B - 1) % 2)
                if i == COUNT_AT:
                    make_table()
                if i == TABLE_AT:
                    dve.wait_ge(table_filled, 1)
                    dve.tensor_copy(table[:, :], od(0)[0:1, 0:256]).then_inc(table_ready, 1)
            for b in range(B):
                dve.wait_ge(acc_done, 2 * B + b + 1)
                dve.scalar_tensor_tensor(out=xs[:, b, :], in0=acc[:, b, :], scalar=tg[:, 1:2], in1=xs[:, b, :],
                                         op0=ALU.mult, op1=ALU.add).then_inc(fin_done, 1)

            def step(b, j):
                buf = j % 2
                if until(b):
                    dve.wait_ge(bx_in[j], (b - j) * 4 + 16)
                    if since(b, WB):
                        dve.wait_ge(added[buf], (b - buf) * 8 - 16)
                    dve.tensor_copy(bid[:, j:j + 1], bx[:, j, T:T + 1]).then_inc(bid_done, 1)
                    e = dve.value_load(table[0:1, bass.ds(b + 128, 1)], min_val=0, max_val=NE - 1)
                    dve.wait_ge(bsilu_done, b + 1)
                    dve.wait_ge(bid_done, b + 1)
                    if since(b, 2):
                        dve.wait_ge(bhT_filled, b - 1)
                    dve.scalar_tensor_tensor(out=bh[:, buf, :], in0=ps[:, buf, M:2 * M],
                                             scalar=bx[:, j, bass.ds(e + (T + 1), 1)], in1=bsg[:, buf, :],
                                             op0=ALU.mult, op1=ALU.mult).then_inc(bh_done, 1)
                if since(b, 1) and until(b - 1):
                    dve.wait_ge(bhT_filled, b)
                    if since(b, 3):
                        dve.wait_ge(by_filled, b - 2)
                    dve.tensor_copy(bhT[:, 1 - buf, :, :],
                                    ps[0:MH, 3 - buf, 0:256].rearrange("p (c t) -> p c t", c=2)).then_inc(bhT_done, 1)
                if since(b, 2) and until(b - 2):
                    dve.wait_ge(by_filled, b - 1)
                    if since(b, 6):
                        dve.wait_ge(added[buf], (b - buf) * 8 - 32)
                    dve.tensor_copy(by[:, (j - 2) % WB, :], ps[:, 4 + buf, 0:T]).then_inc(by_done, 1)

            dve.wait_ge(fin_done, B)
            blocks(dve, step)
            dve.wait_ge(sums_in, 32)
            for b in range(B):
                dve.tensor_tensor(acc1[:, b, :], acc[:, b, :], acc1[:, b, :], ALU.add).then_inc(tail_sum, 1)
            for b in range(B):
                dve.wait_ge(tail_sum, b + 1)
                dve.scalar_tensor_tensor(out=xs[:, b, :], in0=acc1[:, b, :], scalar=tg[:, 1:2], in1=xs[:, b, :],
                                         op0=ALU.mult, op1=ALU.add).then_inc(out_ready, 1)

    return nc


_INS = ["x", "ctx_2048", "g_xattn", "g_ffn", "L0_xattn_Wq", "L0_xattn_bq", "L0_xattn_Wk", "L0_xattn_bk",
        "L0_xattn_Wv", "L0_xattn_bv", "L0_xattn_Wo", "L0_xattn_bo", "L0_ffn_w_router", "L0_ffn_corr_bias",
        "L0_ffn_gate_w", "L0_ffn_up_w", "L0_ffn_down_w", "L0_ffn_sh_gate_w", "L0_ffn_sh_up_w", "L0_ffn_sh_down_w"]
_OUT = (8, 128, 256)


def kernel(**inputs):
    import numpy as np
    import concourse.bacc as bacc
    from concourse.bass_utils import run_bass_kernel_spmd

    nc = bacc.Bacc("TRN2", target_bir_lowering=False, num_devices=1)
    arrays, args = {}, []
    for name in _INS:
        a = np.ascontiguousarray(inputs[name])
        arrays[f"in_{name}"] = a
        args.append(nc.dram_tensor(f"in_{name}", a.shape, mybir.dt.from_np(a.dtype), kind="ExternalInput").ap())
    args.append(nc.dram_tensor("out", _OUT, F32, kind="ExternalOutput").ap())
    build(nc, *args)
    return run_bass_kernel_spmd(nc, [arrays], core_ids=[0]).results[0]["out"]
```

```python
from contextlib import ExitStack

import concourse.bass as bass
from concourse import mybir

F32 = mybir.dt.float32
F16 = mybir.dt.float16
I32 = mybir.dt.int32
U32 = mybir.dt.uint32
ALU = mybir.AluOpType
ACT = mybir.ActivationFunctionType
AXX = mybir.AxisListType.X

B, C, T = 8, 128, 256
NH, KC = 16, 8
NG, NJ = 4, 4
NE, M = 32, 176
MH = M // 2
KT = T // 128
GROUPS, TOPG, TOPK = 8, 4, 6
SCALE = float(KC) ** -0.5
EPS = 1e-5
WS = 64.0
ROW = 3 * KC
ROUTE_STEPS = 29
DISPATCH_STEPS = 4
N = B * C
CAP = N + 128
SPARE = NE * CAP
NB = (N * TOPK + NE * 127) // 128
PAY = T + 1 + NE
WB = 4
WR = 8
WW = KT * 2 * 2 * M
WD = 2 * 2 * T
WX = WW + WD
TABLE_STEPS = 12
PACK_AT = ["A1", "A3", "A5", "A7"]
RANK_AT, COUNT_AT, TABLE_AT = 0, 2, 5
PADS_AT = 4
POOL_PADS = NE - (2 * B - PADS_AT)
RING = 3
NP = 4

TURNS = ["A0", "A1", "B0", "WO", "A2", "RK", "B1", "PROJ", "A3", "B2", "A4", "B3", "XT", "A5", "B4",
         "QS", "KS", "A6", "A7", "B5", "LG", "NMT", "B6", "B7"]
DVE_TURNS = ["next x", "A0", "A1", "residual", "A2", "places", "weights0", "A3", "norm", "A4", "split", "A5", "row",
             "weights1", "A6", "A7", "maxima", "weights2", "route", "weights3", "out"]
USES = [len(TURNS[s::RING]) for s in range(RING)]


def slot(job):
    return TURNS.index(job) % RING


def use(job, n):
    return USES[slot(job)] * n + TURNS.index(job) // RING


def build(nc, x, ctx_in, g_xattn, g_ffn, Wq, bq, Wk, bk, Wv, bv, Wo, bo, w_router, corr_bias,
          gate_w, up_w, down_w, sh_gate_w, sh_up_w, sh_down_w, out):
    with ExitStack() as stack:
        def sb(name, shape, dt=F32):
            return stack.enter_context(nc.sbuf_tensor(name, shape, dt))

        def sem(name):
            return stack.enter_context(nc.semaphore(name))

        ident = sb("ident", [128, 128])
        zeros = sb("zeros", [128, 128])
        ones = sb("ones", [128, NE])
        pick = sb("pick", [128, 4, NJ, NG, 4, KC], F16)
        onesrow = sb("onesrow", [128, 1])
        onesM = sb("onesM", [128, NJ, 128])
        wnat = sb("wnat", [128, 4, 128])
        wT = sb("wT", [128, 4, 128])
        bias = sb("bias", [128, 4])
        gates = sb("gates", [128, 2])
        tg = sb("tg", [128, 2])
        wr = sb("wr", [128, KT, NE])
        corr = sb("corr", [128, NE])
        xs = sb("xs", [128, B, T])
        st = sb("st", [128, B, 6])
        mv = sb("mv", [128, B, 2])
        ve = sb("ve", [128, B])
        lnv = sb("lnv", [128, B])
        r0 = sb("r0", [128, B])
        r1 = sb("r1", [128, B])
        r2 = sb("r2", [128, B])
        r3 = sb("r3", [128, B])
        rstd = sb("rstd", [128, B, 1])
        xnb = sb("xnb", [128, 2, T])
        ctxb = sb("ctxb", [128, B, T])
        ctxv = sb("ctxv", [128, T])
        qk32 = sb("qk32", [128, 2, T])
        v32 = sb("v32", [128, KT, 128])
        qkh = sb("qkh", [128, 2, T], F16)
        qkl = sb("qkl", [128, 2, T], F16)
        qS = sb("qS", [128, 2, NJ, T], F16)
        kS = sb("kS", [128, 2, NJ, T], F16)
        kB = sb("kB", [128, NJ, T], F16)
        wide = sb("wide", [128, (2 * 2 * NJ * NG * T) // 2 + NP * NG * T])
        half_wide = NJ * NG * T
        kM = wide[:, 0:half_wide].bitcast(F16).rearrange("p (b j g t) -> p b j g t", b=2, j=NJ, g=NG)
        q2S = sb("q2S", [128, NJ, T], F16)
        q2M = wide[:, half_wide:2 * half_wide].bitcast(F16).rearrange("p (b j g t) -> p b j g t", b=2, j=NJ, g=NG)
        vM = sb("vM", [128, 2, KT, NJ, 128])
        nmx = sb("nmx", [128, KT, NJ, NG, 32])
        Pb = wide[:, 2 * half_wide:].rearrange("p (n g t) -> p n g t", n=NP, g=NG)
        ring_w = wide[:, 0:WR * WX // 2].bitcast(F16)
        rD = sb("rD", [128, T])
        on = sb("on", [128, T])
        ob = sb("ob", [128, T])
        wo_t = sb("wo_t", [128, T])
        st2 = sb("st2", [128, 6])
        mv2 = sb("mv2", [128, 2])
        ve2 = sb("ve2", [128, 1])
        ln2 = sb("ln2", [128, 1])
        s0 = sb("s0", [128, 1])
        s1 = sb("s1", [128, 1])
        s2 = sb("s2", [128, 1])
        s3 = sb("s3", [128, 1])
        rstd2 = sb("rstd2", [128, 1])
        xc = sb("xc", [128, T])
        xn2 = sb("xn2", [128, T])
        pay = sb("pay", [128, 2, PAY])
        pay16 = [pay[:, i, 0:T].bitcast(F16) for i in range(2)]
        xT32 = sb("xT32", [128, KT, 128])
        xT = sb("xT", [128, B, KT, 2, 128], F16)
        el = sb("el", [128, NE])
        rt = sb("rt", [128, 24, NE])
        tri = sb("tri", [128, 128])
        tri16 = sb("tri16", [128, 128], F16)
        ones16 = sb("ones16", [128, 128], F16)
        em16 = sb("em16", [128, NE], F16)
        emsum = sb("emsum", [128, NE], F16)
        counting = sb("counting", [128, 2 * (NE + 1) + (B + 1) + 8 * NE], I32)
        counts = sb("counts", [128, 2 * (NE + 1) + (B + 1) + 8 * NE])
        first_row = counts[:, 0:NE]
        pad_row = counts[:, NE + 1:2 * NE + 2]
        number = counts[:, 2 * NE + 2:2 * NE + 3 + B]
        full = counts[:, 2 * NE + 3 + B:].rearrange("p (e k) -> p e k", k=8)
        dp = sb("dp", [128, 3, NE])
        place = sb("place", [128, 2, TOPK], U32)
        pad_place = sb("pad_place", [128, NE], U32)
        filling = sb("filling", [128, PAY])
        tb = sb("tb", [128, 4, NE])
        over = sb("over", [128, NE, 8])
        cols = sb("cols", [128, 9])
        delta = sb("delta", [128, 2, NE])
        row_of = sb("row_of", [1, 128], I32)
        expert_of = sb("expert_of", [1, 128], I32)
        loads_of = sb("loads_of", [1, 128], I32)
        place_of = sb("place_of", [1, 2 + 128], I32)
        blocks_to = sb("blocks_to", [1, NE], I32)
        wraw = sb("wraw", [128, 2, KT, 2, M])
        draw = sb("draw", [MH, 2, 2, T])
        pk = sb("pk", [128, 2, WX], F16)
        W = pk[:, :, 0:WW].rearrange("p b (k a m) -> p b k a m", k=KT, a=2)
        D = pk[0:MH, :, WW:WX].rearrange("p b (c a n) -> p b c a n", c=2, a=2)
        sg = sb("sg", [128, 2, M])
        h = sb("h", [128, 2, M])
        hT = sb("hT", [MH, 2, 2, 2, 128], F16)
        acc = sb("acc", [128, B, T])
        acc1 = vM[:, :, :, :, :].rearrange("p a b c d -> p (a b c d)").rearrange("p (b t) -> p b t", b=B)
        bx = sb("bx", [128, WB, PAY])
        bid = sb("bid", [128, WB], U32)
        ident16 = sb("ident16", [128, 128], F16)
        bxT = sb("bxT", [128, 2, 2, KT, 128], F16)
        bsg = sb("bsg", [128, 2, M])
        bh = sb("bh", [128, 2, M])
        bhT = sb("bhT", [MH, 2, 2, 2, 128], F16)
        by = sb("by", [128, WB, T])
        tick = sb("tick", [128, 2])

        XS = nc.dram_tensor("rows_by_expert", (SPARE + 128, PAY), F32).ap()
        PACK = nc.dram_tensor("split_weights", (NE, 128, WX), F16).ap()
        SUM = [nc.dram_tensor(f"routed_sum{i}", (N + 128, T), F32).ap() for i in range(2)]

        ps = stack.enter_context(nc.psum_tensor("ps", [128, 8, 512], F32))

        def ring(job):
            s = slot(job)
            return ps[:, 2 * s:2 * s + 2, :].rearrange("p a b -> p (a b)")

        def od(par):
            return ps[:, 6 + par, :]

        filled = [sem(f"ring_filled{s}") for s in range(RING)]
        emptied = [sem(f"ring_emptied{s}") for s in range(RING)]
        consts_in = sem("consts_in")
        x_in = sem("x_in")
        ctx_in_s = sem("ctx_in_s")
        ctx_placed = sem("ctx_placed")
        memsets = sem("memsets")
        pool_setup = sem("pool_setup")
        setup_done = sem("setup_done")
        wt_filled = sem("wt_filled")
        wt_ready = sem("wt_ready")
        proj0_filled = sem("proj0_filled")
        qkv0_ready = sem("qkv0_ready")
        qs0_filled = sem("qs0_filled")
        ks0_filled = sem("ks0_filled")
        stacks0_ready = sem("stacks0_ready")
        keys_kept = sem("keys_kept")
        tanh_done = sem("tanh_done")
        ln1 = sem("ln1")
        ln1_act = sem("ln1_act")
        xn_ready = sem("xn_ready")
        split_hi = sem("split_hi")
        split_lo = sem("split_lo")
        v_masked = sem("v_masked")
        k_masked = sem("k_masked")
        q2_masked = sem("q2_masked")
        p_used = sem("p_used")
        o_step = sem("o_step")
        x1_step = sem("x1_step")
        rs_act = sem("rs_act")
        rs_step = sem("rs_step")
        xT_ready = sem("xT_ready")
        xT_lo = sem("xT_lo")
        sig_exp = sem("sig_exp")
        rt_step = sem("rt_step")
        w_in = [sem("w_in0"), sem("w_in1")]
        w_scaled = sem("w_scaled")
        w_hi = sem("w_hi")
        w_lo = sem("w_lo")
        gu_done = sem("gu_done")
        silu_done = sem("silu_done")
        h_done = sem("h_done")
        hT_filled = sem("hT_filled")
        hT_hi = sem("hT_hi")
        hT_lo = sem("hT_lo")
        y_done = sem("y_done")
        acc_done = sem("acc_done")
        fin_done = sem("fin_done")
        dp_step = sem("dp_step")
        sent = [sem("sent0"), sem("sent1")]
        pads_sent = sem("pads_sent")
        more_pads_sent = sem("more_pads_sent")
        zeroed = sem("zeroed")
        rank7_filled = sem("rank7_filled")
        counts_filled = sem("counts_filled")
        tb_step = sem("tb_step")
        table_filled = sem("table_filled")
        table_ready = sem("table_ready")
        bx_in = [sem(f"bx_in{j}") for j in range(WB)]
        stored = sem("stored")
        experts_in = sem("experts_in")
        bhT_hi = sem("bhT_hi")
        bid_done = sem("bid_done")
        bxT_filled = sem("bxT_filled")
        bxT_done = sem("bxT_done")
        bgu_done = sem("bgu_done")
        bsilu_done = sem("bsilu_done")
        bh_done = sem("bh_done")
        bhT_filled = sem("bhT_filled")
        bhT_done = sem("bhT_done")
        by_filled = sem("by_filled")
        by_done = sem("by_done")
        added = [sem("added0"), sem("added1")]
        sums_in = sem("sums_in")
        tail_sum = sem("tail_sum")
        pay_step = sem("pay_step")
        send_tick = sem("send_tick")
        add_tick = sem("add_tick")
        rank7_read = sem("rank7_read")
        out_ready = sem("out_ready")
        out_done = sem("out_done")

        block = stack.enter_context(nc.Block())

        def wait_filled(eng, job, n):
            eng.wait_ge(filled[slot(job)], use(job, n) + 1)

        def wait_emptied(eng, job, n):
            eng.wait_ge(emptied[slot(job)], use(job, n) + 1)

        def link(eng, semaphore, base, count):
            done = [0]

            def step(instruction):
                done[0] += 1
                assert done[0] <= count
                instruction.then_inc(semaphore, 1)
                eng.wait_ge(semaphore, base + done[0])
            return step

        def periods(eng, period):
            period(0, 0)
            period(1, 1)
            period(2, 2)
            with eng.Fori(0, 2) as t:
                period(3, t * 2 + 3)
                period(4, t * 2 + 4)
            period(7, 7)
            period(8, 8)
            period(9, 9)

        def blocks(eng, step, begin=lambda b, count: None):
            def steps(start, b, count):
                given = begin(b, count)
                for u in range(count):
                    step(b + u, (start + u) % WB, u, given)

            first = 2 * WB - 1
            rounds = (NB - (WB - 1) - first) // WB
            steps(0, 0, first)
            with eng.Fori(0, rounds) as t:
                steps(first, t * WB + first, WB)
            steps(first, first + WB * rounds, NB + 2 - first - WB * rounds)

        def entries(engine, row, b, count, top):
            return nc.values_load_multi_w_load_instructions(
                row[0:1, bass.ds(b, count)], engines=[engine], min_val=0, max_val=top,
                skip_runtime_bounds_check_because="the tables' entries are bounded by how they are made")[1]

        def since(b, k):
            return not isinstance(b, int) or b >= k

        def until(b):
            return not isinstance(b, int) or b < NB

        def has(kind, job):
            if job[0] == "A" or job == "NMT":
                return kind < B
            if job[0] == "B":
                return 1 <= kind <= B
            if job in ("PROJ", "QS", "KS"):
                return kind < B - 1
            return kind >= (3 if job == "RK" else 2)

        @block.sync
        def _(sp):
            for i, w in enumerate((Wq, Wk, Wv, Wo)):
                sp.dma_start(wnat[:, i, :], w).then_inc(consts_in, 16)
            for i, v in enumerate((bq, bk, bv, bo)):
                sp.dma_start(bias[:, i:i + 1], v.rearrange("(p a) -> p a", a=1)).then_inc(consts_in, 16)
            sp.dma_start(ctxb[:, :, :], ctx_in.rearrange("b p t -> p b t")).then_inc(ctx_in_s, 16)
            for i, v in enumerate((g_xattn, g_ffn)):
                sp.dma_start(gates[:, i:i + 1], v.partition_broadcast(128)).then_inc(consts_in, 16)
            sp.dma_start(wr[:, :, :], w_router.rearrange("(k p) e -> p k e", p=128)).then_inc(consts_in, 16)
            sp.dma_start(corr[:, :], corr_bias.partition_broadcast(128)).then_inc(consts_in, 16)

            def load_expert(par, gate, up, down):
                sp.dma_start(wraw[:, par, :, 0, :], gate.rearrange("(k p) m -> p k m", p=128)).then_inc(w_in[par], 16)
                sp.dma_start(wraw[:, par, :, 1, :], up.rearrange("(k p) m -> p k m", p=128)).then_inc(w_in[par], 16)
                sp.dma_start(draw[:, par, :, :], down.rearrange("(c p) n -> p c n", p=MH)).then_inc(w_in[par], 16)

            for e in range(2):
                load_expert(e, gate_w[e], up_w[e], down_w[e])
            sp.wait_ge(acc_done, B)
            for total in SUM:
                sp.dma_start(total[0:N].rearrange("(b p) t -> p b t", p=128), acc[:, :, :]).then_inc(zeroed, 16)
            sp.dma_start(SUM[1][N:N + 128], acc[:, 0, :]).then_inc(zeroed, 16)

            def period(kind, n):
                if kind >= B:
                    return
                for i in range(4):
                    r = n * 4 + i
                    sp.wait_ge(w_lo, r * 2 + 2)
                    if kind < B - 1 or i < 2:
                        load_expert(i % 2, gate_w[r + 2], up_w[r + 2], down_w[r + 2])
                    else:
                        cols = slice((i - 2) * M, (i - 1) * M)
                        load_expert(i % 2, sh_gate_w[:, cols], sh_up_w[:, cols], sh_down_w[cols, :])
                    if kind > 0 or i > 0:
                        sp.wait_ge(stored, r * 16)
                    sp.dma_start(PACK[r], pk[:, i % 2, :]).then_inc(stored, 16)

            periods(sp, period)
            sp.wait_ge(stored, 16 * NE)
            sp.wait_ge(p_used, 8 * B)

            def fetch_expert(e, u):
                sp.dma_start(ring_w[:, WX * u:WX * u + WX], PACK[e]).then_inc(experts_in, 16)

            for e in range(WR):
                if e >= 1:
                    sp.wait_ge(experts_in, 16 * e)
                fetch_expert(e, e)
            sp.wait_ge(table_ready, 1)
            with sp.Fori(0, NE // WR - 1) as t:
                for u in range(WR):
                    last_block = sp.value_load(blocks_to[0:1, bass.ds(t * WR + u, 1)], min_val=1, max_val=NB + 1)
                    sp.wait_ge(experts_in, t * (16 * WR) + 16 * (u + WR))
                    sp.wait_ge(by_filled, last_block)
                    fetch_expert(t * WR + (WR + u), u)
            for i in range(2):
                sp.wait_ge(added[i], 16 * ((NB + 1 - i) // 2))
                sp.dma_start((acc, acc1)[i][:, :, :], SUM[i][0:N].rearrange("(b p) t -> p b t", p=128)).then_inc(sums_in, 16)
            for b in range(B):
                sp.wait_ge(out_ready, b + 1)
                sp.dma_start(out[b], xs[:, b, :]).then_inc(out_done, 16)
            sp.wait_ge(out_done, 16 * B)

        @block.gpsimd
        def _(pool):
            pool.sem_inc(send_tick, 1)
            pool.wait_ge(memsets, 1)
            nc.gpsimd.affine_select(out=ident[:, :], in_=zeros[:, :], compare_op=ALU.not_equal, fill=1.0, base=0,
                                    pattern=[[-1, 128]], channel_multiplier=1).then_inc(pool_setup, 1)
            nc.gpsimd.affine_select(out=ob[:, 0:NG], in_=zeros[:, 0:NG], compare_op=ALU.not_equal, fill=1.0,
                                    base=-ROW, pattern=[[-32, NG]], channel_multiplier=1).then_inc(pool_setup, 1)
            nc.gpsimd.affine_select(out=tri[:, :], in_=zeros[:, :], compare_op=ALU.is_ge, fill=1.0, base=0,
                                    pattern=[[-1, 128]], channel_multiplier=1).then_inc(pool_setup, 1)
            nc.gpsimd.iota(counting[:, 0:NE + 1], pattern=[[CAP, NE + 1]], base=1, channel_multiplier=0)\
                .then_inc(pool_setup, 1)
            nc.gpsimd.iota(counting[:, NE + 1:2 * NE + 2], pattern=[[CAP, NE + 1]], base=0, channel_multiplier=1)\
                .then_inc(pool_setup, 1)
            nc.gpsimd.iota(counting[:, 2 * NE + 2:2 * NE + 3 + B], pattern=[[128, B + 1]], base=0, channel_multiplier=1)\
                .then_inc(pool_setup, 1)
            nc.gpsimd.iota(counting[:, 2 * NE + 3 + B:], pattern=[[0, NE], [128, 8]], base=0, channel_multiplier=0)\
                .then_inc(pool_setup, 1)

            def split_low(p):
                pool.wait_ge(split_hi, p + 1)
                nc.gpsimd.tensor_tensor(qkl[:, :, :], qk32[:, :, :], qkh[:, :, :], ALU.subtract).then_inc(split_lo, 1)

            def mask_v(par):
                for s in range(KT):
                    for J in range(NJ):
                        cols = slice(KC * J, KC * J + KC)
                        nc.gpsimd.tensor_tensor(
                            vM[:, par, s, J, :].rearrange("p (g c) -> p g c", c=32)[:, :, cols],
                            v32[:, s, :].rearrange("p (g c) -> p g c", c=32)[:, :, cols],
                            zeros[:, :].rearrange("p (g c) -> p g c", c=32)[:, :, cols], ALU.add).then_inc(v_masked, 1)

            def place_ctx(b):
                nc.gpsimd.tensor_tensor(ctxv[:, 0:128], ctxb[:, b, 0:128], zeros[:, :], ALU.add).then_inc(ctx_placed, 1)
                nc.gpsimd.tensor_tensor(ctxv[:, 128:T], ctxb[:, b, 128:T], zeros[:, :], ALU.add).then_inc(ctx_placed, 1)

            pool.wait_ge(ctx_in_s, 16)
            place_ctx(0)
            pool.wait_ge(setup_done, 2)
            nc.gpsimd.dma_start(XS[SPARE:SPARE + 128], filling[:, :]).then_inc(sent[0], 16)
            nc.gpsimd.dma_start(SUM[0][N:N + 128, 0:T], filling[:, 0:T]).then_inc(sent[1], 16)
            pool.wait_ge(qkv0_ready, 3)
            split_low(0)
            mask_v(0)

            def low_weights(r, par):
                pool.wait_ge(w_hi, r * 2 + 2)
                nc.gpsimd.tensor_tensor(W[:, par, :, 1, :], wraw[:, par, :, :, :].rearrange("p k a m -> p k (a m)"),
                                        W[:, par, :, 0, :], ALU.subtract).then_inc(w_lo, 1)
                nc.gpsimd.tensor_tensor(D[:, par, :, 1, :], draw[:, par, :, :], D[:, par, :, 0, :], ALU.subtract)\
                    .then_inc(w_lo, 1)

            def period(kind, n):
                par = kind % 2
                packs = kind < B
                if has(kind, "PROJ"):
                    if kind == 0:
                        pool.wait_ge(proj0_filled, 1)
                    else:
                        wait_filled(pool, "PROJ", n - 1)
                    place_ctx(n + 1)
                if packs:
                    low_weights(n * 4, 0)
                if has(kind, "PROJ"):
                    split_low(n + 1)
                if packs:
                    low_weights(n * 4 + 1, 1)
                if has(kind, "XT"):
                    c = n - 2
                    wait_emptied(pool, "XT", n)
                    nc.gpsimd.tensor_tensor(xT[:, c, :, 1, :], xT32[:, :, :], xT[:, c, :, 0, :], ALU.subtract)\
                        .then_inc(xT_lo, 1)
                if has(kind, "PROJ"):
                    wait_emptied(pool, "PROJ", n)
                    pool.wait_ge(p_used, 8 * n)
                    mask_v(1 - par)
                if packs:
                    low_weights(n * 4 + 2, 0)
                if has(kind, "RK"):
                    send(n - 3, 1 - par)
                if packs:
                    low_weights(n * 4 + 3, 1)
                if kind == B:
                    low_weights(NE, 0)
                    low_weights(NE + 1, 1)

            def send(c, par):
                pool.wait_ge(dp_step, DISPATCH_STEPS * (c + 1) + 1)
                pool.wait_ge(send_tick, c + 1)
                nc.gpsimd.tensor_tensor(tick[:, 0:1], zeros[:, 0:1], zeros[:, 0:1], ALU.add).then_inc(send_tick, 1)
                for k in range(TOPK):
                    nc.gpsimd.indirect_dma_start(XS, bass.IndirectOffsetOnAxis(ap=place[:, par, k:k + 1], axis=0),
                                                 pay[:, par, :], None).then_inc(sent[par], 16)

            periods(pool, period)
            send(B - 1, (B - 1) % 2)
            pool.wait_ge(tb_step, 1)
            for e in range(POOL_PADS):
                nc.gpsimd.indirect_dma_start(XS, bass.IndirectOffsetOnAxis(ap=pad_place[:, e:e + 1], axis=0),
                                             filling[:, :], None).then_inc(pads_sent, 16)

            def add_block(b, j, u, given):
                if not until(b):
                    return
                buf = j % 2
                pool.wait_ge(by_done, b + 1)
                pool.wait_ge(bid_done, b + 1)
                if since(b, 2):
                    pool.wait_ge(added[buf], (b - buf) * 8)
                pool.wait_ge(add_tick, b)
                nc.gpsimd.tensor_tensor(tick[:, 1:2], zeros[:, 0:1], zeros[:, 0:1], ALU.add).then_inc(add_tick, 1)
                nc.gpsimd.indirect_dma_start(SUM[buf], bass.IndirectOffsetOnAxis(ap=bid[:, j:j + 1], axis=0),
                                             by[:, j, :], None, compute_op=ALU.add).then_inc(added[buf], 16)

            pool.wait_ge(zeroed, 16 * 3)
            pool.wait_ge(sent[1], 16)
            blocks(pool, add_block)

        @block.scalar
        def _(act):
            act.dma_start(xs[:, :, :], x.rearrange("b p t -> p b t")).then_inc(x_in, 16)
            act.wait_ge(consts_in, 16 * 12)
            act.activation(tg[:, :], gates[:, :], ACT.Tanh).then_inc(tanh_done, 1)
            act.wait_ge(wt_filled, 1)
            act.activation(wT[:, :, :], ring("A0")[:, 0:512].rearrange("p (a b) -> p a b", a=4), ACT.Copy)\
               .then_inc(wt_ready, 1)
            act.wait_ge(ln1, 17)
            act.activation(lnv[:, :], ve[:, :], ACT.Ln).then_inc(ln1_act, 1)
            act.wait_ge(ln1_act, 1)
            act.activation(r0[:, :], lnv[:, :], ACT.Exp, scale=-0.5).then_inc(ln1_act, 1)

            def evacuate_qkv(src, semaphore, each):
                for i in range(2):
                    ins = act.activation(qk32[:, i, :], src[:, i * T:(i + 1) * T], ACT.Identity, bias=bias[:, i:i + 1])
                    if each:
                        ins.then_inc(semaphore, 1)
                act.activation(v32[:, :, :], src[:, 512:768].rearrange("p (a b) -> p a b", a=KT), ACT.Copy)\
                   .then_inc(semaphore, 1)

            def stack_q(src, par, semaphore):
                act.activation(qS[:, par, :, :], src.rearrange("p (j t) -> p j t", j=NJ), ACT.Copy).then_inc(semaphore, 1)

            def stack_k(src, par, semaphore):
                act.activation(kS[:, par, :, :], src.rearrange("p (j t) -> p j t", j=NJ), ACT.Identity,
                               bias=onesrow[:, 0:1]).then_inc(semaphore, 1)

            def mask_k(par):
                for g in range(NG):
                    rows = slice(32 * g, 32 * g + 32)
                    act.activation(kM[rows, par, :, g, :], kS[rows, par, :, :], ACT.Copy).then_inc(k_masked, 1)

            def exps(u, b, n, kind):
                wait_filled(act, f"B{u}", n)
                if not (kind == 1 and u < NP):
                    act.wait_ge(p_used, 8 * b + u - NP + 1)
                act.activation(Pb[:, u % NP, :, :], ring(f"B{u}").rearrange("p (g t) -> p g t", g=NG), ACT.Exp,
                               scale=SCALE).then_inc(emptied[slot(f"B{u}")], 1)

            act.wait_ge(proj0_filled, 1)
            evacuate_qkv(ring("A1"), qkv0_ready, True)
            act.wait_ge(qs0_filled, 1)
            act.wait_ge(setup_done, 2)
            stack_q(ring("B0"), 0, stacks0_ready)
            act.wait_ge(ks0_filled, 1)
            stack_k(ring("A0"), 0, stacks0_ready)
            act.wait_ge(stacks0_ready, 2)
            mask_k(0)

            def scale_weights(r, par):
                act.wait_ge(w_in[par], (r - par) * 24 + 48)
                act.activation(wraw[:, par, :, :, :], wraw[:, par, :, :, :], ACT.Copy, scale=WS).then_inc(w_scaled, 1)
                act.activation(draw[:, par, :, :], draw[:, par, :, :], ACT.Copy, scale=WS).then_inc(w_scaled, 1)

            def period(kind, n):
                par = kind % 2
                c = n - 2
                for job in TURNS:
                    if job in PACK_AT[:4 if kind < B else 2 if kind == B else 0]:
                        i = PACK_AT.index(job)
                        scale_weights(n * 4 + i, i % 2)
                    if not has(kind, job):
                        continue
                    if job[0] == "B":
                        exps(int(job[1]), n - 1, n, kind)
                    elif job == "WO":
                        act.wait_ge(x1_step, 5 * c + 5)
                        act.activation(ln2[:, :], ve2[:, :], ACT.Ln).then_inc(rs_act, 1)
                        act.wait_ge(rs_act, 2 * c + 1)
                        act.activation(s0[:, :], ln2[:, :], ACT.Exp, scale=-0.5).then_inc(rs_act, 1)
                    elif job == "PROJ":
                        wait_filled(act, job, n)
                        act.wait_ge(v_masked, 8 * (n + 1))
                        act.wait_ge(split_lo, n + 1)
                        evacuate_qkv(ring(job), emptied[slot(job)], False)
                    elif job == "XT":
                        wait_filled(act, job, n)
                        if kind > 2:
                            act.wait_ge(xT_lo, c)
                            wait_filled(act, "LG", n - 1)
                        act.activation(xT32[:, :, :], ring(job)[:, 0:256].rearrange("p (k t) -> p k t", k=KT), ACT.Copy)\
                           .then_inc(xT_ready, 1)
                        act.activation(xT[:, c, :, 0, :], ring(job)[:, 0:256].rearrange("p (k t) -> p k t", k=KT),
                                       ACT.Copy).then_inc(emptied[slot(job)], 1)
                    elif job == "QS":
                        wait_filled(act, job, n)
                        if kind >= 1:
                            wait_emptied(act, "NMT", n - 1)
                        stack_q(ring(job), 1 - par, emptied[slot(job)])
                    elif job == "KS":
                        wait_filled(act, job, n)
                        if kind >= 1:
                            act.wait_ge(keys_kept, n)
                        stack_k(ring(job), 1 - par, emptied[slot(job)])
                        wait_emptied(act, job, n)
                        if kind >= 1:
                            wait_filled(act, "A7", n - 1)
                        mask_k(1 - par)
                    elif job == "LG":
                        wait_filled(act, job, n)
                        act.wait_ge(rt_step, ROUTE_STEPS * c)
                        act.activation(el[:, :], ring(job)[:, 0:NE], ACT.Exp, scale=-1.0).then_inc(emptied[slot(job)], 1)

            periods(act, period)

            def high(i, buf, fresh=False):
                act.wait_ge(hT_filled, i + 1)
                if not fresh:
                    act.wait_ge(y_done, i - 1)
                act.activation(hT[:, buf, 0, :, :], ps[0:MH, 2 + buf, 0:256].rearrange("p (c t) -> p c t", c=2),
                               ACT.Copy).then_inc(hT_hi, 1)

            for i in range(2 * B):
                buf = i % 2
                act.wait_ge(gu_done, i + 1)
                if i >= 2:
                    act.wait_ge(h_done, i - 1)
                act.activation(sg[:, buf, :], ps[:, buf, 0:M], ACT.Silu, scale=1.0 / WS).then_inc(silu_done, 1)
                if i >= 1:
                    high(i - 1, 1 - buf, i < 3)
                if i == PADS_AT:
                    act.wait_ge(tb_step, 1)
                if i >= PADS_AT:
                    e = POOL_PADS + i - PADS_AT
                    row, = entries(mybir.EngineType.Activation, pad_place, e, 1, SPARE)
                    act.dma_start(XS[bass.ds(row, 128)], filling[:, :]).then_inc(more_pads_sent, 16)
            high(2 * B - 1, 1)

            def fetch(b, j, row):
                if since(b, WB):
                    act.wait_ge(bh_done, b - WB + 1)
                act.dma_start(bx[:, j, :], XS[bass.ds(row, 128)]).then_inc(bx_in[j], 16)

            def keep_xT(b, buf):
                if not until(b):
                    return
                loads = act.value_load(loads_of[0:1, bass.ds(b, 1)], min_val=16, max_val=16 * NE)
                act.wait_ge(experts_in, loads)
                act.wait_ge(bxT_filled, b + 1)
                if since(b, 2):
                    act.wait_ge(bgu_done, b - 1)
                act.activation(bxT[:, buf, :, :, :],
                               ps[:, 6 + buf, :].bitcast(F16)[:, 0:512].rearrange("p (a k t) -> p a k t", a=2, k=KT),
                               ACT.Copy).then_inc(bxT_done, 1)

            def begin(b, count):
                return entries(mybir.EngineType.Activation, row_of, b + WB - 1, count, SPARE)

            def step(b, j, u, rows):
                buf = j % 2
                keep_xT(b + 1, 1 - buf)
                if until(b):
                    act.wait_ge(bgu_done, b + 1)
                    if since(b, 2):
                        act.wait_ge(bh_done, b - 1)
                    act.activation(bsg[:, buf, :], ps[:, buf, 0:M], ACT.Silu, scale=1.0 / WS).then_inc(bsilu_done, 1)
                if until(b + WB - 1):
                    fetch(b + WB - 1, (j + WB - 1) % WB, rows[u])
                if since(b, 1) and until(b - 1):
                    act.wait_ge(bhT_filled, b)
                    if since(b, 3):
                        act.wait_ge(by_filled, b - 1)
                    act.activation(bhT[:, 1 - buf, 0, :, :], ps[0:MH, 3 - buf, 0:256].rearrange("p (c t) -> p c t", c=2),
                                   ACT.Copy).then_inc(bhT_hi, 1)

            for par in range(2):
                act.wait_ge(sent[par], 16 * TOPK * B // 2 + 16)
            act.wait_ge(pads_sent, 16 * POOL_PADS)
            act.wait_ge(more_pads_sent, 16 * (NE - POOL_PADS))
            act.wait_ge(table_ready, 1)
            first_rows = entries(mybir.EngineType.Activation, row_of, 0, WB - 1, SPARE)
            for b in range(WB - 1):
                fetch(b, b, first_rows[b])
            keep_xT(0, 0)
            blocks(act, step, begin)

        @block.tensor
        def _(pe):
            def take(job, n, first=False):
                before = use(job, n)
                if not (isinstance(before, int) and before == 0):
                    pe.wait_ge(emptied[slot(job)], before)

            pe.wait_ge(consts_in, 16 * 12)
            pe.wait_ge(pool_setup, 1)
            for i in range(4):
                last = pe.transpose(ring("A0")[:, 128 * i:128 * i + 128], wnat[:, i, :], ident[:, :])
            last.then_inc(wt_filled, 1)

            def project(dst, par, b, semaphore):
                pe.matmul(dst[:, 0:T], wT[:, 0, :], xnb[:, par, :], start=True, stop=True)
                pe.matmul(dst[:, T:2 * T], wT[:, 1, :], ctxb[:, b, :], start=True, stop=True)
                for s in range(KT):
                    last = pe.matmul(dst[:, 512 + 128 * s:640 + 128 * s], ctxv[:, 128 * s:128 * s + 128], wT[:, 2, :],
                                     start=True, stop=True)
                last.then_inc(semaphore, 1)

            def stack_rows(dst, side, semaphore):
                for J in range(NJ):
                    cols = slice(T * J, T * J + T)
                    pe.matmul(dst[:, cols], pick[:, 2 * side, J, :, :, :].rearrange("p g r c -> p (g r c)"),
                              qkh[:, side, :], start=True, stop=False)
                    last = pe.matmul(dst[:, cols], pick[:, 2 * side + 1, J, :, :, :].rearrange("p g r c -> p (g r c)"),
                                     qkl[:, side, :], start=False, stop=True)
                last.then_inc(semaphore, 1)

            pe.wait_ge(wt_ready, 1)
            pe.wait_ge(xn_ready, 1)
            pe.wait_ge(ctx_in_s, 16)
            pe.wait_ge(ctx_placed, 2)
            project(ring("A1"), 0, 0, proj0_filled)
            pe.wait_ge(split_lo, 1)
            pe.wait_ge(setup_done, 2)
            stack_rows(ring("B0"), 0, qs0_filled)
            stack_rows(ring("A0"), 1, ks0_filled)
            pe.wait_ge(stacks0_ready, 2)

            def scores_max(u, n, par):
                tc, J = divmod(u, NJ)
                if u == 0:
                    pe.wait_ge(k_masked, 4 * (n + 1))
                for half in range(2):
                    last = pe.matmul(ring(f"A{u}")[:, 512 * half:512 * half + 512],
                                     qS[:, par, J, 128 * tc:128 * tc + 128],
                                     kM[:, par, J, 2 * half:2 * half + 2, :].rearrange("p g s -> p (g s)"),
                                     start=True, stop=True)
                last.then_inc(filled[slot(f"A{u}")], 1)

            def scores_exp(u, n, par):
                sc, J = divmod(u, NJ)
                if u == 0:
                    pe.wait_ge(q2_masked, 4 * n)
                    pe.wait_ge(keys_kept, n)
                for half in range(2):
                    last = pe.matmul(ring(f"B{u}")[:, 512 * half:512 * half + 512],
                                     kB[:, J, 128 * sc:128 * sc + 128],
                                     q2M[:, par, J, 2 * half:2 * half + 2, :].rearrange("p g t -> p (g t)"),
                                     start=True, stop=True)
                last.then_inc(filled[slot(f"B{u}")], 1)

            def weigh(u, n, kind, par):
                b = n - 1
                sc, J = divmod(u, NJ)
                wait_emptied(pe, f"B{u}", n)
                if u == 0:
                    pe.wait_ge(v_masked, 8 * n)
                    if kind > 2:
                        pe.wait_ge(o_step, 3 * (b - 1))
                for g in range(NG):
                    rows = slice(32 * g, 32 * g + 32)
                    pe.matmul(od(par)[rows, 0:T], vM[:, par, sc, J, rows], Pb[:, u % NP, g, :],
                              start=(u == 0), stop=(u == 7), skip_group_check=True, tile_position=(0, 32 * g))
                    last = pe.matmul(od(par)[rows, T:2 * T], onesM[:, J, rows], Pb[:, u % NP, g, :],
                                     start=False, stop=(u == 7), skip_group_check=True, tile_position=(0, 32 * g))
                last.then_inc(p_used, 1)

            def rank(c, dst, semaphore):
                pe.wait_ge(rt_step, ROUTE_STEPS * (c + 1))
                pe.matmul(dst[:, 0:NE], tri16[:, :], em16[:, :], start=True, stop=False)
                pe.wait_ge(dp_step, DISPATCH_STEPS * c + 1)
                pe.matmul(dst[:, 0:NE], ones16[:, :], emsum[:, :], start=False, stop=True).then_inc(semaphore, 1)

            def period(kind, n):
                par = kind % 2
                for job in TURNS:
                    take(job, n)
                    s = slot(job)
                    if not has(kind, job):
                        pe.sem_inc(filled[s], 1)
                        pe.sem_inc(emptied[s], 1)
                        continue
                    if job[0] == "A":
                        scores_max(int(job[1]), n, par)
                    elif job[0] == "B":
                        u = int(job[1])
                        scores_exp(u, n, 1 - par)
                        if u > 0:
                            weigh(u - 1, n, kind, 1 - par)
                    elif job == "WO":
                        pe.wait_ge(o_step, 3 * (n - 1))
                        pe.matmul(ring(job)[:, 0:T], wT[:, 3, :], ob[:, :], start=True, stop=True).then_inc(filled[s], 1)
                    elif job == "PROJ":
                        pe.wait_ge(xn_ready, n + 2)
                        pe.wait_ge(ctx_placed, 2 * n + 4)
                        project(ring(job), 1 - par, n + 1, filled[s])
                    elif job == "XT":
                        pe.wait_ge(rs_step, 5 * (n - 1))
                        for k in range(KT):
                            last = pe.transpose(ring(job)[:, 128 * k:128 * k + 128],
                                                xn2[:, 128 * k:128 * k + 128], ident[:, :])
                        last.then_inc(filled[s], 1)
                    elif job in ("QS", "KS"):
                        pe.wait_ge(split_lo, n + 2)
                        stack_rows(ring(job), int(job == "KS"), filled[s])
                    elif job == "RK":
                        rank(n - 3, ring(job), filled[s])
                    elif job == "LG":
                        pe.wait_ge(xT_ready, n - 1)
                        for k in range(KT):
                            last = pe.matmul(ring(job)[:, 0:NE], xT32[:, k, :], wr[:, k, :], start=(k == 0),
                                             stop=(k == KT - 1))
                        last.then_inc(filled[s], 1)
                    elif job == "NMT":
                        wait_emptied(pe, "A7", n)
                        for tc in range(KT):
                            for J in range(NJ):
                                last = pe.transpose(ring(job)[:, T * J + 128 * tc:T * J + 128 * tc + 128],
                                                    nmx[:, tc, J, :, :].rearrange("p g c -> p (g c)"), ident[:, :])
                        last.then_inc(filled[s], 1)
                if has(kind, "B7"):
                    weigh(7, n, kind, 1 - par)

            periods(pe, period)

            def gate_up(i, k, par, fresh):
                buf = k % 2
                if not fresh:
                    pe.wait_ge(h_done, i - 1)
                n = 0
                for kt in range(KT):
                    for a, w in ((0, 0), (0, 1), (1, 0)):
                        last = pe.matmul(ps[:, buf, 0:2 * M], xT[:, k, kt, a, :], W[:, par, kt, w, :],
                                         start=(n == 0), stop=(n == 5))
                        n += 1
                last.then_inc(gu_done, 1)

            def turn(i, buf, fresh):
                pe.wait_ge(h_done, i + 1)
                if not fresh:
                    pe.wait_ge(hT_lo, i - 1)
                for c in range(2):
                    last = pe.transpose(ps[0:MH, 2 + buf, 128 * c:128 * c + 128], h[:, buf, MH * c:MH * c + MH],
                                        ident[:, :])
                last.then_inc(hT_filled, 1)

            def down(i, buf, par, fresh):
                pe.wait_ge(hT_lo, i + 1)
                if not fresh:
                    pe.wait_ge(acc_done, i - 1 + B)
                n = 0
                for c in range(2):
                    for a, w in ((0, 0), (0, 1), (1, 0)):
                        last = pe.matmul(ps[:, 4 + buf, 0:T], hT[:, buf, a, c, :], D[:, par, c, w, :],
                                         start=(n == 0), stop=(n == 5))
                        n += 1
                last.then_inc(y_done, 1)

            pe.wait_ge(xT_lo, B)
            for job in ("WO", "XT", "LG"):
                wait_emptied(pe, job, B + 1)
            for i in range(2 * B + 2):
                if i < 2 * B:
                    pe.wait_ge(w_lo, 2 * (NE + i // B + 1))
                    gate_up(i, i % B, i // B, i < 2)
                if 1 <= i <= 2 * B:
                    turn(i - 1, (i - 1) % 2, i < 3)
                if i >= 2:
                    down(i - 2, i % 2, (i - 2) // B, i < 4)
                if i == RANK_AT:
                    pe.wait_ge(o_step, 3 * B)
                    rank(B - 1, od(0), rank7_filled)
                if i == COUNT_AT:
                    pe.wait_ge(dp_step, DISPATCH_STEPS * B + 1)
                    pe.matmul(od(1)[:, 0:NE], ones16[:, :], emsum[:, :], start=True, stop=True)\
                      .then_inc(counts_filled, 1)
                if i == TABLE_AT:
                    pe.wait_ge(tb_step, TABLE_STEPS)
                    for k in range(3):
                        last = pe.matmul(od(0)[0:1, 128 * k:128 * k + 128], cols[:, 6 + k:7 + k],
                                         ident[:, :], start=True, stop=True)
                    last.then_inc(table_filled, 1)

            def turn_x(b, j):
                if not until(b):
                    return
                buf = j % 2
                pe.wait_ge(bx_in[j], (b - j) * 4 + 16)
                for k in range(2 * KT):
                    part = slice(128 * k, 128 * k + 128)
                    last = pe.transpose(ps[:, 6 + buf, :].bitcast(F16)[:, part], bx[:, j, 0:T].bitcast(F16)[:, part],
                                        ident16[:, :])
                last.then_inc(bxT_filled, 1)

            def begin(b, count):
                return entries(mybir.EngineType.PE, place_of, b, count + 2, (WR - 1) * WX)

            def step(b, j, u, places):
                buf = j % 2
                place_2, place_0 = places[u], places[u + 2]
                turn_x(b + 1, (j + 1) % WB)
                if until(b):
                    pe.wait_ge(bxT_done, b + 1)
                    n = 0
                    for k in range(KT):
                        for a, w in ((0, 0), (0, 1), (1, 0)):
                            last = pe.matmul(ps[:, buf, 0:2 * M], bxT[:, buf, a, k, :],
                                             ring_w[:, bass.ds(place_0 + (2 * k + w) * 2 * M, 2 * M)],
                                             start=(n == 0), stop=(n == 5))
                            n += 1
                    last.then_inc(bgu_done, 1)
                if since(b, 1) and until(b - 1):
                    pe.wait_ge(bh_done, b)
                    for c in range(2):
                        last = pe.transpose(ps[0:MH, 3 - buf, 128 * c:128 * c + 128],
                                            bh[:, 1 - buf, MH * c:MH * c + MH], ident[:, :])
                    last.then_inc(bhT_filled, 1)
                if since(b, 2) and until(b - 2):
                    if not until(b - 1):
                        pe.wait_ge(bhT_done, b - 1)
                    n = 0
                    for c in range(2):
                        for a, w in ((0, 0), (0, 1), (1, 0)):
                            last = pe.matmul(ps[:, 4 + buf, 0:T], bhT[:, buf, a, c, :],
                                             ring_w[0:MH, bass.ds(place_2 + (WW + (2 * c + w) * T), T)],
                                             start=(n == 0), stop=(n == 5))
                            n += 1
                    last.then_inc(by_filled, 1)

            pe.wait_ge(acc_done, 3 * B)
            pe.wait_ge(table_ready, 1)
            pe.sem_inc(by_filled, 1)
            turn_x(0, 0)
            blocks(pe, step, begin)

        @block.vector
        def _(dve):
            dve.memset(zeros[:, :], 0.0).then_inc(memsets, 1)
            for tile in (nmx[:, :, :, :, :], pick[:, :, :, :, :, :], onesM[:, :, :], kM[:, :, :, :, :],
                         q2M[:, :, :, :, :], vM[:, :, :, :, :]):
                dve.memset(tile, 0.0).then_inc(memsets, 1)
            dve.memset(filling[:, :], 0.0).then_inc(memsets, 1)
            dve.memset(ones[:, :], 1.0).then_inc(memsets, 1)
            dve.memset(ones16[:, :], 1.0).then_inc(memsets, 1)
            dve.memset(pk[64:128, :, WW:WX], 0.0).then_inc(memsets, 1)
            dve.memset(delta[:, :, :], 0.0).then_inc(memsets, 1)
            dve.memset(place_of[:, 0:2], 0).then_inc(memsets, 1)
            dve.wait_ge(memsets, 13)
            dve.memset(delta[:, 0, 0:NE - 1], float(WX)).then_inc(memsets, 1)
            by_slot = delta[:, 0, :].rearrange("p (a b) -> p a b", b=WR)
            dve.wait_ge(memsets, 14)
            dve.memset(by_slot[:, 0:NE // WR - 1, WR - 1], -float(WX * (WR - 1))).then_inc(memsets, 1)
            dve.memset(delta[:, 1, 0:NE - 1], 1.0).then_inc(memsets, 1)
            dve.memset(emsum[:, :], 0.0).then_inc(dp_step, 1)
            for k in range(B):
                dve.memset(acc[:, k, :], 0.0).then_inc(acc_done, 1)
            dve.wait_ge(memsets, 16)
            for J in range(NJ):
                dve.memset(onesM[:, J, :].rearrange("p (g c) -> p g c", c=32)[:, :, KC * J:KC * J + KC], 1.0)
            dve.wait_ge(pool_setup, 7)
            dve.tensor_copy(tri16[:, :], tri[:, :])
            dve.tensor_copy(ident16[:, :], ident[:, :])
            dve.tensor_copy(counts[:, :], counting[:, :]).then_inc(setup_done, 1)
            dve.wait_ge(setup_done, 1)
            dve.tensor_copy(filling[:, T:T + 1], number[:, B:B + 1])
            by_group = ident[:, :].rearrange("p (g j c) -> p j g c", g=NG, j=NJ)
            for which, rows in enumerate(((0, 1), (2,), (0, 2), (1,))):
                for r in rows:
                    for J in range(NJ):
                        dve.tensor_copy(pick[:, which, J, :, r, :], by_group[:, J, :, :])
            dve.tensor_reduce(onesrow[:, :], ob[:, 0:NG], AXX, ALU.max).then_inc(setup_done, 1)
            dve.wait_ge(x_in, 16)
            for b in range(B):
                dve.bn_stats(st[:, b, :], xs[:, b, :]).then_inc(ln1, 1)
            dve.wait_ge(ln1, B)
            for b in range(B):
                dve.bn_aggr(mv[:, b, :], st[:, b, :]).then_inc(ln1, 1)
            dve.wait_ge(ln1, 2 * B)
            dve.tensor_scalar(ve[:, :], mv[:, :, 1], EPS, None, ALU.add).then_inc(ln1, 1)
            dve.wait_ge(ln1_act, 2)
            step = link(dve, ln1, 2 * B + 1, 4)
            step(dve.tensor_tensor(r1[:, :], r0[:, :], r0[:, :], ALU.mult))
            step(dve.tensor_tensor(r2[:, :], r1[:, :], ve[:, :], ALU.mult))
            step(dve.tensor_scalar(r3[:, :], r2[:, :], -0.5, 1.5, ALU.mult, ALU.add))
            step(dve.tensor_tensor(rstd[:, :, 0], r3[:, :], r0[:, :], ALU.mult))

            def norm_x(b, par):
                dve.tensor_scalar(xnb[:, par, :], xs[:, b, :], mv[:, b, 0:1], rstd[:, b, 0:1], ALU.subtract, ALU.mult)\
                   .then_inc(xn_ready, 1)

            def split(p):
                dve.tensor_copy(qkh[:, :, :], qk32[:, :, :]).then_inc(split_hi, 1)

            norm_x(0, 0)
            dve.wait_ge(qkv0_ready, 2)
            split(0)

            def maxima(u, n, kind):
                tc, J = divmod(u, NJ)
                wait_filled(dve, f"A{u}", n)
                if u == 0 and kind > 0:
                    wait_filled(dve, "NMT", n - 1)
                dve.tensor_reduce(nmx[:, tc, J, :, ROW], ring(f"A{u}").rearrange("p (g s) -> p g s", g=NG), AXX,
                                  ALU.max, negate=True).then_inc(emptied[slot(f"A{u}")], 1)

            def stack_maxima(n, par, kind):
                wait_filled(dve, "NMT", n)
                if kind > 0:
                    dve.wait_ge(q2_masked, 4 * n)
                dve.tensor_tensor(q2S[:, :, :], ring("NMT").rearrange("p (j t) -> p j t", j=NJ), qS[:, par, :, :],
                                  ALU.add).then_inc(emptied[slot("NMT")], 1)
                wait_emptied(dve, "NMT", n)
                for g in range(NG):
                    rows = slice(32 * g, 32 * g + 32)
                    dve.tensor_copy(q2M[rows, par, :, g, :], q2S[rows, :, :]).then_inc(q2_masked, 1)

            def keep_keys(n, par, kind):
                if kind > 0:
                    wait_filled(dve, "B7", n)
                dve.tensor_copy(kB[:, :, :], kS[:, par, :, :]).then_inc(keys_kept, 1)

            def norm_o(n, par):
                dve.wait_ge(p_used, 8 * n)
                step = link(dve, o_step, 3 * (n - 1), 3)
                step(dve.reciprocal(rD[:, :], od(par)[:, T:2 * T]))
                step(dve.tensor_tensor(on[:, :], od(par)[:, 0:T], rD[:, :], ALU.mult))
                step(dve.tensor_scalar(ob[:, :], on[:, :], bias[:, 2:3], None, ALU.add))

            def residual(n):
                c = n - 2
                wait_filled(dve, "WO", n)
                step = link(dve, x1_step, 5 * c, 5)
                dve.tensor_scalar(wo_t[:, :], ring("WO")[:, 0:T], bias[:, 3:4], tg[:, 0:1], ALU.add, ALU.mult)\
                   .then_inc(emptied[slot("WO")], 1)
                wait_emptied(dve, "WO", n)
                step(dve.scalar_tensor_tensor(out=xs[:, c, :], in0=wo_t[:, :], scalar=1.0, in1=xs[:, c, :],
                                              op0=ALU.mult, op1=ALU.add, accum_out=st2[:, 0:1]))
                step(dve.tensor_scalar(mv2[:, 0:1], st2[:, 0:1], 1.0 / T, None, ALU.mult))
                step(dve.tensor_scalar(xc[:, :], xs[:, c, :], mv2[:, 0:1], None, ALU.subtract))
                step(dve.scalar_tensor_tensor(out=wo_t[:, :], in0=xc[:, :], scalar=1.0, in1=xc[:, :], op0=ALU.mult,
                                              op1=ALU.mult, accum_out=st2[:, 1:2]))
                step(dve.tensor_scalar(ve2[:, :], st2[:, 1:2], 1.0 / T, EPS, ALU.mult, ALU.add))

            def norm_x1(n, kind):
                c = n - 2
                dve.wait_ge(rs_act, 2 * c + 2)
                if kind > 2:
                    wait_filled(dve, "XT", n - 1)
                step = link(dve, rs_step, 5 * c, 5)
                step(dve.tensor_tensor(s1[:, :], s0[:, :], s0[:, :], ALU.mult))
                step(dve.tensor_tensor(s2[:, :], s1[:, :], ve2[:, :], ALU.mult))
                step(dve.tensor_scalar(s3[:, :], s2[:, :], -0.5, 1.5, ALU.mult, ALU.add))
                step(dve.tensor_tensor(rstd2[:, :], s3[:, :], s0[:, :], ALU.mult))
                step(dve.tensor_scalar(xn2[:, :], xc[:, :], rstd2[:, 0:1], None, ALU.mult))

            def fill_row(n, par):
                c = n - 2
                if not isinstance(n, int) or n > 3:
                    dve.wait_ge(sent[par], (c - par) * (8 * TOPK) + 16)
                step = link(dve, pay_step, 3 * c, 3)
                step(dve.tensor_copy(pay[:, par, T:T + 1], number[:, bass.ds(c, 1)]))
                step(dve.tensor_copy(pay16[par][:, 0:T], xn2[:, :]))
                step(dve.tensor_tensor(pay16[par][:, T:2 * T], xn2[:, :], pay16[par][:, 0:T], ALU.subtract))

            def route(n, par):
                c = n - 2
                wait_emptied(dve, "LG", n)
                step = link(dve, rt_step, ROUTE_STEPS * c, ROUTE_STEPS)
                NQ = NE // GROUPS

                def row(i, w=NE):
                    return rt[:, i, 0:w]
                step(dve.tensor_scalar(row(0), el[:, :], 1.0, None, ALU.add))
                step(dve.reciprocal(row(1), row(0)))
                step(dve.tensor_tensor(row(2), row(1), corr[:, :], ALU.add))
                q = row(2).rearrange("p (g q) -> p g q", q=NQ)
                pair = q.rearrange("p g (a b) -> p g a b", b=2)
                hi, lo = row(3, 16), row(4, 16)
                step(dve.tensor_tensor(hi.rearrange("p (g a) -> p g a", a=2), pair[:, :, :, 0], pair[:, :, :, 1], ALU.max))
                step(dve.tensor_tensor(lo.rearrange("p (g a) -> p g a", a=2), pair[:, :, :, 0], pair[:, :, :, 1], ALU.min))
                hv, lv = hi.rearrange("p (g a) -> p g a", a=2), lo.rearrange("p (g a) -> p g a", a=2)
                step(dve.tensor_tensor(row(5, 8), hv[:, :, 0], hv[:, :, 1], ALU.max))
                step(dve.tensor_tensor(row(6, 8), hv[:, :, 0], hv[:, :, 1], ALU.min))
                step(dve.tensor_tensor(row(7, 8), lv[:, :, 0], lv[:, :, 1], ALU.max))
                step(dve.tensor_tensor(row(8, 8), row(6, 8), row(7, 8), ALU.max))
                step(dve.tensor_tensor(row(9, 8), row(5, 8), row(8, 8), ALU.add))

                def best(values, width, count, r):
                    dve.tensor_copy(row(r + 1, 8), values[:, 0:8])
                    step(dve.max(row(r, 8), values))
                    kth = row(r, 8)[:, count - 1:count]
                    step(dve.tensor_scalar(row(r + 1, width), values, kth, None, ALU.is_gt))
                    step(dve.tensor_reduce(row(r + 2, 1), row(r + 1, width), AXX, ALU.add))
                    step(dve.tensor_scalar(row(r + 3, width), values, kth, None, ALU.is_equal))
                    step(dve.tensor_tensor_scan(row(r + 4, width), ones[:, 0:width], row(r + 3, width), row(r + 2, 1),
                                                ALU.mult, ALU.add))
                    step(dve.scalar_tensor_tensor(out=row(r + 5, width), in0=row(r + 4, width), scalar=float(count),
                                                  in1=row(r + 3, width), op0=ALU.is_le, op1=ALU.mult))
                    step(dve.tensor_tensor(row(r, width), row(r + 5, width), row(r + 1, width), ALU.add))
                    return row(r, width)

                gm = best(row(9, 8), 8, TOPG, 10)
                gmb = gm.unsqueeze(2).to_broadcast([128, GROUPS, NQ])
                step(dve.tensor_tensor(row(16).rearrange("p (g q) -> p g q", q=NQ), q, gmb, ALU.mult))
                step(dve.tensor_scalar(row(9, 8), gm, -1.0, 3.0e38, ALU.add, ALU.mult))
                step(dve.tensor_tensor(row(17).rearrange("p (g q) -> p g q", q=NQ),
                                       row(16).rearrange("p (g q) -> p g q", q=NQ),
                                       row(9, 8).unsqueeze(2).to_broadcast([128, GROUPS, NQ]), ALU.add))
                em = best(row(17), NE, TOPK, 18)
                step(dve.scalar_tensor_tensor(out=pay[:, par, T + 1:PAY], in0=em, scalar=1.0 / WS, in1=row(1),
                                              op0=ALU.mult, op1=ALU.mult))
                step(dve.tensor_copy(em16[:, :], em))

            def dispatch(c, par):
                step = link(dve, dp_step, DISPATCH_STEPS * c + 1, DISPATCH_STEPS)
                step(dve.tensor_tensor(dp[:, 1, :], dp[:, 0, :], em16[:, :], ALU.mult))
                dve.tensor_copy(dp[:, 2, 8:16], dp[:, 1, 0:8])
                step(dve.max(dp[:, 2, 0:8], dp[:, 1, :]))
                step(dve.tensor_scalar(place[:, par, :], dp[:, 2, 0:TOPK], -1.0, None, ALU.add))
                step(dve.tensor_tensor(emsum[:, :], emsum[:, :], em16[:, :], ALU.add))

            def high_weights(r, par, kind):
                dve.wait_ge(w_scaled, r * 2 + 2)
                if kind > 0:
                    dve.wait_ge(stored, (r - 1) * 16)
                dve.tensor_copy(W[:, par, :, 0, :], wraw[:, par, :, :, :].rearrange("p k a m -> p k (a m)"))\
                   .then_inc(w_hi, 1)
                dve.tensor_copy(D[:, par, :, 0, :], draw[:, par, :, :]).then_inc(w_hi, 1)

            def period(kind, n):
                par = kind % 2
                for job in DVE_TURNS:
                    if job[0] == "A" and has(kind, job):
                        maxima(int(job[1]), n, kind)
                    elif job == "next x" and has(kind, "PROJ"):
                        if kind > 0:
                            wait_filled(dve, "PROJ", n - 1)
                        norm_x(n + 1, 1 - par)
                    elif job == "split" and has(kind, "PROJ"):
                        wait_emptied(dve, "PROJ", n)
                        dve.wait_ge(k_masked, 4 * (n + 1))
                        split(n + 1)
                    elif job == "residual" and has(kind, "WO"):
                        residual(n)
                    elif job == "norm" and has(kind, "WO"):
                        norm_x1(n, kind)
                    elif job == "row" and has(kind, "WO"):
                        fill_row(n, par)
                    elif job == "places" and has(kind, "RK"):
                        wait_filled(dve, "RK", n)
                        dve.tensor_tensor(dp[:, 0, :], ring("RK")[:, 0:NE], first_row, ALU.add)\
                           .then_inc(emptied[slot("RK")], 1)
                        wait_emptied(dve, "RK", n)
                        dispatch(n - 3, 1 - par)
                    elif job[0:7] == "weights":
                        i = int(job[7])
                        if kind < B or kind == B and i < 2:
                            high_weights(n * 4 + i, i % 2, kind if i < 2 else 1)
                    elif job == "maxima" and has(kind, "NMT"):
                        stack_maxima(n, par, kind)
                        keep_keys(n, par, kind)
                    elif job == "route" and has(kind, "LG"):
                        route(n, par)
                    elif job == "out" and has(kind, "B7"):
                        if kind > 1:
                            wait_filled(dve, "WO", n)
                        norm_o(n, 1 - par)

            periods(dve, period)

            def low(i, buf):
                dve.wait_ge(hT_hi, i + 1)
                dve.tensor_tensor(hT[:, buf, 1, :, :], ps[0:MH, 2 + buf, 0:256].rearrange("p (c t) -> p c t", c=2),
                                  hT[:, buf, 0, :, :], ALU.subtract).then_inc(hT_lo, 1)

            def add(i):
                k = i % B
                dve.wait_ge(y_done, i + 1)
                dve.wait_ge(acc_done, i + 1)
                dve.scalar_tensor_tensor(out=acc[:, k, :], in0=ps[:, 4 + i % 2, 0:T], scalar=1.0 / WS, in1=acc[:, k, :],
                                         op0=ALU.mult, op1=ALU.add).then_inc(acc_done, 1)

            def make_table():
                dve.wait_ge(counts_filled, 1)
                n_e = od(1)[:, 0:NE]
                step = link(dve, tb_step, 0, TABLE_STEPS)
                step(dve.tensor_tensor(pad_place[:, 0:NE], n_e, pad_row[:, 0:NE], ALU.add))
                step(dve.tensor_tensor(over[:, :, :], n_e.unsqueeze(2).to_broadcast([128, NE, 8]), full, ALU.is_gt))
                step(dve.tensor_reduce(tb[:, 0, :], over[:, :, :], AXX, ALU.add))
                step(dve.tensor_tensor_scan(tb[:, 1, :], ones[:, 0:NE], tb[:, 0, :], zeros[:, 0:1], ALU.mult, ALU.add))
                b = number[:, 0:1]
                step(dve.scalar_tensor_tensor(out=tb[:, 2, :], in0=tb[:, 1, :], scalar=b, in1=ones[:, 0:NE],
                                              op0=ALU.is_le, op1=ALU.mult, accum_out=cols[:, 0:1]))
                step(dve.scalar_tensor_tensor(out=tb[:, 3, :], in0=tb[:, 1, :], scalar=b, in1=tb[:, 0, :],
                                              op0=ALU.is_le, op1=ALU.mult, accum_out=cols[:, 1:2]))
                step(dve.tensor_tensor(cols[:, 2:3], b, cols[:, 1:2], ALU.subtract))
                step(dve.tensor_scalar(cols[:, 3:4], cols[:, 2:3], 128.0, None, ALU.mult))
                step(dve.scalar_tensor_tensor(out=cols[:, 4:5], in0=cols[:, 0:1], scalar=float(CAP), in1=cols[:, 3:4],
                                              op0=ALU.mult, op1=ALU.add))
                step(dve.tensor_scalar(cols[:, 6:7], cols[:, 4:5], float(SPARE), None, ALU.min))
                for k in range(2):
                    step(dve.scalar_tensor_tensor(out=tb[:, 2, :], in0=tb[:, 1, :], scalar=b, in1=delta[:, k, :],
                                                  op0=ALU.is_le, op1=ALU.mult, accum_out=cols[:, 7 + k:8 + k]))
                dve.tensor_scalar(blocks_to[:, :], tb[0:1, 1, :], 1.0, None, ALU.add)

            dve.wait_ge(zeroed, 16 * 3)
            for i in range(2 * B + 3):
                if i < 2 * B:
                    dve.wait_ge(silu_done, i + 1)
                    if i >= 2:
                        dve.wait_ge(hT_filled, i - 1)
                    dve.scalar_tensor_tensor(out=h[:, i % 2, :], in0=ps[:, i % 2, M:2 * M], scalar=1.0 / WS,
                                             in1=sg[:, i % 2, :], op0=ALU.mult, op1=ALU.mult).then_inc(h_done, 1)
                if 1 <= i <= 2 * B:
                    low(i - 1, (i - 1) % 2)
                if i >= 3:
                    add(i - 3)
                if i == RANK_AT:
                    dve.wait_ge(rank7_filled, 1)
                    dve.tensor_tensor(dp[:, 0, :], od(0)[:, 0:NE], first_row, ALU.add).then_inc(rank7_read, 1)
                    dve.wait_ge(rank7_read, 1)
                    dispatch(B - 1, (B - 1) % 2)
                if i == COUNT_AT:
                    make_table()
                if i == TABLE_AT:
                    dve.wait_ge(table_filled, 1)
                    row, weights, expert = (od(0)[0:1, 128 * k:128 * k + 128] for k in range(3))
                    dve.tensor_scalar(loads_of[:, :], expert, 1.0, 16.0, ALU.add, ALU.mult)
                    dve.tensor_copy(row_of[:, :], row)
                    dve.tensor_copy(place_of[:, 2:130], weights)
                    dve.tensor_copy(expert_of[:, :], expert).then_inc(table_ready, 1)
            for b in range(B):
                dve.wait_ge(acc_done, 2 * B + b + 1)
                dve.scalar_tensor_tensor(out=xs[:, b, :], in0=acc[:, b, :], scalar=tg[:, 1:2], in1=xs[:, b, :],
                                         op0=ALU.mult, op1=ALU.add).then_inc(fin_done, 1)

            def begin(b, count):
                return entries(mybir.EngineType.DVE, expert_of, b, count, NE - 1)

            def step(b, j, u, experts):
                buf = j % 2
                if until(b):
                    dve.wait_ge(bx_in[j], (b - j) * 4 + 16)
                    if since(b, WB):
                        dve.wait_ge(added[buf], (b - buf) * 8 - 16)
                    dve.tensor_copy(bid[:, j:j + 1], bx[:, j, T:T + 1]).then_inc(bid_done, 1)
                if since(b, 1) and until(b - 1):
                    dve.wait_ge(bhT_filled, b)
                    dve.wait_ge(bhT_hi, b)
                    dve.tensor_tensor(bhT[:, 1 - buf, 1, :, :], ps[0:MH, 3 - buf, 0:256].rearrange("p (c t) -> p c t", c=2),
                                      bhT[:, 1 - buf, 0, :, :], ALU.subtract).then_inc(bhT_done, 1)
                if until(b):
                    dve.wait_ge(bsilu_done, b + 1)
                    dve.wait_ge(bid_done, b + 1)
                    dve.scalar_tensor_tensor(out=bh[:, buf, :], in0=ps[:, buf, M:2 * M],
                                             scalar=bx[:, j, bass.ds(experts[u] + (T + 1), 1)], in1=bsg[:, buf, :],
                                             op0=ALU.mult, op1=ALU.mult).then_inc(bh_done, 1)
                if since(b, 2) and until(b - 2):
                    dve.wait_ge(by_filled, b)
                    if since(b, 6):
                        dve.wait_ge(added[buf], (b - buf) * 8 - 32)
                    dve.tensor_scalar(by[:, (j - 2) % WB, :], ps[:, 4 + buf, 0:T], 1.0 / WS, None, ALU.mult)\
                       .then_inc(by_done, 1)

            dve.wait_ge(fin_done, B)
            blocks(dve, step, begin)
            dve.wait_ge(sums_in, 32)
            for b in range(B):
                dve.tensor_tensor(acc1[:, b, :], acc[:, b, :], acc1[:, b, :], ALU.add).then_inc(tail_sum, 1)
            for b in range(B):
                dve.wait_ge(tail_sum, b + 1)
                dve.scalar_tensor_tensor(out=xs[:, b, :], in0=acc1[:, b, :], scalar=tg[:, 1:2], in1=xs[:, b, :],
                                         op0=ALU.mult, op1=ALU.add).then_inc(out_ready, 1)

    return nc


_INS = ["x", "ctx_2048", "g_xattn", "g_ffn", "L0_xattn_Wq", "L0_xattn_bq", "L0_xattn_Wk", "L0_xattn_bk",
        "L0_xattn_Wv", "L0_xattn_bv", "L0_xattn_Wo", "L0_xattn_bo", "L0_ffn_w_router", "L0_ffn_corr_bias",
        "L0_ffn_gate_w", "L0_ffn_up_w", "L0_ffn_down_w", "L0_ffn_sh_gate_w", "L0_ffn_sh_up_w", "L0_ffn_sh_down_w"]
_OUT = (8, 128, 256)


def kernel(**inputs):
    import numpy as np
    import concourse.bacc as bacc
    from concourse.bass_utils import run_bass_kernel_spmd

    nc = bacc.Bacc("TRN2", target_bir_lowering=False, num_devices=1)
    arrays, args = {}, []
    for name in _INS:
        a = np.ascontiguousarray(inputs[name])
        arrays[f"in_{name}"] = a
        args.append(nc.dram_tensor(f"in_{name}", a.shape, mybir.dt.from_np(a.dtype), kind="ExternalInput").ap())
    args.append(nc.dram_tensor("out", _OUT, F32, kind="ExternalOutput").ap())
    build(nc, *args)
    return run_bass_kernel_spmd(nc, [arrays], core_ids=[0]).results[0]["out"]
```

```python
from contextlib import ExitStack

import concourse.bass as bass
from concourse import mybir

F32 = mybir.dt.float32
F16 = mybir.dt.float16
I32 = mybir.dt.int32
U32 = mybir.dt.uint32
ALU = mybir.AluOpType
ACT = mybir.ActivationFunctionType
AXX = mybir.AxisListType.X

B, C, T = 8, 128, 256
NH, KC = 16, 8
NG, NJ = 4, 4
NE, M = 32, 176
MH = M // 2
KT = T // 128
GROUPS, TOPG, TOPK = 8, 4, 6
SCALE = float(KC) ** -0.5
EPS = 1e-5
WS = 64.0
ROW = 3 * KC
ROUTE_STEPS = 29
RSQRT_STEPS = 11
RSQRT_C = -2.0 ** 13
DISPATCH_STEPS = 4
TABLE_STEPS = 12
N = B * C
CAP = N + 128
SPARE = NE * CAP
NB = (N * TOPK + NE * 127) // 128
PAY = T + 1 + NE
RAW = 4
WB = 4
WR = 8
WW = KT * 2 * 2 * M
WD = 2 * 2 * T
WX = WW + WD
PACK_AT = ["PROJ", "B2", "A5", "B5"]
RANK_AT, COUNT_AT, TABLE_AT = 0, 2, 5
PADS_AT = 4
POOL_PADS = NE - (2 * B - PADS_AT)
RING = 3
NP = 4

TURNS = ["A0", "A1", "A2", "WO", "PROJ", "B0", "A3", "B1", "A4", "B2", "XT", "A5", "B3", "KS", "A6", "B4", "A7", "RK",
         "B5", "NMT", "LG", "QS", "B6", "B7"]
POOL_TURNS = ["values", "weights0", "split", "context", "weights1", "weights2", "row", "weights3", "send0", "send1",
              "xT", "send2"]
DVE_TURNS = ["weights0", "next x", "A0", "A1", "A2", "residual", "norm", "A3", "split", "A4", "weights1", "route1",
             "A5", "A6", "route2", "places", "A7", "weights2", "maxima", "weights3", "route0", "out"]
USES = [len(TURNS[s::RING]) for s in range(RING)]


def slot(job):
    return TURNS.index(job) % RING


def use(job, n):
    return USES[slot(job)] * n + TURNS.index(job) // RING


def build(nc, x, ctx_in, g_xattn, g_ffn, Wq, bq, Wk, bk, Wv, bv, Wo, bo, w_router, corr_bias,
          gate_w, up_w, down_w, sh_gate_w, sh_up_w, sh_down_w, out):
    with ExitStack() as stack:
        def sb(name, shape, dt=F32):
            return stack.enter_context(nc.sbuf_tensor(name, shape, dt))

        def sem(name):
            return stack.enter_context(nc.semaphore(name))

        ident = sb("ident", [128, 128])
        zeros = sb("zeros", [128, 128])
        ones = sb("ones", [128, NE])
        pick = sb("pick", [128, 4, NJ, NG, 4, KC], F16)
        onesrow = sb("onesrow", [128, 1])
        onesM = sb("onesM", [128, NJ, 128])
        wnat = sb("wnat", [128, 4, 128])
        wT = sb("wT", [128, 4, 128])
        bias = sb("bias", [128, 4])
        gates = sb("gates", [128, 2])
        tg = sb("tg", [128, 2])
        wr = sb("wr", [128, KT, NE])
        corr = sb("corr", [128, NE])
        xs = sb("xs", [128, B, T])
        st = sb("st", [128, B, 6])
        mv = sb("mv", [128, B, 2])
        ve = sb("ve", [128, B])
        r0 = sb("r0", [128, B])
        r1 = sb("r1", [128, B])
        rstd = sb("rstd", [128, B, 1])
        xnb = sb("xnb", [128, 2, T])
        ctxb = sb("ctxb", [128, B + 1, T])
        ctxv = sb("ctxv", [128, T])
        qk32 = sb("qk32", [128, 2, T])
        v32 = sb("v32", [128, KT, 128])
        qkh = sb("qkh", [128, 2, T], F16)
        qkl = sb("qkl", [128, 2, T], F16)
        qS = sb("qS", [128, 2, NJ, T], F16)
        kS = sb("kS", [128, 2, NJ, T], F16)
        kB = sb("kB", [128, NJ, T], F16)
        wide = sb("wide", [128, (2 * 2 * NJ * NG * T) // 2 + NP * NG * T])
        half_wide = NJ * NG * T
        kM = wide[:, 0:half_wide].bitcast(F16).rearrange("p (b j g t) -> p b j g t", b=2, j=NJ, g=NG)
        q2S = sb("q2S", [128, NJ, T], F16)
        q2M = wide[:, half_wide:2 * half_wide].bitcast(F16).rearrange("p (b j g t) -> p b j g t", b=2, j=NJ, g=NG)
        vM = sb("vM", [128, 2, KT, NJ, 128])
        nmx = sb("nmx", [128, KT, NJ, NG, 32])
        Pb = wide[:, 2 * half_wide:].rearrange("p (n g t) -> p n g t", n=NP, g=NG)
        ring_w = wide[:, 0:WR * WX // 2].bitcast(F16)
        rD = sb("rD", [128, T])
        on = sb("on", [128, T])
        ob = sb("ob", [128, T])
        wo_t = sb("wo_t", [128, T])
        st2 = sb("st2", [128, 6])
        mv2 = sb("mv2", [128, 2])
        ve2 = sb("ve2", [128, 1])
        s0 = sb("s0", [128, 1])
        s1 = sb("s1", [128, 1])
        xc = sb("xc", [128, T])
        xn2 = sb("xn2", [128, T])
        pay = sb("pay", [128, 2, PAY])
        pay16 = [pay[:, i, 0:T].bitcast(F16) for i in range(2)]
        xT32 = sb("xT32", [128, KT, 128])
        xT = sb("xT", [128, B, KT, 2, 128], F16)
        el = sb("el", [128, NE])
        rt = sb("rt", [128, 24, NE])
        tri = sb("tri", [128, 128])
        tri16 = sb("tri16", [128, 128], F16)
        ones16 = sb("ones16", [128, 128], F16)
        em16 = sb("em16", [128, NE], F16)
        emsum = sb("emsum", [128, NE], F16)
        counting = sb("counting", [128, 2 * (NE + 1) + (B + 1) + 8 * NE], I32)
        counts = sb("counts", [128, 2 * (NE + 1) + (B + 1) + 8 * NE])
        first_row = counts[:, 0:NE]
        pad_row = counts[:, NE + 1:2 * NE + 2]
        number = counts[:, 2 * NE + 2:2 * NE + 3 + B]
        full = counts[:, 2 * NE + 3 + B:].rearrange("p (e k) -> p e k", k=8)
        dp = sb("dp", [128, 3, NE])
        place = sb("place", [128, 2, TOPK], U32)
        pad_place = sb("pad_place", [128, NE], U32)
        filling = sb("filling", [128, PAY])
        tb = sb("tb", [128, 4, NE])
        over = sb("over", [128, NE, 8])
        cols = sb("cols", [128, 9])
        delta = sb("delta", [128, 2, NE])
        row_of = sb("row_of", [1, 128], I32)
        expert_of = sb("expert_of", [1, 128], I32)
        loads_of = sb("loads_of", [1, 128], I32)
        place_of = sb("place_of", [1, 2 + 128], I32)
        blocks_to = sb("blocks_to", [1, NE], I32)
        wraw = sb("wraw", [128, RAW, KT, 2, M])
        draw = sb("draw", [MH, RAW, 2, T])
        pk = sb("pk", [128, 2, WX], F16)
        W = pk[:, :, 0:WW].rearrange("p b (k a m) -> p b k a m", k=KT, a=2)
        D = pk[0:MH, :, WW:WX].rearrange("p b (c a n) -> p b c a n", c=2, a=2)
        sg = sb("sg", [128, 2, M])
        h = sb("h", [128, 2, M])
        hT = sb("hT", [MH, 2, 2, 2, 128], F16)
        acc = sb("acc", [128, B, T])
        acc1 = vM[:, :, :, :, :].rearrange("p a b c d -> p (a b c d)").rearrange("p (b t) -> p b t", b=B)
        bx = sb("bx", [128, WB, PAY])
        bid = sb("bid", [128, WB], U32)
        ident16 = sb("ident16", [128, 128], F16)
        bxT = sb("bxT", [128, 2, 2, KT, 128], F16)
        bsg = sb("bsg", [128, 2, M])
        bh = sb("bh", [128, 2, M])
        bhT = sb("bhT", [MH, 2, 2, 2, 128], F16)
        by = sb("by", [128, WB, T])
        tick = sb("tick", [128, 2])

        XS = nc.dram_tensor("rows_by_expert", (SPARE + 128, PAY), F32).ap()
        PACK = nc.dram_tensor("split_weights", (NE, 128, WX), F16).ap()
        SUM = [nc.dram_tensor(f"routed_sum{i}", (N + 128, T), F32).ap() for i in range(2)]

        ps = stack.enter_context(nc.psum_tensor("ps", [128, 8, 512], F32))

        def ring(job):
            s = slot(job)
            return ps[:, 2 * s:2 * s + 2, :].rearrange("p a b -> p (a b)")

        def od(par):
            return ps[:, 6 + par, :]

        filled = [sem(f"ring_filled{s}") for s in range(RING)]
        emptied = [sem(f"ring_emptied{s}") for s in range(RING)]
        consts_in = sem("consts_in")
        x_in = sem("x_in")
        ctx_in_s = sem("ctx_in_s")
        ctx_placed = sem("ctx_placed")
        memsets = sem("memsets")
        pool_setup = sem("pool_setup")
        pool_zeroed = sem("pool_zeroed")
        setup_done = sem("setup_done")
        wt_filled = sem("wt_filled")
        wt_ready = sem("wt_ready")
        proj0_filled = sem("proj0_filled")
        qkv0_ready = sem("qkv0_ready")
        qs0_filled = sem("qs0_filled")
        ks0_filled = sem("ks0_filled")
        stacks0_ready = sem("stacks0_ready")
        keys_kept = sem("keys_kept")
        tanh_done = sem("tanh_done")
        ln1 = sem("ln1")
        xn_ready = sem("xn_ready")
        split_hi = sem("split_hi")
        split_lo = sem("split_lo")
        v_masked = sem("v_masked")
        k_masked = sem("k_masked")
        q2_masked = sem("q2_masked")
        p_used = sem("p_used")
        o_step = sem("o_step")
        x1_step = sem("x1_step")
        rs_step = sem("rs_step")
        xT_ready = sem("xT_ready")
        xT_lo = sem("xT_lo")
        rt_step = sem("rt_step")
        w_in = [sem(f"w_in{i}") for i in range(RAW)]
        w_scaled = sem("w_scaled")
        w_hi = sem("w_hi")
        d_hi = sem("d_hi")
        w_lo = sem("w_lo")
        gu_done = sem("gu_done")
        silu_done = sem("silu_done")
        h_done = sem("h_done")
        hT_filled = sem("hT_filled")
        hT_hi = sem("hT_hi")
        hT_lo = sem("hT_lo")
        y_done = sem("y_done")
        acc_done = sem("acc_done")
        fin_done = sem("fin_done")
        dp_step = sem("dp_step")
        sent = [sem("sent0"), sem("sent1")]
        pads_sent = sem("pads_sent")
        more_pads_sent = sem("more_pads_sent")
        zeroed = sem("zeroed")
        rank7_filled = sem("rank7_filled")
        counts_filled = sem("counts_filled")
        tb_step = sem("tb_step")
        table_filled = sem("table_filled")
        table_ready = sem("table_ready")
        bx_in = [sem(f"bx_in{j}") for j in range(WB)]
        stored = sem("stored")
        experts_in = sem("experts_in")
        bhT_hi = sem("bhT_hi")
        bid_done = sem("bid_done")
        bxT_filled = sem("bxT_filled")
        bxT_done = sem("bxT_done")
        bgu_done = sem("bgu_done")
        bsilu_done = sem("bsilu_done")
        bh_done = sem("bh_done")
        bhT_filled = sem("bhT_filled")
        bhT_done = sem("bhT_done")
        by_filled = sem("by_filled")
        by_done = sem("by_done")
        added = [sem("added0"), sem("added1")]
        odd_sum_in = sem("odd_sum_in")
        even_sum_in = [sem("even_sum_in0"), sem("even_sum_in1")]
        tail_sum = sem("tail_sum")
        pay_step = sem("pay_step")
        send_tick = sem("send_tick")
        add_tick = sem("add_tick")
        rank7_read = sem("rank7_read")
        out_ready = sem("out_ready")
        out_done = sem("out_done")

        block = stack.enter_context(nc.Block())

        def wait_filled(eng, job, n):
            eng.wait_ge(filled[slot(job)], use(job, n) + 1)

        def wait_emptied(eng, job, n):
            eng.wait_ge(emptied[slot(job)], use(job, n) + 1)

        def link(eng, semaphore, base, count):
            done = [0]

            def step(instruction):
                done[0] += 1
                assert done[0] <= count
                instruction.then_inc(semaphore, 1)
                eng.wait_ge(semaphore, base + done[0])
            return step

        def periods(eng, period):
            period(0, 0)
            period(1, 1)
            period(2, 2)
            with eng.Fori(0, 2) as t:
                period(3, t * 2 + 3)
                period(4, t * 2 + 4)
            period(7, 7)
            period(8, 8)
            period(9, 9)

        def blocks(eng, step, begin=lambda b, count: None):
            def steps(start, b, count):
                given = begin(b, count)
                for u in range(count):
                    step(b + u, (start + u) % WB, u, given)

            first = 2 * WB - 1
            rounds = (NB - (WB - 1) - first) // WB
            steps(0, 0, first)
            with eng.Fori(0, rounds) as t:
                steps(first, t * WB + first, WB)
            steps(first, first + WB * rounds, NB + 2 - first - WB * rounds)

        def entries(engine, row, b, count, top):
            return nc.values_load_multi_w_load_instructions(
                row[0:1, bass.ds(b, count)], engines=[engine], min_val=0, max_val=top,
                skip_runtime_bounds_check_because="the tables' entries are bounded by how they are made")[1]

        def since(b, k):
            return not isinstance(b, int) or b >= k

        def until(b):
            return not isinstance(b, int) or b < NB

        def has(kind, job):
            if job[0] == "A" or job == "NMT":
                return kind < B
            if job[0] == "B":
                return 1 <= kind <= B
            if job in ("PROJ", "QS", "KS"):
                return kind < B - 1
            return kind >= (3 if job == "RK" else 2)

        @block.sync
        def _(sp):
            for i, w in enumerate((Wq, Wk, Wv, Wo)):
                sp.dma_start(wnat[:, i, :], w).then_inc(consts_in, 16)
            for i, v in enumerate((bq, bk, bv, bo)):
                sp.dma_start(bias[:, i:i + 1], v.rearrange("(p a) -> p a", a=1)).then_inc(consts_in, 16)
            sp.dma_start(ctxb[:, 0:B, :], ctx_in.rearrange("b p t -> p b t")).then_inc(ctx_in_s, 16)
            for i, v in enumerate((g_xattn, g_ffn)):
                sp.dma_start(gates[:, i:i + 1], v.partition_broadcast(128)).then_inc(consts_in, 16)
            sp.dma_start(wr[:, :, :], w_router.rearrange("(k p) e -> p k e", p=128)).then_inc(consts_in, 16)
            sp.dma_start(corr[:, :], corr_bias.partition_broadcast(128)).then_inc(consts_in, 16)

            def load_expert(par, gate, up, down):
                sp.dma_start(wraw[:, par, :, 0, :], gate.rearrange("(k p) m -> p k m", p=128)).then_inc(w_in[par], 16)
                sp.dma_start(wraw[:, par, :, 1, :], up.rearrange("(k p) m -> p k m", p=128)).then_inc(w_in[par], 16)
                sp.dma_start(draw[:, par, :, :], down.rearrange("(c p) n -> p c n", p=MH)).then_inc(w_in[par], 16)

            for e in range(RAW):
                load_expert(e, gate_w[e], up_w[e], down_w[e])
            sp.wait_ge(acc_done, B)
            for total in SUM:
                sp.dma_start(total[0:N].rearrange("(b p) t -> p b t", p=128), acc[:, :, :]).then_inc(zeroed, 16)
            sp.dma_start(SUM[1][N:N + 128], acc[:, 0, :]).then_inc(zeroed, 16)

            def period(kind, n):
                if kind >= B:
                    return
                for i in range(4):
                    r = n * 4 + i
                    sp.wait_ge(w_lo, r * 2 + 2)
                    if kind < B - 1:
                        load_expert(i, gate_w[r + RAW], up_w[r + RAW], down_w[r + RAW])
                    elif i < 2:
                        half = slice(i * M, (i + 1) * M)
                        load_expert(i, sh_gate_w[:, half], sh_up_w[:, half], sh_down_w[half, :])
                    if kind > 0 or i > 0:
                        sp.wait_ge(stored, r * 16)
                    sp.dma_start(PACK[r], pk[:, i % 2, :]).then_inc(stored, 16)

            periods(sp, period)
            sp.wait_ge(stored, 16 * NE)
            sp.wait_ge(p_used, 8 * B)

            def fetch_expert(e, u):
                sp.dma_start(ring_w[:, WX * u:WX * u + WX], PACK[e]).then_inc(experts_in, 16)

            for e in range(WR):
                if e >= 1:
                    sp.wait_ge(experts_in, 16 * e)
                fetch_expert(e, e)
            sp.wait_ge(table_ready, 1)
            with sp.Fori(0, NE // WR - 1) as t:
                for u in range(WR):
                    last_block = sp.value_load(blocks_to[0:1, bass.ds(t * WR + u, 1)], min_val=1, max_val=NB + 1)
                    sp.wait_ge(experts_in, t * (16 * WR) + 16 * (u + WR))
                    sp.wait_ge(by_filled, last_block)
                    fetch_expert(t * WR + (WR + u), u)
            half = B // 2
            sp.wait_ge(added[1], 16 * (NB // 2))
            sp.dma_start(acc1[:, :, :], SUM[1][0:N].rearrange("(b p) t -> p b t", p=128)).then_inc(odd_sum_in, 16)
            sp.wait_ge(added[0], 16 * ((NB + 1) // 2))
            for i in range(2):
                sp.dma_start(acc[:, half * i:half * i + half, :],
                             SUM[0][128 * half * i:128 * half * (i + 1)].rearrange("(b p) t -> p b t", p=128))\
                  .then_inc(even_sum_in[i], 16)
            for b in range(0, B, 2):
                sp.wait_ge(out_ready, b + 2)
                sp.dma_start(out[b:b + 2].rearrange("b p t -> p b t"), xs[:, b:b + 2, :]).then_inc(out_done, 16)
            sp.wait_ge(out_done, 16 * (B // 2))

        @block.gpsimd
        def _(pool):
            pool.sem_inc(send_tick, 1)
            pool.wait_ge(memsets, 1)
            nc.gpsimd.affine_select(out=ident[:, :], in_=zeros[:, :], compare_op=ALU.not_equal, fill=1.0, base=0,
                                    pattern=[[-1, 128]], channel_multiplier=1).then_inc(pool_setup, 1)
            nc.gpsimd.affine_select(out=ob[:, 0:NG], in_=zeros[:, 0:NG], compare_op=ALU.not_equal, fill=1.0,
                                    base=-ROW, pattern=[[-32, NG]], channel_multiplier=1).then_inc(pool_setup, 1)
            nc.gpsimd.affine_select(out=tri[:, :], in_=zeros[:, :], compare_op=ALU.is_ge, fill=1.0, base=0,
                                    pattern=[[-1, 128]], channel_multiplier=1).then_inc(pool_setup, 1)
            nc.gpsimd.iota(counting[:, 0:NE + 1], pattern=[[CAP, NE + 1]], base=1, channel_multiplier=0)\
                .then_inc(pool_setup, 1)
            nc.gpsimd.iota(counting[:, NE + 1:2 * NE + 2], pattern=[[CAP, NE + 1]], base=0, channel_multiplier=1)\
                .then_inc(pool_setup, 1)
            nc.gpsimd.iota(counting[:, 2 * NE + 2:2 * NE + 3 + B], pattern=[[128, B + 1]], base=0, channel_multiplier=1)\
                .then_inc(pool_setup, 1)
            nc.gpsimd.iota(counting[:, 2 * NE + 3 + B:], pattern=[[0, NE], [128, 8]], base=0, channel_multiplier=0)\
                .then_inc(pool_setup, 1)
            nc.gpsimd.memset(kM[:, :, :, :, :], 0.0).then_inc(pool_zeroed, 1)

            def split_low(p):
                pool.wait_ge(split_hi, p + 1)
                nc.gpsimd.tensor_tensor(qkl[:, :, :], qk32[:, :, :], qkh[:, :, :], ALU.subtract).then_inc(split_lo, 1)

            def mask_v(par):
                for s in range(KT):
                    for J in range(NJ):
                        cols = slice(KC * J, KC * J + KC)
                        nc.gpsimd.tensor_tensor(
                            vM[:, par, s, J, :].rearrange("p (g c) -> p g c", c=32)[:, :, cols],
                            v32[:, s, :].rearrange("p (g c) -> p g c", c=32)[:, :, cols],
                            zeros[:, :].rearrange("p (g c) -> p g c", c=32)[:, :, cols], ALU.add).then_inc(v_masked, 1)

            def place_ctx(b):
                nc.gpsimd.tensor_tensor(ctxv[:, 0:128], ctxb[:, b, 0:128], zeros[:, :], ALU.add).then_inc(ctx_placed, 1)
                nc.gpsimd.tensor_tensor(ctxv[:, 128:T], ctxb[:, b, 128:T], zeros[:, :], ALU.add).then_inc(ctx_placed, 1)

            pool.wait_ge(ctx_in_s, 16)
            place_ctx(0)
            for tile in (vM[:, :, :, :, :], q2M[:, :, :, :, :]):
                nc.gpsimd.memset(tile, 0.0).then_inc(pool_zeroed, 1)
            pool.wait_ge(setup_done, 2)
            pool.wait_ge(pool_zeroed, 3)
            nc.gpsimd.dma_start(XS[SPARE:SPARE + 128], filling[:, :]).then_inc(sent[0], 16)
            nc.gpsimd.dma_start(SUM[0][N:N + 128, 0:T], filling[:, 0:T]).then_inc(sent[1], 16)
            pool.wait_ge(qkv0_ready, 3)
            split_low(0)
            mask_v(0)

            pool.wait_ge(proj0_filled, 1)
            place_ctx(1)

            def low_weights(r, i):
                par = i % 2
                pool.wait_ge(w_hi, r + 1)
                pool.wait_ge(d_hi, r + 1)
                nc.gpsimd.tensor_tensor(W[:, par, :, 1, :], wraw[:, i, :, :, :].rearrange("p k a m -> p k (a m)"),
                                        W[:, par, :, 0, :], ALU.subtract).then_inc(w_lo, 1)
                nc.gpsimd.tensor_tensor(D[:, par, :, 1, :], draw[:, i, :, :], D[:, par, :, 0, :], ALU.subtract)\
                    .then_inc(w_lo, 1)

            def fill_row(n, par):
                c = n - 2
                if not isinstance(n, int) or n > 3:
                    pool.wait_ge(sent[par], (c - par) * (8 * TOPK) + 16)
                pool.wait_ge(rs_step, (RSQRT_STEPS + 1) * (c + 1))
                no = zeros[:, :].unsqueeze(1).to_broadcast([128, KT, 128])
                high, low = (pay16[par][:, T * i:T * i + T].rearrange("p (k t) -> p k t", k=KT) for i in range(2))
                x = xn2[:, :].rearrange("p (k t) -> p k t", k=KT)
                nc.gpsimd.tensor_tensor(high, x, no, ALU.add).then_inc(pay_step, 1)
                nc.gpsimd.tensor_tensor(pay[:, par, T:T + 1], number[:, bass.ds(c, 1)], zeros[:, 0:1], ALU.add)\
                    .then_inc(pay_step, 1)
                pool.wait_ge(pay_step, 3 * c + 2)
                nc.gpsimd.tensor_tensor(low, x, high, ALU.subtract).then_inc(pay_step, 1)

            def send(c, par, ks=range(TOPK)):
                if ks[0] == 0:
                    pool.wait_ge(dp_step, DISPATCH_STEPS * (c + 1) + 1)
                    pool.wait_ge(pay_step, 3 * (c + 1))
                    pool.wait_ge(send_tick, c + 1)
                    nc.gpsimd.tensor_tensor(tick[:, 0:1], zeros[:, 0:1], zeros[:, 0:1], ALU.add).then_inc(send_tick, 1)
                for k in ks:
                    nc.gpsimd.indirect_dma_start(XS, bass.IndirectOffsetOnAxis(ap=place[:, par, k:k + 1], axis=0),
                                                 pay[:, par, :], None).then_inc(sent[par], 16)

            def period(kind, n):
                par = kind % 2
                for job in POOL_TURNS:
                    if job == "context" and has(kind, "PROJ"):
                        wait_filled(pool, "PROJ", n)
                        place_ctx(n + 2)
                    elif job[0:7] == "weights":
                        i = int(job[7])
                        if kind < B or kind == B and i < 2:
                            low_weights(n * 4 + i, i)
                    elif job == "split" and has(kind, "PROJ"):
                        split_low(n + 1)
                    elif job == "xT" and has(kind, "XT"):
                        c = n - 2
                        wait_emptied(pool, "XT", n)
                        nc.gpsimd.tensor_tensor(xT[:, c, :, 1, :], xT32[:, :, :], xT[:, c, :, 0, :], ALU.subtract)\
                            .then_inc(xT_lo, 1)
                    elif job == "values" and 1 <= kind < B:
                        wait_emptied(pool, "PROJ", n - 1)
                        if kind > 1:
                            pool.wait_ge(p_used, 8 * (n - 1))
                        mask_v(par)
                    elif job == "row" and has(kind, "WO"):
                        fill_row(n, par)
                    elif job[0:4] == "send" and has(kind, "RK"):
                        k = 2 * int(job[4])
                        send(n - 3, 1 - par, range(k, k + 2))

            periods(pool, period)
            send(B - 1, (B - 1) % 2)
            pool.wait_ge(tb_step, 1)
            for e in range(POOL_PADS):
                nc.gpsimd.indirect_dma_start(XS, bass.IndirectOffsetOnAxis(ap=pad_place[:, e:e + 1], axis=0),
                                             filling[:, :], None).then_inc(pads_sent, 16)

            def add_block(b, j, u, given):
                if not until(b):
                    return
                buf = j % 2
                pool.wait_ge(by_done, b + 1)
                pool.wait_ge(bid_done, b + 1)
                if since(b, 2):
                    pool.wait_ge(added[buf], (b - buf) * 8)
                pool.wait_ge(add_tick, b)
                nc.gpsimd.tensor_tensor(tick[:, 1:2], zeros[:, 0:1], zeros[:, 0:1], ALU.add).then_inc(add_tick, 1)
                nc.gpsimd.indirect_dma_start(SUM[buf], bass.IndirectOffsetOnAxis(ap=bid[:, j:j + 1], axis=0),
                                             by[:, j, :], None, compute_op=ALU.add).then_inc(added[buf], 16)

            pool.wait_ge(zeroed, 16 * 3)
            pool.wait_ge(sent[1], 16)
            blocks(pool, add_block)

        @block.scalar
        def _(act):
            act.dma_start(xs[:, :, :], x.rearrange("b p t -> p b t")).then_inc(x_in, 16)
            act.wait_ge(consts_in, 16 * 12)
            act.activation(tg[:, :], gates[:, :], ACT.Tanh).then_inc(tanh_done, 1)
            act.wait_ge(wt_filled, 1)
            act.activation(wT[:, :, :], ring("A0")[:, 0:512].rearrange("p (a b) -> p a b", a=4), ACT.Copy)\
               .then_inc(wt_ready, 1)
            def evacuate_qkv(src, semaphore, each):
                for i in range(2):
                    ins = act.activation(qk32[:, i, :], src[:, i * T:(i + 1) * T], ACT.Identity, bias=bias[:, i:i + 1])
                    if each:
                        ins.then_inc(semaphore, 1)
                act.activation(v32[:, :, :], src[:, 512:768].rearrange("p (a b) -> p a b", a=KT), ACT.Copy)\
                   .then_inc(semaphore, 1)

            def stack_q(src, par, semaphore):
                act.activation(qS[:, par, :, :], src.rearrange("p (j t) -> p j t", j=NJ), ACT.Copy).then_inc(semaphore, 1)

            def stack_k(src, par, semaphore):
                act.activation(kS[:, par, :, :], src.rearrange("p (j t) -> p j t", j=NJ), ACT.Identity,
                               bias=onesrow[:, 0:1]).then_inc(semaphore, 1)

            def mask_k(par):
                for g in range(NG):
                    rows = slice(32 * g, 32 * g + 32)
                    act.activation(kM[rows, par, :, g, :], kS[rows, par, :, :], ACT.Copy).then_inc(k_masked, 1)

            def exps(u, b, n, kind):
                wait_filled(act, f"B{u}", n)
                if not (kind == 1 and u < NP):
                    act.wait_ge(p_used, 8 * b + u - NP + 1)
                act.activation(Pb[:, u % NP, :, :], ring(f"B{u}").rearrange("p (g t) -> p g t", g=NG), ACT.Exp,
                               scale=SCALE).then_inc(emptied[slot(f"B{u}")], 1)

            act.wait_ge(proj0_filled, 1)
            evacuate_qkv(ring("A1"), qkv0_ready, True)
            act.wait_ge(qs0_filled, 1)
            act.wait_ge(setup_done, 2)
            stack_q(ring("B0"), 0, stacks0_ready)
            act.wait_ge(ks0_filled, 1)
            stack_k(ring("A0"), 0, stacks0_ready)
            act.wait_ge(stacks0_ready, 2)
            act.wait_ge(pool_zeroed, 1)
            mask_k(0)

            def scale_weights(r, i, kind):
                act.wait_ge(w_in[i], (r - i) * (48 // RAW) + 48)
                act.activation(wraw[:, i, :, :, :], wraw[:, i, :, :, :], ACT.Copy, scale=WS).then_inc(w_scaled, 1)
                act.activation(draw[:, i, :, :], draw[:, i, :, :], ACT.Copy, scale=WS).then_inc(w_scaled, 1)
                if kind > 0 or i > 1:
                    act.wait_ge(stored, (r - 1) * 16)
                act.wait_ge(w_scaled, r * 2 + 2)
                act.activation(D[:, i % 2, :, 0, :], draw[:, i, :, :], ACT.Copy).then_inc(d_hi, 1)

            def period(kind, n):
                par = kind % 2
                c = n - 2
                for job in TURNS:
                    if job in PACK_AT[:4 if kind < B else 2 if kind == B else 0]:
                        i = PACK_AT.index(job)
                        scale_weights(n * 4 + i, i, kind)
                    if not has(kind, job):
                        continue
                    if job[0] == "B":
                        exps(int(job[1]), n - 1, n, kind)
                    elif job == "PROJ":
                        wait_filled(act, job, n)
                        act.wait_ge(v_masked, 8 * (n + 1))
                        act.wait_ge(split_lo, n + 1)
                        evacuate_qkv(ring(job), emptied[slot(job)], False)
                    elif job == "XT":
                        wait_filled(act, job, n)
                        if kind > 2:
                            act.wait_ge(xT_lo, c)
                            wait_filled(act, "LG", n - 1)
                        act.activation(xT32[:, :, :], ring(job)[:, 0:256].rearrange("p (k t) -> p k t", k=KT), ACT.Copy)\
                           .then_inc(xT_ready, 1)
                        act.activation(xT[:, c, :, 0, :], ring(job)[:, 0:256].rearrange("p (k t) -> p k t", k=KT),
                                       ACT.Copy).then_inc(emptied[slot(job)], 1)
                    elif job == "QS":
                        wait_filled(act, job, n)
                        if kind >= 1:
                            wait_emptied(act, "NMT", n - 1)
                        stack_q(ring(job), 1 - par, emptied[slot(job)])
                    elif job == "KS":
                        wait_filled(act, job, n)
                        if kind >= 1:
                            act.wait_ge(keys_kept, n)
                        stack_k(ring(job), 1 - par, emptied[slot(job)])
                        wait_emptied(act, job, n)
                        if kind >= 1:
                            wait_filled(act, "A7", n - 1)
                        mask_k(1 - par)
                    elif job == "LG":
                        wait_filled(act, job, n)
                        act.wait_ge(rt_step, ROUTE_STEPS * c)
                        act.activation(el[:, :], ring(job)[:, 0:NE], ACT.Exp, scale=-1.0).then_inc(emptied[slot(job)], 1)

            periods(act, period)

            def high(i, buf, fresh=False):
                act.wait_ge(hT_filled, i + 1)
                if not fresh:
                    act.wait_ge(y_done, i - 1)
                act.activation(hT[:, buf, 0, :, :], ps[0:MH, 2 + buf, 0:256].rearrange("p (c t) -> p c t", c=2),
                               ACT.Copy).then_inc(hT_hi, 1)

            for i in range(2 * B):
                buf = i % 2
                act.wait_ge(gu_done, i + 1)
                if i >= 2:
                    act.wait_ge(h_done, i - 1)
                act.activation(sg[:, buf, :], ps[:, buf, 0:M], ACT.Silu, scale=1.0 / WS).then_inc(silu_done, 1)
                if i >= 1:
                    high(i - 1, 1 - buf, i < 3)
                if i == PADS_AT:
                    act.wait_ge(tb_step, 1)
                if i >= PADS_AT:
                    e = POOL_PADS + i - PADS_AT
                    row, = entries(mybir.EngineType.Activation, pad_place, e, 1, SPARE)
                    act.dma_start(XS[bass.ds(row, 128)], filling[:, :]).then_inc(more_pads_sent, 16)
            high(2 * B - 1, 1)

            def fetch(b, j, row):
                if since(b, WB):
                    act.wait_ge(bid_done, b - WB + 1)
                act.dma_start(bx[:, j, :], XS[bass.ds(row, 128)]).then_inc(bx_in[j], 16)

            def keep_xT(b, buf):
                if not until(b):
                    return
                loads = act.value_load(loads_of[0:1, bass.ds(b, 1)], min_val=16, max_val=16 * NE)
                act.wait_ge(experts_in, loads)
                act.wait_ge(bxT_filled, b + 1)
                if since(b, 2):
                    act.wait_ge(bgu_done, b - 1)
                act.activation(bxT[:, buf, :, :, :],
                               ps[:, 6 + buf, :].bitcast(F16)[:, 0:512].rearrange("p (a k t) -> p a k t", a=2, k=KT),
                               ACT.Copy).then_inc(bxT_done, 1)

            def begin(b, count):
                return entries(mybir.EngineType.Activation, row_of, b + WB - 1, count, SPARE)

            def step(b, j, u, rows):
                buf = j % 2
                keep_xT(b + 1, 1 - buf)
                if until(b):
                    act.wait_ge(bgu_done, b + 1)
                    if isinstance(b, int) and b >= 2:
                        act.wait_ge(bh_done, b - 1)
                    act.activation(bsg[:, buf, :], ps[:, buf, 0:M], ACT.Silu, scale=1.0 / WS).then_inc(bsilu_done, 1)
                if until(b + WB - 1):
                    fetch(b + WB - 1, (j + WB - 1) % WB, rows[u])
                if since(b, 1) and until(b - 1):
                    act.wait_ge(bhT_filled, b)
                    if since(b, 3):
                        act.wait_ge(by_filled, b - 1)
                    act.activation(bhT[:, 1 - buf, 0, :, :], ps[0:MH, 3 - buf, 0:256].rearrange("p (c t) -> p c t", c=2),
                                   ACT.Copy).then_inc(bhT_hi, 1)

            for par in range(2):
                act.wait_ge(sent[par], 16 * TOPK * B // 2 + 16)
            act.wait_ge(pads_sent, 16 * POOL_PADS)
            act.wait_ge(more_pads_sent, 16 * (NE - POOL_PADS))
            act.wait_ge(table_ready, 1)
            first_rows = entries(mybir.EngineType.Activation, row_of, 0, WB - 1, SPARE)
            for b in range(WB - 1):
                fetch(b, b, first_rows[b])
            keep_xT(0, 0)
            blocks(act, step, begin)

        @block.tensor
        def _(pe):
            def take(job, n, first=False):
                before = use(job, n)
                if not (isinstance(before, int) and before == 0):
                    pe.wait_ge(emptied[slot(job)], before)

            pe.wait_ge(consts_in, 16 * 12)
            pe.wait_ge(pool_setup, 1)
            for i in range(4):
                last = pe.transpose(ring("A0")[:, 128 * i:128 * i + 128], wnat[:, i, :], ident[:, :])
            last.then_inc(wt_filled, 1)

            def project(dst, par, b, semaphore):
                pe.matmul(dst[:, 0:T], wT[:, 0, :], xnb[:, par, :], start=True, stop=True)
                pe.matmul(dst[:, T:2 * T], wT[:, 1, :], ctxb[:, b, :], start=True, stop=True)
                for s in range(KT):
                    last = pe.matmul(dst[:, 512 + 128 * s:640 + 128 * s], ctxv[:, 128 * s:128 * s + 128], wT[:, 2, :],
                                     start=True, stop=True)
                last.then_inc(semaphore, 1)

            def stack_rows(dst, side, semaphore):
                for J in range(NJ):
                    cols = slice(T * J, T * J + T)
                    pe.matmul(dst[:, cols], pick[:, 2 * side, J, :, :, :].rearrange("p g r c -> p (g r c)"),
                              qkh[:, side, :], start=True, stop=False)
                    last = pe.matmul(dst[:, cols], pick[:, 2 * side + 1, J, :, :, :].rearrange("p g r c -> p (g r c)"),
                                     qkl[:, side, :], start=False, stop=True)
                last.then_inc(semaphore, 1)

            pe.wait_ge(wt_ready, 1)
            pe.wait_ge(xn_ready, 1)
            pe.wait_ge(ctx_in_s, 16)
            pe.wait_ge(ctx_placed, 2)
            project(ring("A1"), 0, 0, proj0_filled)
            pe.wait_ge(split_lo, 1)
            pe.wait_ge(setup_done, 2)
            stack_rows(ring("B0"), 0, qs0_filled)
            stack_rows(ring("A0"), 1, ks0_filled)
            pe.wait_ge(stacks0_ready, 2)

            def scores_max(u, n, par):
                tc, J = divmod(u, NJ)
                if u == 0:
                    pe.wait_ge(k_masked, 4 * (n + 1))
                for half in range(2):
                    last = pe.matmul(ring(f"A{u}")[:, 512 * half:512 * half + 512],
                                     qS[:, par, J, 128 * tc:128 * tc + 128],
                                     kM[:, par, J, 2 * half:2 * half + 2, :].rearrange("p g s -> p (g s)"),
                                     start=True, stop=True)
                last.then_inc(filled[slot(f"A{u}")], 1)

            def scores_exp(u, n, par):
                sc, J = divmod(u, NJ)
                if u == 0:
                    pe.wait_ge(q2_masked, 4 * n)
                    pe.wait_ge(keys_kept, n)
                for half in range(2):
                    last = pe.matmul(ring(f"B{u}")[:, 512 * half:512 * half + 512],
                                     kB[:, J, 128 * sc:128 * sc + 128],
                                     q2M[:, par, J, 2 * half:2 * half + 2, :].rearrange("p g t -> p (g t)"),
                                     start=True, stop=True)
                last.then_inc(filled[slot(f"B{u}")], 1)

            def weigh(u, n, kind, par):
                b = n - 1
                sc, J = divmod(u, NJ)
                wait_emptied(pe, f"B{u}", n)
                if u == 0:
                    pe.wait_ge(v_masked, 8 * n)
                    if kind > 2:
                        pe.wait_ge(o_step, 3 * (b - 1))
                for g in range(NG):
                    rows = slice(32 * g, 32 * g + 32)
                    pe.matmul(od(par)[rows, 0:T], vM[:, par, sc, J, rows], Pb[:, u % NP, g, :],
                              start=(u == 0), stop=(u == 7), skip_group_check=True, tile_position=(0, 32 * g))
                    last = pe.matmul(od(par)[rows, T:2 * T], onesM[:, J, rows], Pb[:, u % NP, g, :],
                                     start=False, stop=(u == 7), skip_group_check=True, tile_position=(0, 32 * g))
                last.then_inc(p_used, 1)

            def rank(c, dst, semaphore):
                pe.wait_ge(rt_step, ROUTE_STEPS * (c + 1))
                pe.matmul(dst[:, 0:NE], tri16[:, :], em16[:, :], start=True, stop=False)
                pe.wait_ge(dp_step, DISPATCH_STEPS * c + 1)
                pe.matmul(dst[:, 0:NE], ones16[:, :], emsum[:, :], start=False, stop=True).then_inc(semaphore, 1)

            def period(kind, n):
                par = kind % 2
                for job in TURNS:
                    take(job, n)
                    s = slot(job)
                    if not has(kind, job):
                        pe.sem_inc(filled[s], 1)
                        pe.sem_inc(emptied[s], 1)
                        continue
                    if job[0] == "A":
                        scores_max(int(job[1]), n, par)
                    elif job[0] == "B":
                        u = int(job[1])
                        scores_exp(u, n, 1 - par)
                        if u > 0:
                            weigh(u - 1, n, kind, 1 - par)
                    elif job == "WO":
                        pe.wait_ge(o_step, 3 * (n - 1))
                        pe.matmul(ring(job)[:, 0:T], wT[:, 3, :], ob[:, :], start=True, stop=True).then_inc(filled[s], 1)
                    elif job == "PROJ":
                        pe.wait_ge(xn_ready, n + 2)
                        pe.wait_ge(ctx_placed, 2 * n + 4)
                        project(ring(job), 1 - par, n + 1, filled[s])
                    elif job == "XT":
                        pe.wait_ge(rs_step, (RSQRT_STEPS + 1) * (n - 1))
                        for k in range(KT):
                            last = pe.transpose(ring(job)[:, 128 * k:128 * k + 128],
                                                xn2[:, 128 * k:128 * k + 128], ident[:, :])
                        last.then_inc(filled[s], 1)
                    elif job in ("QS", "KS"):
                        pe.wait_ge(split_lo, n + 2)
                        stack_rows(ring(job), int(job == "KS"), filled[s])
                    elif job == "RK":
                        rank(n - 3, ring(job), filled[s])
                    elif job == "LG":
                        pe.wait_ge(xT_ready, n - 1)
                        for k in range(KT):
                            last = pe.matmul(ring(job)[:, 0:NE], xT32[:, k, :], wr[:, k, :], start=(k == 0),
                                             stop=(k == KT - 1))
                        last.then_inc(filled[s], 1)
                    elif job == "NMT":
                        wait_emptied(pe, "A7", n)
                        for tc in range(KT):
                            for J in range(NJ):
                                last = pe.transpose(ring(job)[:, T * J + 128 * tc:T * J + 128 * tc + 128],
                                                    nmx[:, tc, J, :, :].rearrange("p g c -> p (g c)"), ident[:, :])
                        last.then_inc(filled[s], 1)
                if has(kind, "B7"):
                    weigh(7, n, kind, 1 - par)

            periods(pe, period)

            def gate_up(i, k, par, fresh):
                buf = k % 2
                if not fresh:
                    pe.wait_ge(h_done, i - 1)
                n = 0
                for kt in range(KT):
                    for a, w in ((0, 0), (0, 1), (1, 0)):
                        last = pe.matmul(ps[:, buf, 0:2 * M], xT[:, k, kt, a, :], W[:, par, kt, w, :],
                                         start=(n == 0), stop=(n == 5))
                        n += 1
                last.then_inc(gu_done, 1)

            def turn(i, buf, fresh):
                pe.wait_ge(h_done, i + 1)
                if not fresh:
                    pe.wait_ge(hT_lo, i - 1)
                for c in range(2):
                    last = pe.transpose(ps[0:MH, 2 + buf, 128 * c:128 * c + 128], h[:, buf, MH * c:MH * c + MH],
                                        ident[:, :])
                last.then_inc(hT_filled, 1)

            def down(i, buf, par, fresh):
                pe.wait_ge(hT_lo, i + 1)
                if not fresh:
                    pe.wait_ge(acc_done, i - 1 + B)
                n = 0
                for c in range(2):
                    for a, w in ((0, 0), (0, 1), (1, 0)):
                        last = pe.matmul(ps[:, 4 + buf, 0:T], hT[:, buf, a, c, :], D[:, par, c, w, :],
                                         start=(n == 0), stop=(n == 5))
                        n += 1
                last.then_inc(y_done, 1)

            pe.wait_ge(xT_lo, B)
            for job in ("WO", "XT", "LG"):
                wait_emptied(pe, job, B + 1)
            for i in range(2 * B + 2):
                if i < 2 * B:
                    pe.wait_ge(w_lo, 2 * (NE + i // B + 1))
                    gate_up(i, i % B, i // B, i < 2)
                if 1 <= i <= 2 * B:
                    turn(i - 1, (i - 1) % 2, i < 3)
                if i >= 2:
                    down(i - 2, i % 2, (i - 2) // B, i < 4)
                if i == RANK_AT:
                    pe.wait_ge(o_step, 3 * B)
                    rank(B - 1, od(0), rank7_filled)
                if i == COUNT_AT:
                    pe.wait_ge(dp_step, DISPATCH_STEPS * B + 1)
                    pe.matmul(od(1)[:, 0:NE], ones16[:, :], emsum[:, :], start=True, stop=True)\
                      .then_inc(counts_filled, 1)
                if i == TABLE_AT:
                    pe.wait_ge(tb_step, TABLE_STEPS)
                    for k in range(3):
                        last = pe.matmul(od(0)[0:1, 128 * k:128 * k + 128], cols[:, 6 + k:7 + k],
                                         ident[:, :], start=True, stop=True)
                    last.then_inc(table_filled, 1)

            def turn_x(b, j):
                if not until(b):
                    return
                buf = j % 2
                pe.wait_ge(bx_in[j], (b - j) * 4 + 16)
                for k in range(2 * KT):
                    part = slice(128 * k, 128 * k + 128)
                    last = pe.transpose(ps[:, 6 + buf, :].bitcast(F16)[:, part], bx[:, j, 0:T].bitcast(F16)[:, part],
                                        ident16[:, :])
                last.then_inc(bxT_filled, 1)

            def begin(b, count):
                return entries(mybir.EngineType.PE, place_of, b, count + 2, (WR - 1) * WX)

            def step(b, j, u, places):
                buf = j % 2
                place_2, place_0 = places[u], places[u + 2]
                turn_x(b + 1, (j + 1) % WB)
                if until(b):
                    pe.wait_ge(bxT_done, b + 1)
                    n = 0
                    for k in range(KT):
                        for a, w in ((0, 0), (0, 1), (1, 0)):
                            last = pe.matmul(ps[:, buf, 0:2 * M], bxT[:, buf, a, k, :],
                                             ring_w[:, bass.ds(place_0 + (2 * k + w) * 2 * M, 2 * M)],
                                             start=(n == 0), stop=(n == 5))
                            n += 1
                    last.then_inc(bgu_done, 1)
                if since(b, 1) and until(b - 1):
                    pe.wait_ge(bh_done, b)
                    for c in range(2):
                        last = pe.transpose(ps[0:MH, 3 - buf, 128 * c:128 * c + 128],
                                            bh[:, 1 - buf, MH * c:MH * c + MH], ident[:, :])
                    last.then_inc(bhT_filled, 1)
                if since(b, 2) and until(b - 2):
                    pe.wait_ge(bhT_done, b - 1)
                    n = 0
                    for c in range(2):
                        for a, w in ((0, 0), (0, 1), (1, 0)):
                            last = pe.matmul(ps[:, 4 + buf, 0:T], bhT[:, buf, a, c, :],
                                             ring_w[0:MH, bass.ds(place_2 + (WW + (2 * c + w) * T), T)],
                                             start=(n == 0), stop=(n == 5))
                            n += 1
                    last.then_inc(by_filled, 1)

            pe.wait_ge(acc_done, 3 * B)
            pe.wait_ge(table_ready, 1)
            pe.sem_inc(by_filled, 1)
            turn_x(0, 0)
            blocks(pe, step, begin)

        @block.vector
        def _(dve):
            dve.memset(zeros[:, :], 0.0).then_inc(memsets, 1)
            for tile in (nmx[:, :, :, :, :], pick[:, :, :, :, :, :], onesM[:, :, :]):
                dve.memset(tile, 0.0).then_inc(memsets, 1)
            dve.memset(filling[:, :], 0.0).then_inc(memsets, 1)
            dve.memset(ctxb[:, B, :], 0.0).then_inc(memsets, 1)
            dve.memset(ones[:, :], 1.0).then_inc(memsets, 1)
            dve.memset(ones16[:, :], 1.0).then_inc(memsets, 1)
            dve.memset(pk[64:128, :, WW:WX], 0.0).then_inc(memsets, 1)
            dve.memset(delta[:, :, :], 0.0).then_inc(memsets, 1)
            dve.memset(place_of[:, 0:2], 0).then_inc(memsets, 1)
            dve.wait_ge(memsets, 11)
            dve.memset(delta[:, 0, 0:NE - 1], float(WX)).then_inc(memsets, 1)
            by_slot = delta[:, 0, :].rearrange("p (a b) -> p a b", b=WR)
            dve.wait_ge(memsets, 12)
            dve.memset(by_slot[:, 0:NE // WR - 1, WR - 1], -float(WX * (WR - 1))).then_inc(memsets, 1)
            dve.memset(delta[:, 1, 0:NE - 1], 1.0).then_inc(memsets, 1)
            dve.memset(emsum[:, :], 0.0).then_inc(dp_step, 1)
            dve.wait_ge(memsets, 14)
            for J in range(NJ):
                dve.memset(onesM[:, J, :].rearrange("p (g c) -> p g c", c=32)[:, :, KC * J:KC * J + KC], 1.0)
            dve.wait_ge(pool_setup, 7)
            dve.tensor_copy(tri16[:, :], tri[:, :])
            dve.tensor_copy(ident16[:, :], ident[:, :])
            dve.tensor_copy(counts[:, :], counting[:, :]).then_inc(setup_done, 1)
            dve.wait_ge(setup_done, 1)
            dve.tensor_copy(filling[:, T:T + 1], number[:, B:B + 1])
            dve.memset(full[:, :, 0], -1.0)
            by_group = ident[:, :].rearrange("p (g j c) -> p j g c", g=NG, j=NJ)
            for which, rows in enumerate(((0, 1), (2,), (0, 2), (1,))):
                for r in rows:
                    for J in range(NJ):
                        dve.tensor_copy(pick[:, which, J, :, r, :], by_group[:, J, :, :])
            dve.tensor_reduce(onesrow[:, :], ob[:, 0:NG], AXX, ALU.max).then_inc(setup_done, 1)
            dve.wait_ge(setup_done, 2)
            dve.wait_ge(x_in, 16)
            for b in range(B):
                dve.bn_stats(st[:, b, :], xs[:, b, :]).then_inc(ln1, 1)
            dve.wait_ge(ln1, B)
            for b in range(B):
                dve.bn_aggr(mv[:, b, :], st[:, b, :]).then_inc(ln1, 1)
            dve.wait_ge(ln1, 2 * B)
            def inverse_root(step, v, w):
                bits = [a.bitcast(I32) for a in w]
                step(dve.tensor_scalar(bits[1], v.bitcast(I32), 1, None, ALU.logical_shift_right))
                step(dve.tensor_scalar(bits[0], bits[1], -1.0, 1597463007.0, ALU.mult, ALU.add))
                c = 1.0
                for _ in range(3):
                    step(dve.tensor_tensor(w[1], w[0], w[0], ALU.mult))
                    step(dve.tensor_tensor(w[1], w[1], v, ALU.mult))
                    step(dve.scalar_tensor_tensor(out=w[0], in0=w[1], scalar=-3.0 * c * c, in1=w[0], op0=ALU.add,
                                                  op1=ALU.mult))
                    c = -2.0 * c * c * c
                assert c == RSQRT_C

            step = link(dve, ln1, 2 * B, 2 + RSQRT_STEPS)
            step(dve.tensor_scalar(ve[:, :], mv[:, :, 1], EPS, None, ALU.add))
            inverse_root(step, ve[:, :], (r0[:, :], r1[:, :]))
            step(dve.tensor_scalar(rstd[:, :, 0], r0[:, :], 1.0 / RSQRT_C, None, ALU.mult))

            def norm_x(b, par):
                dve.tensor_scalar(xnb[:, par, :], xs[:, b, :], mv[:, b, 0:1], rstd[:, b, 0:1], ALU.subtract, ALU.mult)\
                   .then_inc(xn_ready, 1)

            def split(p):
                dve.tensor_copy(qkh[:, :, :], qk32[:, :, :]).then_inc(split_hi, 1)

            norm_x(0, 0)
            for k in range(B):
                dve.memset(acc[:, k, :], 0.0).then_inc(acc_done, 1)
            dve.wait_ge(pool_zeroed, 3)
            dve.wait_ge(qkv0_ready, 2)
            split(0)

            def maxima(u, n, kind):
                tc, J = divmod(u, NJ)
                wait_filled(dve, f"A{u}", n)
                if u == 0 and kind > 0:
                    wait_filled(dve, "NMT", n - 1)
                dve.tensor_reduce(nmx[:, tc, J, :, ROW], ring(f"A{u}").rearrange("p (g s) -> p g s", g=NG), AXX,
                                  ALU.max, negate=True).then_inc(emptied[slot(f"A{u}")], 1)

            def stack_maxima(n, par, kind):
                wait_filled(dve, "NMT", n)
                if kind > 0:
                    dve.wait_ge(q2_masked, 4 * n)
                dve.tensor_tensor(q2S[:, :, :], ring("NMT").rearrange("p (j t) -> p j t", j=NJ), qS[:, par, :, :],
                                  ALU.add).then_inc(emptied[slot("NMT")], 1)
                wait_emptied(dve, "NMT", n)
                for g in range(NG):
                    rows = slice(32 * g, 32 * g + 32)
                    dve.tensor_copy(q2M[rows, par, :, g, :], q2S[rows, :, :]).then_inc(q2_masked, 1)

            def keep_keys(n, par, kind):
                if kind > 0:
                    wait_filled(dve, "B7", n)
                dve.tensor_copy(kB[:, :, :], kS[:, par, :, :]).then_inc(keys_kept, 1)

            def norm_o(n, par):
                dve.wait_ge(p_used, 8 * n)
                step = link(dve, o_step, 3 * (n - 1), 3)
                step(dve.reciprocal(rD[:, :], od(par)[:, T:2 * T]))
                step(dve.tensor_tensor(on[:, :], od(par)[:, 0:T], rD[:, :], ALU.mult))
                step(dve.tensor_scalar(ob[:, :], on[:, :], bias[:, 2:3], None, ALU.add))

            def residual(n):
                c = n - 2
                wait_filled(dve, "WO", n)
                step = link(dve, x1_step, 5 * c, 5)
                dve.tensor_scalar(wo_t[:, :], ring("WO")[:, 0:T], bias[:, 3:4], tg[:, 0:1], ALU.add, ALU.mult)\
                   .then_inc(emptied[slot("WO")], 1)
                wait_emptied(dve, "WO", n)
                step(dve.scalar_tensor_tensor(out=xs[:, c, :], in0=wo_t[:, :], scalar=1.0, in1=xs[:, c, :],
                                              op0=ALU.mult, op1=ALU.add, accum_out=st2[:, 0:1]))
                step(dve.tensor_scalar(mv2[:, 0:1], st2[:, 0:1], 1.0 / T, None, ALU.mult))
                step(dve.tensor_scalar(xc[:, :], xs[:, c, :], mv2[:, 0:1], None, ALU.subtract))
                step(dve.scalar_tensor_tensor(out=wo_t[:, :], in0=xc[:, :], scalar=1.0, in1=xc[:, :], op0=ALU.mult,
                                              op1=ALU.mult, accum_out=st2[:, 1:2]))
                step(dve.tensor_scalar(ve2[:, :], st2[:, 1:2], 1.0 / T, EPS, ALU.mult, ALU.add))

            def norm_x1(n, kind):
                c = n - 2
                if kind > 2:
                    wait_filled(dve, "XT", n - 1)
                dve.wait_ge(pay_step, 3 * c)
                step = link(dve, rs_step, (RSQRT_STEPS + 1) * c, RSQRT_STEPS + 1)
                inverse_root(step, ve2[:, :], (s0[:, :], s1[:, :]))
                step(dve.tensor_scalar(xn2[:, :], xc[:, :], s0[:, 0:1], 1.0 / RSQRT_C, ALU.mult, ALU.mult))

            def route(part, c, par):
                step = link(dve, rt_step, c * ROUTE_STEPS + (0, 5, 20)[part], (5, 15, 9)[part])
                NQ = NE // GROUPS

                def row(i, w=NE):
                    return rt[:, i, 0:w]
                q = row(2).rearrange("p (g q) -> p g q", q=NQ)
                pair = q.rearrange("p g (a b) -> p g a b", b=2)
                hi, lo = row(3, 16), row(4, 16)
                hv, lv = hi.rearrange("p (g a) -> p g a", a=2), lo.rearrange("p (g a) -> p g a", a=2)

                def best(values, width, count, r):
                    dve.tensor_copy(row(r + 1, 8), values[:, 0:8])
                    step(dve.max(row(r, 8), values))
                    kth = row(r, 8)[:, count - 1:count]
                    step(dve.tensor_scalar(row(r + 1, width), values, kth, None, ALU.is_gt))
                    step(dve.tensor_reduce(row(r + 2, 1), row(r + 1, width), AXX, ALU.add))
                    step(dve.tensor_scalar(row(r + 3, width), values, kth, None, ALU.is_equal))
                    step(dve.tensor_tensor_scan(row(r + 4, width), ones[:, 0:width], row(r + 3, width), row(r + 2, 1),
                                                ALU.mult, ALU.add))
                    step(dve.scalar_tensor_tensor(out=row(r + 5, width), in0=row(r + 4, width), scalar=float(count),
                                                  in1=row(r + 3, width), op0=ALU.is_le, op1=ALU.mult))
                    step(dve.tensor_tensor(row(r, width), row(r + 5, width), row(r + 1, width), ALU.add))
                    return row(r, width)

                if part == 0:
                    step(dve.tensor_scalar(row(0), el[:, :], 1.0, None, ALU.add))
                    step(dve.reciprocal(row(1), row(0)))
                    step(dve.tensor_tensor(row(2), row(1), corr[:, :], ALU.add))
                    step(dve.tensor_tensor(hi.rearrange("p (g a) -> p g a", a=2), pair[:, :, :, 0], pair[:, :, :, 1], ALU.max))
                    step(dve.tensor_tensor(lo.rearrange("p (g a) -> p g a", a=2), pair[:, :, :, 0], pair[:, :, :, 1], ALU.min))
                elif part == 1:
                    step(dve.tensor_tensor(row(5, 8), hv[:, :, 0], hv[:, :, 1], ALU.max))
                    step(dve.tensor_tensor(row(6, 8), hv[:, :, 0], hv[:, :, 1], ALU.min))
                    step(dve.tensor_tensor(row(7, 8), lv[:, :, 0], lv[:, :, 1], ALU.max))
                    step(dve.tensor_tensor(row(8, 8), row(6, 8), row(7, 8), ALU.max))
                    step(dve.tensor_tensor(row(9, 8), row(5, 8), row(8, 8), ALU.add))
                    gm = best(row(9, 8), 8, TOPG, 10)
                    gmb = gm.unsqueeze(2).to_broadcast([128, GROUPS, NQ])
                    step(dve.tensor_tensor(row(16).rearrange("p (g q) -> p g q", q=NQ), q, gmb, ALU.mult))
                    step(dve.tensor_scalar(row(9, 8), gm, -1.0, 3.0e38, ALU.add, ALU.mult))
                    step(dve.tensor_tensor(row(17).rearrange("p (g q) -> p g q", q=NQ),
                                           row(16).rearrange("p (g q) -> p g q", q=NQ),
                                           row(9, 8).unsqueeze(2).to_broadcast([128, GROUPS, NQ]), ALU.add))
                else:
                    em = best(row(17), NE, TOPK, 18)
                    dve.wait_ge(pay_step, 3 * c + 3)
                    step(dve.scalar_tensor_tensor(out=pay[:, par, T + 1:PAY], in0=em, scalar=1.0 / WS, in1=row(1),
                                                  op0=ALU.mult, op1=ALU.mult))
                    step(dve.tensor_copy(em16[:, :], em))

            def dispatch(c, par):
                step = link(dve, dp_step, DISPATCH_STEPS * c + 1, DISPATCH_STEPS)
                step(dve.tensor_tensor(dp[:, 1, :], dp[:, 0, :], em16[:, :], ALU.mult))
                dve.tensor_copy(dp[:, 2, 8:16], dp[:, 1, 0:8])
                step(dve.max(dp[:, 2, 0:8], dp[:, 1, :]))
                step(dve.tensor_scalar(place[:, par, :], dp[:, 2, 0:TOPK], -1.0, None, ALU.add))
                step(dve.tensor_tensor(emsum[:, :], emsum[:, :], em16[:, :], ALU.add))

            def high_weights(r, i, kind):
                par = i % 2
                dve.wait_ge(w_scaled, r * 2 + 2)
                if kind > 0:
                    dve.wait_ge(stored, (r - 1) * 16)
                dve.tensor_copy(W[:, par, :, 0, :], wraw[:, i, :, :, :].rearrange("p k a m -> p k (a m)"))\
                   .then_inc(w_hi, 1)

            def period(kind, n):
                par = kind % 2
                for job in DVE_TURNS:
                    if job[0] == "A" and has(kind, job):
                        maxima(int(job[1]), n, kind)
                    elif job == "next x" and has(kind, "PROJ"):
                        if kind > 0:
                            wait_filled(dve, "PROJ", n - 1)
                        norm_x(n + 1, 1 - par)
                    elif job == "split" and has(kind, "PROJ"):
                        wait_emptied(dve, "PROJ", n)
                        dve.wait_ge(k_masked, 4 * (n + 1))
                        split(n + 1)
                    elif job == "residual" and has(kind, "WO"):
                        residual(n)
                    elif job == "norm" and has(kind, "WO"):
                        norm_x1(n, kind)
                    elif job == "places" and has(kind, "RK"):
                        wait_filled(dve, "RK", n)
                        dve.tensor_tensor(dp[:, 0, :], ring("RK")[:, 0:NE], first_row, ALU.add)\
                           .then_inc(emptied[slot("RK")], 1)
                        wait_emptied(dve, "RK", n)
                        dispatch(n - 3, 1 - par)
                    elif job[0:7] == "weights":
                        i = int(job[7])
                        if kind < B or kind == B and i < 2:
                            high_weights(n * 4 + i, i, kind if i < 2 else 1)
                    elif job == "maxima" and has(kind, "NMT"):
                        stack_maxima(n, par, kind)
                        keep_keys(n, par, kind)
                    elif job == "route0" and has(kind, "LG"):
                        wait_emptied(dve, "LG", n)
                        route(0, n - 2, par)
                    elif job in ("route1", "route2") and has(kind, "RK"):
                        route(int(job[5]), n - 3, 1 - par)
                    elif job == "out" and has(kind, "B7"):
                        if kind > 1:
                            wait_filled(dve, "WO", n)
                        norm_o(n, 1 - par)

            periods(dve, period)
            for part in (1, 2):
                route(part, B - 1, (B - 1) % 2)

            def low(i, buf):
                dve.wait_ge(hT_hi, i + 1)
                dve.tensor_tensor(hT[:, buf, 1, :, :], ps[0:MH, 2 + buf, 0:256].rearrange("p (c t) -> p c t", c=2),
                                  hT[:, buf, 0, :, :], ALU.subtract).then_inc(hT_lo, 1)

            def add(i):
                k = i % B
                dve.wait_ge(y_done, i + 1)
                dve.wait_ge(acc_done, i + 1)
                dve.scalar_tensor_tensor(out=acc[:, k, :], in0=ps[:, 4 + i % 2, 0:T], scalar=1.0 / WS, in1=acc[:, k, :],
                                         op0=ALU.mult, op1=ALU.add).then_inc(acc_done, 1)

            def make_table():
                dve.wait_ge(counts_filled, 1)
                n_e = od(1)[:, 0:NE]
                step = link(dve, tb_step, 0, TABLE_STEPS)
                step(dve.tensor_tensor(pad_place[:, 0:NE], n_e, pad_row[:, 0:NE], ALU.add))
                step(dve.tensor_tensor(over[:, :, :], n_e.unsqueeze(2).to_broadcast([128, NE, 8]), full, ALU.is_gt))
                step(dve.tensor_reduce(tb[:, 0, :], over[:, :, :], AXX, ALU.add))
                step(dve.tensor_tensor_scan(tb[:, 1, :], ones[:, 0:NE], tb[:, 0, :], zeros[:, 0:1], ALU.mult, ALU.add))
                b = number[:, 0:1]
                step(dve.scalar_tensor_tensor(out=tb[:, 2, :], in0=tb[:, 1, :], scalar=b, in1=ones[:, 0:NE],
                                              op0=ALU.is_le, op1=ALU.mult, accum_out=cols[:, 0:1]))
                step(dve.scalar_tensor_tensor(out=tb[:, 3, :], in0=tb[:, 1, :], scalar=b, in1=tb[:, 0, :],
                                              op0=ALU.is_le, op1=ALU.mult, accum_out=cols[:, 1:2]))
                step(dve.tensor_tensor(cols[:, 2:3], b, cols[:, 1:2], ALU.subtract))
                step(dve.tensor_scalar(cols[:, 3:4], cols[:, 2:3], 128.0, None, ALU.mult))
                step(dve.scalar_tensor_tensor(out=cols[:, 4:5], in0=cols[:, 0:1], scalar=float(CAP), in1=cols[:, 3:4],
                                              op0=ALU.mult, op1=ALU.add))
                step(dve.tensor_scalar(cols[:, 6:7], cols[:, 4:5], float(SPARE), None, ALU.min))
                for k in range(2):
                    step(dve.scalar_tensor_tensor(out=tb[:, 2, :], in0=tb[:, 1, :], scalar=b, in1=delta[:, k, :],
                                                  op0=ALU.is_le, op1=ALU.mult, accum_out=cols[:, 7 + k:8 + k]))
                dve.tensor_scalar(blocks_to[:, :], tb[0:1, 1, :], 1.0, None, ALU.add)

            dve.wait_ge(zeroed, 16 * 3)
            for i in range(2 * B + 3):
                if i < 2 * B:
                    dve.wait_ge(silu_done, i + 1)
                    if i >= 2:
                        dve.wait_ge(hT_filled, i - 1)
                    dve.scalar_tensor_tensor(out=h[:, i % 2, :], in0=ps[:, i % 2, M:2 * M], scalar=1.0 / WS,
                                             in1=sg[:, i % 2, :], op0=ALU.mult, op1=ALU.mult).then_inc(h_done, 1)
                if 1 <= i <= 2 * B:
                    low(i - 1, (i - 1) % 2)
                if i >= 3:
                    add(i - 3)
                if i == RANK_AT:
                    dve.wait_ge(rank7_filled, 1)
                    dve.tensor_tensor(dp[:, 0, :], od(0)[:, 0:NE], first_row, ALU.add).then_inc(rank7_read, 1)
                    dve.wait_ge(rank7_read, 1)
                    dispatch(B - 1, (B - 1) % 2)
                if i == COUNT_AT:
                    make_table()
                if i == TABLE_AT:
                    dve.wait_ge(table_filled, 1)
                    row, weights, expert = (od(0)[0:1, 128 * k:128 * k + 128] for k in range(3))
                    dve.tensor_scalar(loads_of[:, :], expert, 1.0, 16.0, ALU.add, ALU.mult)
                    dve.tensor_copy(row_of[:, :], row)
                    dve.tensor_copy(place_of[:, 2:130], weights)
                    dve.tensor_copy(expert_of[:, :], expert).then_inc(table_ready, 1)
            for b in range(B):
                dve.wait_ge(acc_done, 2 * B + b + 1)
                dve.scalar_tensor_tensor(out=xs[:, b, :], in0=acc[:, b, :], scalar=tg[:, 1:2], in1=xs[:, b, :],
                                         op0=ALU.mult, op1=ALU.add).then_inc(fin_done, 1)

            def begin(b, count):
                return entries(mybir.EngineType.DVE, expert_of, b, count, NE - 1)

            def step(b, j, u, experts):
                buf = j % 2
                if until(b):
                    dve.wait_ge(bsilu_done, b + 1)
                    dve.scalar_tensor_tensor(out=bh[:, buf, :], in0=ps[:, buf, M:2 * M],
                                             scalar=bx[:, j, bass.ds(experts[u] + (T + 1), 1)], in1=bsg[:, buf, :],
                                             op0=ALU.mult, op1=ALU.mult).then_inc(bh_done, 1)
                    if since(b, WB):
                        dve.wait_ge(added[buf], (b - buf) * 8 - 16)
                    dve.tensor_copy(bid[:, j:j + 1], bx[:, j, T:T + 1]).then_inc(bid_done, 1)
                if since(b, 1) and until(b - 1):
                    dve.wait_ge(bhT_hi, b)
                    dve.tensor_tensor(bhT[:, 1 - buf, 1, :, :], ps[0:MH, 3 - buf, 0:256].rearrange("p (c t) -> p c t", c=2),
                                      bhT[:, 1 - buf, 0, :, :], ALU.subtract).then_inc(bhT_done, 1)
                if since(b, 2) and until(b - 2):
                    dve.wait_ge(by_filled, b)
                    dve.tensor_scalar(by[:, (j - 2) % WB, :], ps[:, 4 + buf, 0:T], 1.0 / WS, None, ALU.mult)\
                       .then_inc(by_done, 1)

            dve.wait_ge(fin_done, B)
            blocks(dve, step, begin)
            dve.wait_ge(odd_sum_in, 16)
            for b in range(B):
                dve.scalar_tensor_tensor(out=xs[:, b, :], in0=acc1[:, b, :], scalar=tg[:, 1:2], in1=xs[:, b, :],
                                         op0=ALU.mult, op1=ALU.add).then_inc(tail_sum, 1)
            for b in range(B):
                dve.wait_ge(even_sum_in[b // (B // 2)], 16)
                dve.wait_ge(tail_sum, b + 1)
                dve.scalar_tensor_tensor(out=xs[:, b, :], in0=acc[:, b, :], scalar=tg[:, 1:2], in1=xs[:, b, :],
                                         op0=ALU.mult, op1=ALU.add).then_inc(out_ready, 1)

    return nc


_INS = ["x", "ctx_2048", "g_xattn", "g_ffn", "L0_xattn_Wq", "L0_xattn_bq", "L0_xattn_Wk", "L0_xattn_bk",
        "L0_xattn_Wv", "L0_xattn_bv", "L0_xattn_Wo", "L0_xattn_bo", "L0_ffn_w_router", "L0_ffn_corr_bias",
        "L0_ffn_gate_w", "L0_ffn_up_w", "L0_ffn_down_w", "L0_ffn_sh_gate_w", "L0_ffn_sh_up_w", "L0_ffn_sh_down_w"]
_OUT = (8, 128, 256)


def kernel(**inputs):
    import numpy as np
    import concourse.bacc as bacc
    from concourse.bass_utils import run_bass_kernel_spmd

    nc = bacc.Bacc("TRN2", target_bir_lowering=False, num_devices=1)
    arrays, args = {}, []
    for name in _INS:
        a = np.ascontiguousarray(inputs[name])
        arrays[f"in_{name}"] = a
        args.append(nc.dram_tensor(f"in_{name}", a.shape, mybir.dt.from_np(a.dtype), kind="ExternalInput").ap())
    args.append(nc.dram_tensor("out", _OUT, F32, kind="ExternalOutput").ap())
    build(nc, *args)
    return run_bass_kernel_spmd(nc, [arrays], core_ids=[0]).results[0]["out"]
```
